# Optimizing a Trainium2 kernel written in Bass

```python
import numpy as np
import jax
import jax.numpy as jnp

def _softmax(x, axis=-1):
    return jax.nn.softmax(x, axis=axis)

def _gelu(x):
    return jax.nn.gelu(x, approximate=True)

def _silu(x):
    return jax.nn.silu(x)

def _sigmoid(x):
    return jax.nn.sigmoid(x)

def _layernorm(x, axis=-1, eps=1e-05):
    m = jnp.mean(x, axis=axis, keepdims=True)
    v = jnp.var(x, axis=axis, keepdims=True)
    return (x - m) / jnp.sqrt(v + eps)

def _scatter_add(tgt, idx, src, axis=0):
    return tgt.at[idx].add(src)

def _segment_sum(src, seg, n):
    return jax.ops.segment_sum(src, seg, n)
kernel_name = 'mk_lm_tower_d1_tok_ids512_r4_53b00f'

def setup_inputs(seed: int=0):
    np.random.seed(seed)
    _w = jnp.asarray

    def _rec_inputs():
        import jax
        import jax.numpy as jnp
        _rk = jax.random.key(seed)
        x = jax.random.randint(jax.random.fold_in(_rk, 1), (32, 256), 0, 31993, jnp.int32)
        return x
    x = _rec_inputs()

    def _L0_tok_setup():
        import jax, jax.numpy as jnp
        import numpy as np
        V, D, L, F, H, NL = (8000, 128, 1024, 512, 8, 2)
        NB, NHASH, CS = (64, 4, 64)
        DH = D // H
        B, S = (2, 1024)

        def layer_norm(x, scale, bias):
            mu = jnp.mean(x, axis=-1, keepdims=True)
            var = jnp.var(x, axis=-1, keepdims=True)
            return (x - mu) * jax.lax.rsqrt(var + 1e-05) * scale + bias

        def lsh_attention(x, Wqk, Wv, Wo, rots):
            b, s, d = x.shape
            qk = (x @ Wqk).reshape(b, s, H, DH).transpose(0, 2, 1, 3)
            v = (x @ Wv).reshape(b, s, H, DH).transpose(0, 2, 1, 3)
            rot = jnp.einsum('bhsd,hrdk->bhrsk', qk, rots)
            buckets = jnp.argmax(jnp.concatenate([rot, -rot], -1), -1)
            order = jnp.argsort(buckets, axis=-1)
            inv = jnp.argsort(order, axis=-1)
            gather = lambda t: jnp.take_along_axis(jnp.broadcast_to(t[:, :, None], (b, H, NHASH, s, DH)), order[..., None], axis=3)
            sqk = gather(qk).reshape(b, H, NHASH, s // CS, CS, DH)
            sv = gather(v).reshape(b, H, NHASH, s // CS, CS, DH)
            k = sqk / (jnp.linalg.norm(sqk, axis=-1, keepdims=True) + 1e-06)
            kk = jnp.concatenate([k, jnp.roll(k, 1, axis=3)], axis=4)
            vv = jnp.concatenate([sv, jnp.roll(sv, 1, axis=3)], axis=4)
            scores = jnp.einsum('bhrcwd,bhrcud->bhrcwu', sqk, kk) / jnp.sqrt(jnp.float32(DH))
            attn = jax.nn.softmax(scores, axis=-1)
            out = jnp.einsum('bhrcwu,bhrcud->bhrcwd', attn, vv).reshape(b, H, NHASH, s, DH)
            out = jnp.take_along_axis(out, inv[..., None], axis=3).mean(axis=2)
            out = out.transpose(0, 2, 1, 3).reshape(b, s, d)
            return out @ Wo

        def ffn(x, W1, b1, W2, b2):
            return jax.nn.gelu(x @ W1 + b1) @ W2 + b2
        key = jax.random.key(seed)
        ks = jax.random.split(key, 16)
        sd = 0.02
        inp = {'x': jax.random.randint(ks[0], (B, S), 0, V), 'emb': jax.random.normal(ks[1], (V, D), jnp.float32) * sd, 'pos': jax.random.normal(ks[2], (1, L, D), jnp.float32) * sd, 'ln1_s': jnp.ones((NL, D), jnp.float32), 'ln1_b': jnp.zeros((NL, D), jnp.float32), 'Wqk': jax.random.normal(ks[3], (NL, D, D), jnp.float32) * sd, 'Wv': jax.random.normal(ks[4], (NL, D, D), jnp.float32) * sd, 'Wo': jax.random.normal(ks[5], (NL, D, D), jnp.float32) * sd, 'rots': jax.random.normal(ks[6], (NL, H, NHASH, DH, NB // 2), jnp.float32), 'ln2_s': jnp.ones((NL, D), jnp.float32), 'ln2_b': jnp.zeros((NL, D), jnp.float32), 'W1': jax.random.normal(ks[7], (NL, D, F), jnp.float32) * sd, 'b1': jnp.zeros((NL, F), jnp.float32), 'W2': jax.random.normal(ks[8], (NL, F, D), jnp.float32) * sd, 'b2': jnp.zeros((NL, D), jnp.float32)}
        return inp
    _L0_tok_all = _L0_tok_setup()
    _L0_tok_in = {k: v for k, v in _L0_tok_all.items() if k in ('emb', 'pos', 'ln1_s', 'ln1_b', 'Wqk', 'Wv', 'Wo', 'rots', 'ln2_s', 'ln2_b', 'W1', 'b1', 'W2', 'b2')}
    del _L0_tok_all

    def _L0_attn_setup():
        import jax, jax.numpy as jnp
        import numpy as np
        LN_EPS = 1e-10

        def _log_g(x):
            return jnp.where(x >= 0, jnp.log(jax.nn.relu(x) + 0.5), -jax.nn.softplus(-x))

        def _reference_tuple_inner(x, ln_gamma, ln_beta, W_gh):
            mu = jnp.mean(x, axis=-1, keepdims=True)
            var = jnp.mean(jnp.square(x - mu), axis=-1, keepdims=True)
            xn = (x - mu) * jax.lax.rsqrt(var + LN_EPS) * ln_gamma + ln_beta
            gh = jnp.einsum('btd,dh->bth', xn, W_gh)
            H = W_gh.shape[1] // 2
            k_gate, h_pre = (gh[..., :H], gh[..., H:])
            log_z = -jax.nn.softplus(-k_gate)
            log_coeffs = -jax.nn.softplus(k_gate)
            log_values = log_z + _log_g(h_pre)
            a_star = jnp.cumsum(log_coeffs, axis=1)
            log_h = a_star + jax.lax.cumlogsumexp(log_values - a_star, axis=1)
            h = jnp.exp(log_h)
            out = h + x
            hidden = h[:, -1]
            return (out, hidden)
        key = jax.random.key(seed)
        k1, k2 = jax.random.split(key)
        B, T, D, H = (8, 1024, 128, 128)
        x = jax.random.normal(k1, (B, T, D), dtype=jnp.float32)
        ln_gamma = jnp.ones((D,), dtype=jnp.float32)
        ln_beta = jnp.zeros((D,), dtype=jnp.float32)
        W_gh = jax.random.normal(k2, (D, 2 * H), dtype=jnp.float32) * 0.02
        return {'x': x, 'ln_gamma': ln_gamma, 'ln_beta': ln_beta, 'W_gh': W_gh}
    _L0_attn_all = _L0_attn_setup()
    _L0_attn_in = {k: v for k, v in _L0_attn_all.items() if k in ('ln_gamma', 'ln_beta', 'W_gh')}
    del _L0_attn_all

    def _L0_ffn_setup():
        import jax, jax.numpy as jnp
        import numpy as np
        DIM = 128
        NE = 8
        TOPK = 2
        CF = 1.2
        HID = 4 * DIM
        B, S = (8, 1024)
        key = jax.random.key(seed)
        ks = jax.random.split(key, 4)
        s = 0.02
        return {'x': jax.random.normal(ks[0], (B, S, DIM), jnp.float32), 'gate_w': jax.random.normal(ks[1], (NE, DIM), jnp.float32) * s, 'gate_b': jnp.zeros((NE,), jnp.float32), 'w1': jax.random.normal(ks[2], (NE, DIM, HID), jnp.float32) * s, 'b1': jnp.zeros((NE, HID), jnp.float32), 'w2': jax.random.normal(ks[3], (NE, HID, DIM), jnp.float32) * s, 'b2': jnp.zeros((NE, DIM), jnp.float32)}
    _L0_ffn_all = _L0_ffn_setup()
    _L0_ffn_in = {k: v for k, v in _L0_ffn_all.items() if k in ('gate_w', 'gate_b', 'w1', 'b1', 'w2', 'b2')}
    del _L0_ffn_all
    return {'x': x, 'L0_tok_emb': _L0_tok_in['emb'], 'L0_tok_pos': _L0_tok_in['pos'], 'L0_tok_ln1_s': _L0_tok_in['ln1_s'], 'L0_tok_ln1_b': _L0_tok_in['ln1_b'], 'L0_tok_Wqk': _L0_tok_in['Wqk'], 'L0_tok_Wv': _L0_tok_in['Wv'], 'L0_tok_Wo': _L0_tok_in['Wo'], 'L0_tok_rots': _L0_tok_in['rots'], 'L0_tok_ln2_s': _L0_tok_in['ln2_s'], 'L0_tok_ln2_b': _L0_tok_in['ln2_b'], 'L0_tok_W1': _L0_tok_in['W1'], 'L0_tok_b1': _L0_tok_in['b1'], 'L0_tok_W2': _L0_tok_in['W2'], 'L0_tok_b2': _L0_tok_in['b2'], 'L0_attn_ln_gamma': _L0_attn_in['ln_gamma'], 'L0_attn_ln_beta': _L0_attn_in['ln_beta'], 'L0_attn_W_gh': _L0_attn_in['W_gh'], 'L0_ffn_gate_w': _L0_ffn_in['gate_w'], 'L0_ffn_gate_b': _L0_ffn_in['gate_b'], 'L0_ffn_w1': _L0_ffn_in['w1'], 'L0_ffn_b1': _L0_ffn_in['b1'], 'L0_ffn_w2': _L0_ffn_in['w2'], 'L0_ffn_b2': _L0_ffn_in['b2']}

def reference(x, L0_tok_emb, L0_tok_pos, L0_tok_ln1_s, L0_tok_ln1_b, L0_tok_Wqk, L0_tok_Wv, L0_tok_Wo, L0_tok_rots, L0_tok_ln2_s, L0_tok_ln2_b, L0_tok_W1, L0_tok_b1, L0_tok_W2, L0_tok_b2, L0_attn_ln_gamma, L0_attn_ln_beta, L0_attn_W_gh, L0_ffn_gate_w, L0_ffn_gate_b, L0_ffn_w1, L0_ffn_b1, L0_ffn_w2, L0_ffn_b2):
    import jax
    import jax.numpy as jnp

    def _L0_tok_ref(x, emb, pos, ln1_s, ln1_b, Wqk, Wv, Wo, rots, ln2_s, ln2_b, W1, b1, W2, b2):
        import jax, jax.numpy as jnp
        import numpy as np
        V, D, L, F, H, NL = (8000, 128, 1024, 512, 8, 2)
        NB, NHASH, CS = (64, 4, 64)
        DH = D // H
        B, S = (2, 1024)

        def layer_norm(x, scale, bias):
            mu = jnp.mean(x, axis=-1, keepdims=True)
            var = jnp.var(x, axis=-1, keepdims=True)
            return (x - mu) * jax.lax.rsqrt(var + 1e-05) * scale + bias

        def lsh_attention(x, Wqk, Wv, Wo, rots):
            b, s, d = x.shape
            qk = (x @ Wqk).reshape(b, s, H, DH).transpose(0, 2, 1, 3)
            v = (x @ Wv).reshape(b, s, H, DH).transpose(0, 2, 1, 3)
            rot = jnp.einsum('bhsd,hrdk->bhrsk', qk, rots)
            buckets = jnp.argmax(jnp.concatenate([rot, -rot], -1), -1)
            order = jnp.argsort(buckets, axis=-1)
            inv = jnp.argsort(order, axis=-1)
            gather = lambda t: jnp.take_along_axis(jnp.broadcast_to(t[:, :, None], (b, H, NHASH, s, DH)), order[..., None], axis=3)
            sqk = gather(qk).reshape(b, H, NHASH, s // CS, CS, DH)
            sv = gather(v).reshape(b, H, NHASH, s // CS, CS, DH)
            k = sqk / (jnp.linalg.norm(sqk, axis=-1, keepdims=True) + 1e-06)
            kk = jnp.concatenate([k, jnp.roll(k, 1, axis=3)], axis=4)
            vv = jnp.concatenate([sv, jnp.roll(sv, 1, axis=3)], axis=4)
            scores = jnp.einsum('bhrcwd,bhrcud->bhrcwu', sqk, kk) / jnp.sqrt(jnp.float32(DH))
            attn = jax.nn.softmax(scores, axis=-1)
            out = jnp.einsum('bhrcwu,bhrcud->bhrcwd', attn, vv).reshape(b, H, NHASH, s, DH)
            out = jnp.take_along_axis(out, inv[..., None], axis=3).mean(axis=2)
            out = out.transpose(0, 2, 1, 3).reshape(b, s, d)
            return out @ Wo

        def ffn(x, W1, b1, W2, b2):
            return jax.nn.gelu(x @ W1 + b1) @ W2 + b2
        h = emb[x] + pos[:, :x.shape[1], :]
        x1, x2 = (h, jnp.zeros_like(h))
        for l in range(NL):
            y1 = x1 + lsh_attention(layer_norm(x2, ln1_s[l], ln1_b[l]), Wqk[l], Wv[l], Wo[l], rots[l])
            y2 = x2 + ffn(layer_norm(y1, ln2_s[l], ln2_b[l]), W1[l], b1[l], W2[l], b2[l])
            x1, x2 = (y1, y2)
        return (x1 + x2) / 2

    def _L0_attn_ref(x, ln_gamma, ln_beta, W_gh):
        import jax, jax.numpy as jnp
        import numpy as np
        LN_EPS = 1e-10

        def _log_g(x):
            return jnp.where(x >= 0, jnp.log(jax.nn.relu(x) + 0.5), -jax.nn.softplus(-x))

        def _reference_tuple_inner(x, ln_gamma, ln_beta, W_gh):
            mu = jnp.mean(x, axis=-1, keepdims=True)
            var = jnp.mean(jnp.square(x - mu), axis=-1, keepdims=True)
            xn = (x - mu) * jax.lax.rsqrt(var + LN_EPS) * ln_gamma + ln_beta
            gh = jnp.einsum('btd,dh->bth', xn, W_gh)
            H = W_gh.shape[1] // 2
            k_gate, h_pre = (gh[..., :H], gh[..., H:])
            log_z = -jax.nn.softplus(-k_gate)
            log_coeffs = -jax.nn.softplus(k_gate)
            log_values = log_z + _log_g(h_pre)
            a_star = jnp.cumsum(log_coeffs, axis=1)
            log_h = a_star + jax.lax.cumlogsumexp(log_values - a_star, axis=1)
            h = jnp.exp(log_h)
            out = h + x
            hidden = h[:, -1]
            return (out, hidden)
        return _reference_tuple_inner(x, ln_gamma, ln_beta, W_gh)[0]

    def _L0_ffn_ref(x, gate_w, gate_b, w1, b1, w2, b2):
        import jax, jax.numpy as jnp
        import numpy as np
        DIM = 128
        NE = 8
        TOPK = 2
        CF = 1.2
        HID = 4 * DIM
        B, S = (8, 1024)
        Bq, Sq, D = x.shape
        T = Bq * Sq
        cap = int(CF * T / NE)
        xf = x.reshape(T, D)
        probs = jax.nn.softmax(xf @ gate_w.T + gate_b, axis=-1)
        topw, topi = jax.lax.top_k(probs, TOPK)
        onehot = jax.nn.one_hot(topi, NE, dtype=topw.dtype)
        w_te = jnp.einsum('tk,tke->te', topw, onehot)
        routed = onehot.sum(axis=1) > 0
        wm = jnp.where(routed, w_te, -1.0)
        sel_w, sel_idx = jax.lax.top_k(wm.T, cap)
        sel_w = jnp.maximum(sel_w, 0.0)
        xg = xf[sel_idx]
        h = jax.nn.gelu(jnp.einsum('ecd,edh->ech', xg, w1) + b1[:, None, :], approximate=False)
        out = jnp.einsum('ech,ehd->ecd', h, w2) + b2[:, None, :]
        weighted = out * sel_w[..., None]
        of = jnp.zeros((T, D), x.dtype).at[sel_idx.reshape(-1)].add(weighted.reshape(-1, D))
        return of.reshape(Bq, Sq, D)
    h = _L0_tok_ref(x, L0_tok_emb, L0_tok_pos, L0_tok_ln1_s, L0_tok_ln1_b, L0_tok_Wqk, L0_tok_Wv, L0_tok_Wo, L0_tok_rots, L0_tok_ln2_s, L0_tok_ln2_b, L0_tok_W1, L0_tok_b1, L0_tok_W2, L0_tok_b2)
    h = h + _L0_attn_ref(_layernorm(h, axis=-1), L0_attn_ln_gamma, L0_attn_ln_beta, L0_attn_W_gh)
    h = h + _L0_ffn_ref(_layernorm(h, axis=-1), L0_ffn_gate_w, L0_ffn_gate_b, L0_ffn_w1, L0_ffn_b1, L0_ffn_w2, L0_ffn_b2)
    return h

_drawn_inputs = setup_inputs


def setup_inputs(seed=0):
    import zlib

    import numpy as np

    out = dict(_drawn_inputs(seed))
    spreads = {'L0_tok_ln1_s': (1.0, 0.2),
     'L0_tok_ln1_b': (0.0, 0.1),
     'L0_tok_ln2_s': (1.0, 0.2),
     'L0_tok_ln2_b': (0.0, 0.1),
     'L0_tok_b1': (0.0, 0.1),
     'L0_tok_b2': (0.0, 0.1),
     'L0_attn_ln_gamma': (1.0, 0.6),
     'L0_attn_ln_beta': (0.0, 0.591),
     'L0_ffn_gate_b': (0.0, 0.8),
     'L0_ffn_b1': (0.0, 0.8),
     'L0_ffn_b2': (0.0, 0.8)}
    factors = {'L0_tok_Wqk': 8.0,
     'L0_tok_rots': 7.643,
     'L0_ffn_gate_w': 5.232,
     'L0_ffn_w1': 8.0,
     'L0_ffn_w2': 8.0}
    for name, (base, spread) in spreads.items():
        noise = np.random.default_rng([zlib.crc32(name.encode()), seed]).standard_normal(out[name].shape)
        drawn = base * np.exp(spread * noise) if base else spread * noise
        out[name] = jnp.asarray(drawn.astype(out[name].dtype))
    for name, factor in factors.items():
        out[name] = (out[name] * factor).astype(out[name].dtype)
    return out
```

```python
from contextlib import ExitStack

import numpy as np

import concourse.bass as bass
from concourse import mybir

ALU = mybir.AluOpType
ACT = mybir.ActivationFunctionType
AX = mybir.AxisListType
F32 = mybir.dt.float32
BF16 = mybir.dt.bfloat16
I32 = mybir.dt.int32

P = 128
B, S = 32, 256
T = B * S
NT = T // P
V = 8000
F = 512
FC = F // P
H, DH = 8, 16
NHASH, NBUCKET, CS = 4, 64, 64
NC_ = S // CS
NK = NBUCKET // 2
BLK = 512
NBLK = T // BLK
GB = 4
NG = B // GB
GT = GB * S
E, HID, EC = 8, 512, 4
CAP = int(1.2 * T / E)
SLOTS = -(-CAP // P)
LN_EPS = 1e-5
GRU_EPS = 1e-10

_COLS = {}
_WIDTH = 0
for _name, _n in (("ident", P), ("block_sum", P), ("window", P), ("den_sum", P), ("before", P),
                  ("same_expert", P), ("iota", P), ("first_k", NK), ("guard_one", 1), ("guard_q", 1),
                  ("partition", 1), ("ranks", 3), ("ones", P), ("last", E),
                  ("token", NT), ("spare_row", E * SLOTS)):
    _COLS[_name] = (_WIDTH, _WIDTH + _n)
    _WIDTH += _n


def shape_constants():
    c = np.zeros((P, _WIDTH), np.float32)
    p, q = np.meshgrid(np.arange(P), np.arange(P), indexing="ij")

    def put(name, value):
        c[:, slice(*_COLS[name])] = value

    put("ident", p == q)
    put("block_sum", p // 32 == q // 32)
    same_head, same_hash = p // 16 == q // 16, p % 4 == q % 4
    cp, cq = p % 16 // 4, q % 16 // 4
    put("window", same_head & same_hash & ((cp == cq) | (cp == (cq + 1) % NC_)))
    put("den_sum", NHASH * (same_head & same_hash))
    put("before", p < q)
    put("same_expert", p % E == q % E)
    put("iota", q)
    put("first_k", NK - np.arange(NK)[None, :])
    put("guard_one", (np.arange(P) % 32 == 16)[:, None])
    put("guard_q", -0.25 * (np.arange(P) % 32 == 16)[:, None])
    put("partition", np.arange(P)[:, None])
    put("ranks", CS * np.arange(1, NC_)[None, :])
    put("ones", 1.0)
    put("last", E - np.arange(E)[None, :])
    put("token", np.arange(NT)[None, :] * P + np.arange(P)[:, None])
    put("spare_row", 2 * T + np.arange(E * SLOTS)[None, :] * P + np.arange(P)[:, None])
    return c


class Chain:

    def __init__(self, eng, sem, base=0):
        self.eng, self.sem, self.base, self.n = eng, sem, base, 0

    def __call__(self, ins):
        self.n += 1
        ins.then_inc(self.sem, 1)
        self.eng.wait_ge(self.sem, self.base + self.n)


def build(nc, a, out):
    with ExitStack() as ctx:
        def sb(name, shape, dt=F32, c=ctx):
            return c.enter_context(nc.sbuf_tensor(name, shape, dt))

        def sem(name, c=ctx):
            return c.enter_context(nc.semaphore(name))

        ps = ctx.enter_context(nc.psum_tensor("ps", [P, 8, 512], F32))
        x1 = sb("x1", [P, NT * P])
        x2 = sb("x2", [P, NT * P])
        const = sb("const", [P, _WIDTH])
        stats = sb("stats", [P, NT, 6])
        mean = sb("mean", [P, NT])
        rstd = sb("rstd", [P, NT])
        tmp = sb("tmp", [P, 2, NT])
        w1 = sb("w1", [P, 2, F])
        w2 = sb("w2", [P, 2, FC, P])
        b1c = sb("b1c", [P, 2, FC])
        b2r = sb("b2r", [P, 2, P])
        lncol = sb("lncol", [P, 8])
        s_load = sem("s_load")
        s_dv = sem("s_dv")
        s_sq = sem("s_sq")
        dv_count = [0]

        def C(name):
            return const[:, _COLS[name][0]:_COLS[name][1]]

        ident = C("ident")

        def finish_stats(dve, act_block_sem):
            link = Chain(dve, s_dv, dv_count[0])
            me, mo = stats[:, :, 1], stats[:, :, 4]
            link(nc.vector.tensor_tensor(mean[:], me, mo, ALU.add))
            link(nc.vector.tensor_tensor(tmp[:, 0, :], me, mo, ALU.subtract))
            link(nc.vector.tensor_scalar(mean[:], mean[:], 0.5, None, ALU.mult))
            link(nc.vector.scalar_tensor_tensor(out=tmp[:, 0, :], in0=tmp[:, 0, :], scalar=0.25, in1=tmp[:, 0, :],
                                                op0=ALU.mult, op1=ALU.mult))
            link(nc.vector.tensor_tensor(tmp[:, 1, :], stats[:, :, 2], stats[:, :, 5], ALU.add))
            link(nc.vector.scalar_tensor_tensor(out=tmp[:, 1, :], in0=tmp[:, 1, :], scalar=1.0 / P, in1=tmp[:, 0, :],
                                                op0=ALU.mult, op1=ALU.add))
            return link

        def rstd_phase(name, eps, gru=False):
            s_var = sem(f"{name}_var")
            s_root = sem(f"{name}_root")
            with nc.Block() as block:
                @block.vector
                def _(dve):
                    link = finish_stats(dve, s_var)
                    nc.vector.tensor_scalar(tmp[:, 0, :], tmp[:, 1, :], eps, None, ALU.add).then_inc(s_var, 1)
                    dve.wait_ge(s_root, 1)
                    link(nc.vector.reciprocal(rstd[:], rstd[:]))
                    if gru:
                        link(nc.vector.tensor_tensor(tmp[:, 0, :], rstd[:], rstd[:], ALU.mult))
                        link(nc.vector.tensor_tensor(tmp[:, 1, :], tmp[:, 1, :], tmp[:, 0, :], ALU.mult))
                        nc.vector.tensor_scalar(tmp[:, 0, :], tmp[:, 1, :], GRU_EPS, None, ALU.add).then_inc(s_var, 1)
                        dve.wait_ge(s_root, 2)
                        link(nc.vector.reciprocal(gru_r[:], gru_r[:]))
                    dv_count[0] += link.n

                @block.scalar
                def _(act):
                    act.wait_ge(s_var, 1)
                    nc.scalar.activation(rstd[:], tmp[:, 0, :], ACT.Sqrt).then_inc(s_root, 1)
                    if gru:
                        act.wait_ge(s_var, 2)
                        nc.scalar.activation(gru_r[:], tmp[:, 0, :], ACT.Sqrt).then_inc(s_root, 1)

        gru_r = sb("gru_r", [P, NT])

        with ExitStack() as ph:
            pos = sb("pos", [P, 2, P], c=ph)
            posc = sb("posc", [P, 2, P], c=ph)
            ids = sb("ids", [P, NT], I32, c=ph)
            idf = sb("idf", [P, 2, NT], c=ph)
            wv0 = sb("wv0", [P, P], c=ph)
            wo0 = sb("wo0", [P, P], c=ph)
            lb0 = sb("lb0", [P, 1], c=ph)
            t1 = sb("t1", [P, P], c=ph)
            GG = 8
            s_ids = sem("s_ids")
            s_idx = sem("s_idx")
            s_gather = [sem(f"s_gather{g}") for g in range(GG)]
            s_c0 = sem("s_c0")
            s_t1 = sem("s_t1")
            s_x = sem("s_x")
            NLOAD = 12
            with nc.Block() as block:
                @block.sync
                def _(sp):
                    sp.dma_start(ids[:], a["ids"]).then_inc(s_ids, 16)
                    sp.dma_start(const[:], a["consts"]).then_inc(s_load, 16)
                    sp.dma_start(pos[:], a["pos"][0, 0:S, :].rearrange("(t p) d -> p t d", p=P)).then_inc(s_load, 16)
                    sp.dma_start(wv0[:], a["Wv"][0]).then_inc(s_load, 16)
                    sp.dma_start(wo0[:], a["Wo"][0]).then_inc(s_load, 16)
                    sp.dma_start(lb0[:], a["ln1_b0"]).then_inc(s_load, 16)
                    sp.dma_start(w1[:], a["W1"].rearrange("l p f -> p l f")).then_inc(s_load, 16)
                    sp.dma_start(w2[:], a["W2"].rearrange("l (c p) d -> p l c d", p=P)).then_inc(s_load, 16)
                    sp.dma_start(b1c[:], a["b1c"]).then_inc(s_load, 16)
                    sp.dma_start(b2r[:], a["b2r"]).then_inc(s_load, 16)
                    sp.dma_start(lncol[:], a["lncol"]).then_inc(s_load, 16)
                    sp.wait_ge(s_load, 10 * 16)

                @block.vector
                def _(dve):
                    link = Chain(dve, s_dv, dv_count[0])
                    dve.wait_ge(s_ids, 16)
                    link(nc.vector.tensor_copy(idf[:, 0, :], ids[:]))
                    link(nc.vector.tensor_scalar(idf[:, 1, :], idf[:, 0, :], 0.0, float(V), ALU.is_lt, ALU.mult))
                    link(nc.vector.tensor_tensor(idf[:, 0, :], idf[:, 0, :], idf[:, 1, :], ALU.add))
                    nc.vector.tensor_scalar(ids[:], idf[:, 0, :], 0.0, float(V - 1), ALU.max, ALU.min).then_inc(s_idx, 1)
                    dve.wait_ge(s_c0, 1)
                    nc.vector.tensor_scalar(t1[:], C("ones"), ps[:, 0, 0:1], None, ALU.mult).then_inc(s_t1, 1)
                    dve.wait_ge(s_c0, 2)
                    for t in range(2):
                        link(nc.vector.tensor_tensor(posc[:, t, :], ps[:, 1, 0:P], pos[:, t, :], ALU.add))
                    for g in range(GG):
                        n = NT // GG
                        dve.wait_ge(s_gather[g], 16 * n)
                        for t in range(g * n, (g + 1) * n):
                            nc.vector.tensor_tensor(x1[:, t * P:(t + 1) * P], x1[:, t * P:(t + 1) * P], posc[:, t % 2, :],
                                                    ALU.add).then_inc(s_x, 1)
                        dve.wait_ge(s_x, (g + 1) * n)
                        for t in range(g * n, (g + 1) * n):
                            nc.vector.bn_stats(stats[:, t, :], x1[:, t * P:(t + 1) * P])
                    dv_count[0] += link.n

                @block.tensor
                def _(pe):
                    pe.wait_ge(s_load, 160)
                    nc.tensor.matmul(ps[:, 0, 0:1], wv0[:], lb0[:], start=True, stop=True).then_inc(s_c0, 1)
                    pe.wait_ge(s_t1, 1)
                    nc.tensor.matmul(ps[:, 1, 0:P], t1[:], wo0[:], start=True, stop=True).then_inc(s_c0, 1)

                @block.gpsimd
                def _(pool):
                    pool.wait_ge(s_idx, 1)
                    for t in range(NT):
                        nc.gpsimd.indirect_dma_start(
                            out=x1[:, t * P:(t + 1) * P], out_offset=None, in_=a["emb"],
                            in_offset=bass.IndirectOffsetOnAxis(ap=ids[:, t:t + 1], axis=0),
                        ).then_inc(s_gather[t // (NT // GG)], 16)

        rstd_phase("ln2_0", LN_EPS)

        def feed_forward(layer):
            with ExitStack() as ph:
                L = f"f{layer}_"
                xh = sb(L + "xh", [P, 2, BLK], c=ph)
                lt = sb(L + "lt", [P, 2, BLK], c=ph)
                ht = sb(L + "ht", [P, FC, BLK], c=ph)
                s_xh, s_tp, s_lt = sem(L + "normed"), sem(L + "turned"), sem(L + "lt_ready")
                s_h, s_ht, s_y = sem(L + "hidden"), sem(L + "gelu"), sem(L + "output")
                s_x2 = sem(L + "x2")
                lns, lnb = lncol[:, 2 + 2 * layer:3 + 2 * layer], lncol[:, 3 + 2 * layer:4 + 2 * layer]
                STEPS = 1 if layer == 0 else 4
                H0, Y0 = 2, 6

                with nc.Block() as block:
                    @block.vector
                    def _(dve):
                        def norm(i, u):
                            for t in range(4):
                                ins = nc.vector.tensor_scalar(
                                    xh[:, u, t * P:(t + 1) * P], x1[:, bass.ds(i * BLK + t * P, P)],
                                    mean[:, bass.ds(i * 4 + t, 1)], rstd[:, bass.ds(i * 4 + t, 1)],
                                    ALU.subtract, ALU.mult)
                            ins.then_inc(s_xh, 1)

                        def residual(i, u):
                            link = Chain(dve, s_x2, i * STEPS)
                            x2b = x2[:, bass.ds(i * BLK, BLK)]
                            x2v = x2b.rearrange("p (t d) -> p t d", t=4)
                            bias = b2r[:, layer, :].unsqueeze(1).broadcast_to((P, 4, P))
                            dve.wait_ge(s_y, i + 1)
                            if layer == 0:
                                y = ps[:, Y0 + u, :].rearrange("p (t d) -> p t d", t=4)
                                link(nc.vector.tensor_tensor(x2v, y, bias, ALU.add))
                            else:
                                link(nc.vector.tensor_tensor(x2b, ps[:, Y0 + u, :], x2b, ALU.add))
                                link(nc.vector.tensor_tensor(x2v, x2v, bias, ALU.add))
                                link(nc.vector.tensor_tensor(x2b, x2b, x1[:, bass.ds(i * BLK, BLK)], ALU.add))
                                link(nc.vector.tensor_scalar(x2b, x2b, 0.5, None, ALU.mult))
                            for t in range(4):
                                nc.vector.bn_stats(stats[:, bass.ds(i * 4 + t, 1), :].rearrange("p a b -> p (a b)"),
                                                   x2[:, bass.ds(i * BLK + t * P, P)])

                        norm(0, 0)
                        with dve.Fori(0, NBLK // 2 - 1) as k:
                            for u in range(2):
                                norm(k * 2 + u + 1, 1 - u)
                                residual(k * 2 + u, u)
                        norm(NBLK - 1, 1)
                        residual(NBLK - 2, 0)
                        residual(NBLK - 1, 1)

                    @block.tensor
                    def _(pe):
                        def turn(i, u):
                            pe.wait_ge(s_xh, i + 1)
                            for t in range(4):
                                ins = nc.tensor.transpose(ps[:, u, t * P:(t + 1) * P], xh[:, u, t * P:(t + 1) * P], ident)
                            ins.then_inc(s_tp, 1)

                        def hidden(i, u):
                            pe.wait_ge(s_lt, i + 1)
                            for c in range(FC):
                                nc.tensor.matmul(ps[:, H0 + c, :], w1[:, layer, c * P:(c + 1) * P], lt[:, u, :],
                                                 start=True, stop=True).then_inc(s_h, 1)

                        def output(i, u):
                            pe.wait_ge(s_ht, i * FC + FC)
                            for t in range(4):
                                for c in range(FC):
                                    ins = nc.tensor.matmul(ps[:, Y0 + u, t * P:(t + 1) * P],
                                                           ht[:, c, t * P:(t + 1) * P], w2[:, layer, c, :],
                                                           start=(c == 0), stop=(c == FC - 1))
                            ins.then_inc(s_y, 1)

                        turn(0, 0)
                        with pe.Fori(0, NBLK // 2 - 1) as k:
                            for u in range(2):
                                hidden(k * 2 + u, u)
                                turn(k * 2 + u + 1, 1 - u)
                                output(k * 2 + u, u)
                        hidden(NBLK - 2, 0)
                        turn(NBLK - 1, 1)
                        output(NBLK - 2, 0)
                        hidden(NBLK - 1, 1)
                        output(NBLK - 1, 1)

                    @block.scalar
                    def _(act):
                        nc.scalar.preload_act_table(ACT.Gelu_apprx_tanh)

                        def evac(i, u):
                            act.wait_ge(s_tp, i + 1)
                            nc.scalar.activation(lt[:, u, :], ps[:, u, :], ACT.Identity, scale=lns, bias=lnb)\
                                .then_inc(s_lt, 1)

                        def gelus(i):
                            for c in range(FC):
                                act.wait_ge(s_h, i * FC + c + 1)
                                nc.scalar.activation(ht[:, c, :], ps[:, H0 + c, :], ACT.Gelu_apprx_tanh,
                                                     bias=b1c[:, layer, c:c + 1]).then_inc(s_ht, 1)

                        evac(0, 0)
                        with act.Fori(0, NBLK // 2 - 1) as k:
                            for u in range(2):
                                gelus(k * 2 + u)
                                evac(k * 2 + u + 1, 1 - u)
                        gelus(NBLK - 2)
                        evac(NBLK - 1, 1)
                        gelus(NBLK - 1)

        feed_forward(0)
        rstd_phase("ln1_1", LN_EPS)

        def attention():
            with ExitStack() as ph:
                def psb(name, shape, dt=F32):
                    return sb("at_" + name, shape, dt, ph)

                def psem(name):
                    return sem("at_" + name, ph)

                QP = 32
                HS = 4
                NS = H // HS
                wqk = psb("wqk", [P, NS, HS, QP])
                wv = psb("wv", [P, H, 32])
                wo = psb("wo", [P, P])
                rots = psb("rots", [P, NS, HS * NHASH * NK])
                xh = psb("xh", [P, 2, BLK])
                lt = psb("lt", [P, 2, BLK])
                sq = xh
                q = psb("q", [P, 2, NS, BLK])
                nrm = psb("nrm", [P, 2, NS, BLK])
                qn = psb("qn", [P, NS, GT])
                kn = psb("kn", [P, NS, GT])
                vp = psb("vp", [P, GT // P, H, 32])
                qd = psb("qd", [P, 2, NS, HS, S])
                wd = psb("wd", [P, H, S])
                ee = psb("ee", [P, 2, 2, H, S])
                cp = psb("cp", [P, 2, GB, H, 32])
                hi_ = psb("hi", [P, 2, H * NHASH])
                ext_ = psb("ext", [P, 2, H * NHASH])
                wins_ = psb("pos_wins", [P, 2, H * NHASH], I32)
                hit = lt[:, 0, :].bitcast(BF16).rearrange("p (x k) -> p x k", k=NK)
                cn = lt[:, 1, :].bitcast(BF16).rearrange("p (t b d) -> p t b d", t=2, b=GB)
                identb = psb("identb", [P, P], BF16)
                fk = psb("fk", [P, NK], BF16)
                bt = psb("bt", [P, 2, GB, H * NHASH])
                rows, chunk = nrm[:, 1, 0, 0:S], nrm[:, 1, 1, 0:S]
                flags = nrm[:, 0, :, :].rearrange("p s (k w) -> p (s k) w", w=S)
                ct, mt, xw, rc = (q[:, 0, i // 2, i % 2 * S:(i % 2 + 1) * S] for i in range(4))
                ws, ot = (q[:, 1, 0, i * S:(i + 1) * S] for i in range(2))
                thr = psb("thr", [P, 6, 3])
                ones = psb("ones", [P, S])
                ctb = ps[:, 0, 0:P].bitcast(BF16)
                s_cp = psem("cp")
                s_hold = psem("hold")
                s_zero, s_w = psem("zero"), psem("weights")
                s_xh, s_tp, s_lt, s_q, s_v, s_sq, s_vp, s_qc, s_n2, s_nrm, s_qk = (
                    psem(n) for n in ("normed", "turned", "lt", "q", "v", "squares", "vp", "q_copied", "norm2", "norm",
                                      "qk"))
                s_rot, s_am, s_bt, s_rows, s_chunk, s_chT, s_c = (
                    psem(n) for n in ("rot", "argmax", "buckets_turned", "rows", "chunk", "chunk_turned", "c"))
                s_qd = [psem(f"qd{u}") for u in range(2)]
                s_s, s_exp, s_ct, s_cts, s_mt, s_mts, s_d, s_xw, s_den, s_ws, s_wd, s_g, s_a, s_o, s_ot, s_y, s_x1 = (
                    psem(n) for n in ("scores", "exp", "ct", "ct_out", "mt", "mt_out", "d", "xw", "den", "ws", "wd", "g",
                                      "a", "o", "ot", "y", "x1"))
                s_ch = psem("chain")
                KCH = 145
                s_wload = psem("wload")

                with nc.Block() as block:
                    @block.gpsimd
                    def _(pool):
                        for t in (wqk, wv, rots, qd, wd, cp):
                            nc.gpsimd.memset(t[:], 0.0).then_inc(s_zero, 1)

                    @block.vector
                    def _(dve):
                        nc.vector.tensor_copy(fk[:], C("first_k")).then_inc(s_w, 1)
                        nc.vector.memset(ones[:], 1.0).then_inc(s_w, 1)
                        nc.vector.tensor_copy(identb[:], ident).then_inc(s_w, 1)

                    @block.sync
                    def _(sp):
                        sp.wait_ge(s_zero, 6)
                        sp.dma_start(wo[:], a["Wo"][1]).then_inc(s_wload, 16)
                        n = 16
                        for s in range(NS):
                            sp.dma_start(wqk[:, s, :, 0:DH], a["Wqk"][1][:, s * 64:(s + 1) * 64]
                                         .rearrange("p (j d) -> p j d", j=HS)).then_inc(s_wload, 16)
                            n += 16
                            for j in range(HS):
                                dst = rots[32 * j:32 * j + DH, s, j * P:(j + 1) * P].rearrange("d (r k) -> d r k", r=NHASH)
                                sp.dma_start(dst, a["rots"][1, s * HS + j].rearrange("r d k -> d r k"))\
                                    .then_inc(s_wload, 16)
                                n += 16
                        wvv = wv[:].rearrange("p (j e) w -> p j e w", e=2)
                        src = a["Wv"][1].rearrange("p (j e d) -> p j e d", e=2, d=DH)
                        for e in range(2):
                            sp.dma_start(wvv[:, :, e, 16 * e:16 * e + DH], src[:, :, e, :]).then_inc(s_wload, 16)
                            n += 16
                        sp.wait_ge(s_wload, n)

                with nc.Block() as block:
                    @block.vector
                    def _(dve):
                        with dve.Fori(0, NG) as g:
                            link = Chain(dve, s_ch, g * KCH)
                            for n in range(2):
                                for t in range(4):
                                    tile = g * 8 + n * 4 + t
                                    ins = nc.vector.tensor_scalar(
                                        xh[:, n, t * P:(t + 1) * P], x2[:, bass.ds(tile * P, P)],
                                        mean[:, bass.ds(tile, 1)], rstd[:, bass.ds(tile, 1)], ALU.subtract, ALU.mult)
                                ins.then_inc(s_xh, 1)
                            for n in range(2):
                                dve.wait_ge(s_sq, g * 4 + n * 2 + 2)
                                nc.vector.tensor_copy(q[:, n, :, :], ps[:, 2 + 2 * n:4 + 2 * n, :]).then_inc(s_qc, 1)
                            dve.wait_ge(s_qc, g * 2 + 2)
                            for n in range(2):
                                for s in range(NS):
                                    dve.wait_ge(s_nrm, g * 4 + n * 2 + s + 1)
                                    cols = slice(n * BLK, (n + 1) * BLK)
                                    nc.vector.scalar_tensor_tensor(out=qn[:, s, cols], in0=nrm[:, n, s, :], scalar=C("guard_q"),
                                                                   in1=q[:, n, s, :], op0=ALU.mult, op1=ALU.add)\
                                        .then_inc(s_qk, 1)
                                    link(nc.vector.tensor_scalar(kn[:, s, cols], nrm[:, n, s, :], 1e-6, None, ALU.add))
                                    link(nc.vector.reciprocal(kn[:, s, cols], kn[:, s, cols]))
                                    link(nc.vector.scalar_tensor_tensor(out=kn[:, s, cols], in0=q[:, n, s, :], scalar=0.25,
                                                                        in1=kn[:, s, cols], op0=ALU.mult, op1=ALU.mult))
                                    nc.vector.tensor_scalar(kn[:, s, cols], kn[:, s, cols], C("guard_one"), None, ALU.add)\
                                        .then_inc(s_qk, 1)
                            for t in range(8):
                                pair = 2 + 2 * (t % 3)
                                hi, ext, pos_wins = hi_[:, t % 2, :], ext_[:, t % 2, :], wins_[:, t % 2, :]
                                rot = ps[:, pair:pair + 2, :].rearrange("p b (x k) -> p (b x) k", k=NK)
                                dve.wait_ge(s_rot, g * 8 + t + 1)
                                link(nc.vector.tensor_reduce(hi, rot, AX.X, ALU.max))
                                link(nc.vector.tensor_reduce(ext, rot, AX.X, ALU.min))
                                link(nc.vector.scalar_tensor_tensor(out=pos_wins, in0=ext, scalar=-1.0, in1=hi,
                                                                    op0=ALU.mult, op1=ALU.is_le))
                                dve.sem_inc(s_hold, 1)
                                link(nc.vector.copy_predicated(ext, pos_wins, hi))
                                ins = nc.vector.tensor_tensor(hit, rot, ext.unsqueeze(2).broadcast_to((P, H * NHASH, NK)),
                                                              ALU.is_equal)
                                link(ins)
                                link(nc.vector.tensor_tensor(hit, hit, fk[:].unsqueeze(1).broadcast_to((P, H * NHASH, NK)),
                                                             ALU.mult))
                                link(nc.vector.tensor_reduce(hi, hit, AX.X, ALU.max))
                                link(nc.vector.scalar_tensor_tensor(out=hi, in0=pos_wins, scalar=float(NK), in1=hi,
                                                                    op0=ALU.mult, op1=ALU.add))
                                nc.vector.tensor_scalar(bt[:, t % 2, t // 2, :], hi, -1.0, float(NBUCKET),
                                                        ALU.mult, ALU.add).then_inc(s_am, 1)
                            dve.wait_ge(s_bt, g + 1)
                            link(nc.vector.tensor_copy(rows, ps[:, 0, 0:S]))
                            low, cand, count, below, ok, rest = (thr[:, i, :] for i in range(6))
                            bit = NBUCKET // 2
                            link(nc.vector.memset(low, 0.0))
                            link(nc.vector.memset(below, 0.0))
                            while bit >= 1:
                                link(nc.vector.tensor_scalar(cand, low, float(bit), None, ALU.add))
                                for k in range(3):
                                    ins = nc.vector.tensor_scalar(flags[:, k, :], rows, cand[:, k:k + 1], None, ALU.is_lt,
                                                                  ALU.add, accum_out=count[:, k:k + 1])
                                    link(ins)
                                link(nc.vector.tensor_tensor(ok, count, C("ranks"), ALU.is_le))
                                link(nc.vector.scalar_tensor_tensor(out=low, in0=ok, scalar=float(bit), in1=low,
                                                                    op0=ALU.mult, op1=ALU.add))
                                link(nc.vector.tensor_tensor(count, count, ok, ALU.mult))
                                link(nc.vector.tensor_tensor(below, below, count, ALU.max))
                                bit //= 2
                            link(nc.vector.tensor_tensor(rest, C("ranks"), below, ALU.subtract))
                            for k in range(3):
                                same, run, at = flags[:, 0, :], flags[:, 1, :], flags[:, 2, :]
                                link(nc.vector.tensor_scalar(same, rows, low[:, k:k + 1], None, ALU.is_equal))
                                link(nc.vector.tensor_tensor_scan(run, ones[:], same, 0.0, ALU.mult, ALU.add))
                                link(nc.vector.scalar_tensor_tensor(out=at, in0=run, scalar=rest[:, k:k + 1], in1=same,
                                                                    op0=ALU.is_gt, op1=ALU.mult))
                                link(nc.vector.scalar_tensor_tensor(out=(chunk if k == 0 else flags[:, 3, :]), in0=rows,
                                                                    scalar=low[:, k:k + 1], in1=at, op0=ALU.is_gt, op1=ALU.add))
                                if k == 1:
                                    link(nc.vector.tensor_tensor(chunk, chunk, flags[:, 3, :], ALU.add))
                                elif k == 2:
                                    nc.vector.tensor_tensor(chunk, chunk, flags[:, 3, :], ALU.add).then_inc(s_chunk, 1)
                            dve.wait_ge(s_chT, g + 1)
                            for t in range(2):
                                src = ps[:, 1, t * P:(t + 1) * P].rearrange("p (x r) -> p x r", r=NHASH)
                                dst = cn[:, t, :, :].rearrange("p b (h c r) -> p (b h) c r", c=NC_, r=NHASH)
                                for c in range(NC_):
                                    ins = nc.vector.tensor_scalar(dst[:, :, c, :], src, float(c), None, ALU.is_equal)
                            ins.then_inc(s_c, 1)

                            for b in range(GB):
                                B_ = g * GB + b
                                dve.wait_ge(s_d, B_ + 1)
                                dve.wait_ge(s_mts, B_ + 1)
                                nc.vector.tensor_tensor(xw, ps[:, 6, 0:S], mt, ALU.mult).then_inc(s_xw, 1)
                                dve.wait_ge(s_den, B_ + 1)
                                link(nc.vector.reciprocal(rc, ps[:, 6, S:2 * S]))
                                nc.vector.tensor_tensor(ws, rc, mt, ALU.mult).then_inc(s_ws, 1)
                                for k in range(8):
                                    t, pr = k // 4, k % 4
                                    dve.wait_ge(s_g, B_ * 8 + k + 1)
                                    e2 = ee[:, b % 2, t, 2 * pr:2 * pr + 2, :]
                                    nc.vector.tensor_tensor(e2, ps[:, 4 + k % 2, :].rearrange("p (h w) -> p h w", h=2), e2,
                                                            ALU.mult).then_inc(s_a, 1)
                                dve.wait_ge(s_y, B_ + 1)
                                xb = x1[:, bass.ds(B_ * S, S)]
                                nc.vector.tensor_tensor(xb, ps[:, 7, S:2 * S], xb, ALU.add).then_inc(s_x1, 1)
                                dve.wait_ge(s_x1, B_ + 1)
                                for t in range(2):
                                    nc.vector.bn_stats(stats[:, bass.ds(B_ * 2 + t, 1), :].rearrange("p a b -> p (a b)"),
                                                       x1[:, bass.ds(B_ * S + t * P, P)])
                            assert link.n == KCH, link.n

                    @block.tensor
                    def _(pe):
                        with pe.Fori(0, NG) as g:
                            for n in range(2):
                                pe.wait_ge(s_xh, g * 2 + n + 1)
                                for t in range(4):
                                    ins = nc.tensor.transpose(ps[:, n, t * P:(t + 1) * P], xh[:, n, t * P:(t + 1) * P], ident)
                                ins.then_inc(s_tp, 1)
                            for n in range(2):
                                pe.wait_ge(s_lt, g * 2 + n + 1)
                                for s in range(NS):
                                    ins = nc.tensor.matmul(ps[:, 2 + 2 * n + s, :], wqk[:, s, :, :].rearrange("p j d -> p (j d)"),
                                                           lt[:, n, :], start=True, stop=True)
                                ins.then_inc(s_q, 1)
                                if n:
                                    pe.wait_ge(s_vp, g * 2 + 1)
                                for t in range(4):
                                    ins = nc.tensor.matmul(ps[:, 6 + t // 2, (t % 2) * S:(t % 2 + 1) * S],
                                                           lt[:, n, t * P:(t + 1) * P], wv[:].rearrange("p h d -> p (h d)"),
                                                           start=True, stop=True)
                                ins.then_inc(s_v, 1)
                            for n in range(2):
                                for s in range(NS):
                                    pe.wait_ge(s_sq, g * 4 + n * 2 + s + 1)
                                    if n:
                                        pe.wait_ge(s_nrm, g * 4 + s + 1)
                                    nc.tensor.matmul(ps[:, s, :], C("block_sum"), sq[:, s, :], start=True, stop=True)\
                                        .then_inc(s_n2, 1)
                            for t in range(8):
                                pe.wait_ge(s_qk, g * 8 + 4 * (t // 4) + 4)
                                if t == 0:
                                    pe.wait_ge(s_vp, g * 2 + 2)
                                    pe.wait_ge(s_qc, g * 2 + 2)
                                if t >= 3:
                                    pe.wait_ge(s_am, g * 8 + t - 2)
                                for s in range(NS):
                                    ins = nc.tensor.matmul(ps[:, 2 + 2 * (t % 3) + s, :], qn[:, s, t * P:(t + 1) * P],
                                                           rots[:, s, :], start=True, stop=True)
                                ins.then_inc(s_rot, 1)
                            pe.wait_ge(s_am, g * 8 + 8)
                            pe.wait_ge(s_nrm, g * 4 + 4)
                            for t in range(2):
                                ins = nc.tensor.transpose(ps[:, 0, t * P:(t + 1) * P],
                                                          bt[:, t, :, :].rearrange("p b x -> p (b x)"), ident)
                            ins.then_inc(s_bt, 1)

                            def scores(b):
                                B_ = g * GB + b
                                pe.wait_ge(s_qd[b % 2], 128 * (g * 2 + b // 2 + 1))
                                for k in range(8):
                                    t, s, pr = k // 4, k // 2 % 2, k % 2
                                    if b or k >= 2:
                                        pe.wait_ge(s_exp, B_ * 8 + k - 1)
                                    nc.tensor.matmul(ps[:, 2 + k % 2, :], kn[:, s, b * S + t * P:b * S + (t + 1) * P],
                                                     qd[:, b % 2, s, 2 * pr:2 * pr + 2, :].rearrange("p j w -> p (j w)"),
                                                     start=True, stop=True).then_inc(s_s, 1)

                            scores(0)
                            pe.wait_ge(s_chunk, g + 1)
                            for t in range(2):
                                ins = nc.tensor.transpose(ps[:, 1, t * P:(t + 1) * P], chunk[:, t * P:(t + 1) * P], ident)
                            ins.then_inc(s_chT, 1)
                            pe.wait_ge(s_c, g + 1)
                            for b in range(GB):
                                B_ = g * GB + b
                                for t in range(2):
                                    ins = nc.tensor.transpose(ctb[:, t * P:(t + 1) * P], cn[:, t, b, :], identb[:])
                                ins.then_inc(s_ct, 1)
                                pe.wait_ge(s_cts, B_ + 1)
                                nc.tensor.matmul(ps[:, 0, S:2 * S], C("window"), ct, start=True, stop=True).then_inc(s_mt, 1)
                                pe.wait_ge(s_exp, B_ * 8 + 8)
                                if b == 0:
                                    pe.wait_ge(s_cp, g * 2 + 2)
                                for i, (e, t) in enumerate(((0, 0), (0, 1), (1, 0), (1, 1))):
                                    for j in range(4):
                                        h = 2 * j + e
                                        ins = nc.tensor.matmul(ps[32 * j:32 * j + 32, 6, 0:S], cp[:, t, b, h, :],
                                                               ee[:, b % 2, t, h, :], start=(i == 0), stop=(i == 3))
                                ins.then_inc(s_d, 1)
                                pe.wait_ge(s_xw, B_ + 1)
                                nc.tensor.matmul(ps[:, 6, S:2 * S], C("den_sum"), xw, start=True, stop=True)\
                                    .then_inc(s_den, 1)
                                if b + 1 < GB:
                                    scores(b + 1)
                                pe.wait_ge(s_wd, 128 * (B_ + 1))
                                for k in range(8):
                                    t, pr = k // 4, k % 4
                                    if k >= 2:
                                        pe.wait_ge(s_a, B_ * 8 + k - 1)
                                    nc.tensor.matmul(ps[:, 4 + k % 2, :], ct[:, t * P:(t + 1) * P],
                                                     wd[:, 2 * pr:2 * pr + 2, :].rearrange("p h w -> p (h w)"),
                                                     start=True, stop=True).then_inc(s_g, 1)
                                pe.wait_ge(s_a, B_ * 8 + 8)
                                for i, (e, t) in enumerate(((0, 0), (0, 1), (1, 0), (1, 1))):
                                    for j in range(4):
                                        h = 2 * j + e
                                        ins = nc.tensor.matmul(ps[32 * j:32 * j + 32, 7, 0:S], vp[:, 2 * b + t, h, :],
                                                               ee[:, b % 2, t, h, :], start=(i == 0), stop=(i == 3))
                                ins.then_inc(s_o, 1)
                                pe.wait_ge(s_ot, B_ + 1)
                                for t in range(2):
                                    ins = nc.tensor.matmul(ps[:, 7, S + t * P:S + (t + 1) * P], ot[:, t * P:(t + 1) * P],
                                                           wo[:], start=True, stop=True)
                                ins.then_inc(s_y, 1)

                    @block.scalar
                    def _(act):
                        with act.Fori(0, NG) as g:
                            for n in range(2):
                                act.wait_ge(s_tp, g * 2 + n + 1)
                                nc.scalar.activation(lt[:, n, :], ps[:, n, :], ACT.Identity, scale=lncol[:, 0:1],
                                                     bias=lncol[:, 1:2]).then_inc(s_lt, 1)
                            for n in range(2):
                                act.wait_ge(s_q, g * 2 + n + 1)
                                if n:
                                    act.wait_ge(s_n2, g * 4 + 2)
                                for s in range(NS):
                                    nc.scalar.activation(sq[:, s, :], ps[:, 2 + 2 * n + s, :], ACT.Square).then_inc(s_sq, 1)
                                act.wait_ge(s_v, g * 2 + n + 1)
                                dst = vp[:, 4 * n:4 * n + 4, :, :].rearrange("p t h d -> p (t h d)")
                                nc.scalar.activation(dst, ps[:, 6:8, :].rearrange("p b w -> p (b w)"), ACT.Identity)\
                                    .then_inc(s_vp, 1)
                                for s in range(NS):
                                    act.wait_ge(s_n2, g * 4 + n * 2 + s + 1)
                                    nc.scalar.activation(nrm[:, n, s, :], ps[:, s, :], ACT.Sqrt).then_inc(s_nrm, 1)

                            def exps(b):
                                B_ = g * GB + b
                                for k in range(8):
                                    t, pr = k // 4, k % 4
                                    act.wait_ge(s_s, B_ * 8 + k + 1)
                                    nc.scalar.activation(ee[:, b % 2, t, 2 * pr:2 * pr + 2, :].rearrange("p h w -> p (h w)"),
                                                         ps[:, 2 + k % 2, :], ACT.Exp).then_inc(s_exp, 1)

                            exps(0)
                            for b in range(GB):
                                B_ = g * GB + b
                                act.wait_ge(s_ct, B_ + 1)
                                nc.scalar.activation(ct, ctb, ACT.Identity).then_inc(s_cts, 1)
                                act.wait_ge(s_mt, B_ + 1)
                                nc.scalar.activation(mt, ps[:, 0, S:2 * S], ACT.Identity).then_inc(s_mts, 1)
                                if b + 1 < GB:
                                    exps(b + 1)
                                act.wait_ge(s_o, B_ + 1)
                                nc.scalar.activation(ot, ps[:, 7, 0:S], ACT.Identity).then_inc(s_ot, 1)

                    @block.gpsimd
                    def _(pool):
                        with pool.Fori(0, NG) as g:
                            pool.wait_ge(s_c, g + 1)
                            pool.sem_inc(s_hold, 1)
                            src = cn.rearrange("p t b (j e d) -> p (t b j) e d", e=2, d=16)
                            dst = cp[:].rearrange("p t b (j e) w -> p (t b j) e w", e=2)
                            for e in range(2):
                                ins = nc.gpsimd.tensor_copy(dst[:, :, e, 16 * e:16 * e + 16], src[:, :, e, :])
                                ins.then_inc(s_cp, 1)

                    @block.sync
                    def _(sp):
                        with sp.Fori(0, NG) as g:
                            def place_q(b):
                                if b >= 2:
                                    sp.wait_ge(s_s, (g * GB + b - 1) * 8)
                                    sp.sem_inc(s_hold, 1)
                                if b in (0, 2):
                                    sp.wait_ge(s_qk, g * 8 + 4 * (b // 2) + 4)
                                sp.sem_inc(s_hold, 1)
                                for s in range(NS):
                                    for j in range(HS):
                                        sp.dma_start(qd[32 * j:32 * j + 32, b % 2, s, j, :],
                                                     qn[32 * j:32 * j + 32, s, b * S:(b + 1) * S]).then_inc(s_qd[b % 2], 16)

                            place_q(0)
                            place_q(1)
                            for b in range(GB):
                                B_ = g * GB + b
                                if b + 1 < GB and b >= 1:
                                    place_q(b + 1)
                                sp.wait_ge(s_ws, B_ + 1)
                                sp.sem_inc(s_hold, 1)
                                for h in range(H):
                                    sp.dma_start(wd[16 * h:16 * h + 16, h, :], ws[16 * h:16 * h + 16, :]).then_inc(s_wd, 16)

        attention()
        rstd_phase("ln2_1", LN_EPS)
        feed_forward(1)
        rstd_phase("gru", LN_EPS, gru=True)

        def recurrence():
            with ExitStack() as ph:
                def psb(name, shape, dt=F32):
                    return sb("re_" + name, shape, dt, ph)

                def psem(name):
                    return sem("re_" + name, ph)

                xh, lt = psb("xh", [P, 2, BLK]), psb("lt", [P, 2, BLK])
                wgh = psb("wgh", [P, 2 * P])
                rr = psb("rr", [P, 3, NT])
                gate = psb("gate", [P, 3, BLK])
                g_, st = psb("g", [P, BLK]), psb("state", [P, 2, BLK])
                s_w, s_rr = psem("weights"), psem("factors")
                s_xh, s_tp, s_lt, s_gh, s_sig, s_st, s_bk, s_c = (
                    psem(n) for n in ("normed", "turned", "lt", "gates", "sigmoids", "states", "back", "chain"))
                K = 7
                with nc.Block() as block:
                    @block.sync
                    def _(sp):
                        sp.dma_start(wgh[:], a["W_gh"]).then_inc(s_w, 16)
                        sp.wait_ge(s_w, 16)

                    @block.vector
                    def _(dve):
                        link = Chain(dve, s_rr)
                        link(nc.vector.tensor_tensor(rr[:, 0, :], rstd[:], gru_r[:], ALU.mult))
                        link(nc.vector.tensor_scalar(rr[:, 1, :], rstd[:], 1.0, None, ALU.add))
                        link(nc.vector.scalar_tensor_tensor(out=rr[:, 2, :], in0=mean[:], scalar=-1.0, in1=rstd[:],
                                                            op0=ALU.mult, op1=ALU.mult))

                with nc.Block() as block:
                    @block.vector
                    def _(dve):
                        def norm(i, u):
                            for t in range(4):
                                ins = nc.vector.tensor_scalar(
                                    xh[:, u, t * P:(t + 1) * P], x2[:, bass.ds(i * BLK + t * P, P)],
                                    mean[:, bass.ds(i * 4 + t, 1)], rr[:, 0, bass.ds(i * 4 + t, 1)],
                                    ALU.subtract, ALU.mult)
                            ins.then_inc(s_xh, 1)

                        def mix(i, u):
                            link = Chain(dve, s_c, i * K)
                            for t in range(4):
                                h = x2[:, bass.ds(i * BLK + t * P, P)]
                                link(nc.vector.tensor_scalar(h, h, rr[:, 1, bass.ds(i * 4 + t, 1)],
                                                             rr[:, 2, bass.ds(i * 4 + t, 1)], ALU.mult, ALU.add))
                            dve.wait_ge(s_sig, i * 3 + 3)
                            link(nc.vector.tensor_scalar(g_[:], ps[:, 3 + 2 * u, :], 0.0, None, ALU.max))
                            link(nc.vector.scalar_tensor_tensor(out=g_[:], in0=gate[:, 2, :], scalar=0.5, in1=g_[:],
                                                                op0=ALU.min, op1=ALU.add))
                            link(nc.vector.tensor_tensor(g_[:], g_[:], gate[:, 0, :], ALU.mult))
                            for t in range(2):
                                w = slice(t * S, (t + 1) * S)
                                nc.vector.tensor_tensor_scan(st[:, u, w], gate[:, 1, w], g_[:, w], 0.0, ALU.mult, ALU.add)\
                                    .then_inc(s_st, 1)
                            assert link.n == K

                        def residual(i, u):
                            dve.wait_ge(s_bk, i + 1)
                            x2b = x2[:, bass.ds(i * BLK, BLK)]
                            nc.vector.tensor_tensor(x2b, ps[:, 6 + u, :], x2b, ALU.add).then_inc(s_rr, 1)
                            dve.wait_ge(s_rr, 3 + i + 1)
                            for t in range(4):
                                nc.vector.bn_stats(stats[:, bass.ds(i * 4 + t, 1), :].rearrange("p a b -> p (a b)"),
                                                   x2[:, bass.ds(i * BLK + t * P, P)])

                        norm(0, 0)
                        with dve.Fori(0, NBLK // 2 - 1) as k:
                            for u in range(2):
                                norm(k * 2 + u + 1, 1 - u)
                                mix(k * 2 + u, u)
                                residual(k * 2 + u, u)
                        norm(NBLK - 1, 1)
                        mix(NBLK - 2, 0)
                        residual(NBLK - 2, 0)
                        mix(NBLK - 1, 1)
                        residual(NBLK - 1, 1)

                    @block.tensor
                    def _(pe):
                        def turn(i, u):
                            pe.wait_ge(s_xh, i + 1)
                            for t in range(4):
                                ins = nc.tensor.transpose(ps[:, u, t * P:(t + 1) * P], xh[:, u, t * P:(t + 1) * P], ident)
                            ins.then_inc(s_tp, 1)

                        def gates(i, u):
                            pe.wait_ge(s_lt, i + 1)
                            for c in range(2):
                                ins = nc.tensor.matmul(ps[:, 2 + 2 * u + c, :], wgh[:, c * P:(c + 1) * P], lt[:, u, :],
                                                       start=True, stop=True)
                            ins.then_inc(s_gh, 1)

                        def back(i, u):
                            pe.wait_ge(s_st, i * 2 + 2)
                            for t in range(4):
                                ins = nc.tensor.transpose(ps[:, 6 + u, t * P:(t + 1) * P], st[:, u, t * P:(t + 1) * P], ident)
                            ins.then_inc(s_bk, 1)

                        turn(0, 0)
                        with pe.Fori(0, NBLK // 2 - 1) as k:
                            for u in range(2):
                                gates(k * 2 + u, u)
                                turn(k * 2 + u + 1, 1 - u)
                                back(k * 2 + u, u)
                        gates(NBLK - 2, 0)
                        turn(NBLK - 1, 1)
                        back(NBLK - 2, 0)
                        gates(NBLK - 1, 1)
                        back(NBLK - 1, 1)

                    @block.scalar
                    def _(act):
                        nc.scalar.preload_act_table(ACT.Sigmoid)

                        def evac(i, u):
                            act.wait_ge(s_tp, i + 1)
                            nc.scalar.activation(lt[:, u, :], ps[:, u, :], ACT.Identity, scale=lncol[:, 6:7],
                                                 bias=lncol[:, 7:8]).then_inc(s_lt, 1)

                        def sigmoids(i, u):
                            act.wait_ge(s_gh, i + 1)
                            for c, (bank, scale) in enumerate(((0, 1.0), (0, -1.0), (1, 1.0))):
                                nc.scalar.activation(gate[:, c, :], ps[:, 2 + 2 * u + bank, :], ACT.Sigmoid, scale=scale)\
                                    .then_inc(s_sig, 1)

                        evac(0, 0)
                        with act.Fori(0, NBLK // 2 - 1) as k:
                            for u in range(2):
                                sigmoids(k * 2 + u, u)
                                evac(k * 2 + u + 1, 1 - u)
                        sigmoids(NBLK - 2, 0)
                        evac(NBLK - 1, 1)
                        sigmoids(NBLK - 1, 1)

        recurrence()
        rstd_phase("ln3", LN_EPS)

        XW = P + 2 * E
        rows_dram = nc.dram_tensor("expert_rows", [T, XW], F32, kind="Internal").ap()
        y_dram = nc.dram_tensor("expert_out", [2 * T + E * SLOTS * P, P], F32, kind="Internal").ap()
        TE = NT * E
        gather_i = sb("gather_i", [P, E, SLOTS], I32)
        valid = sb("valid", [P, E, SLOTS])
        spare = sb("spare", [P, E, SLOTS])

        def routing():
            with ExitStack() as ph:
                def psb(name, shape, dt=F32):
                    return sb("ro_" + name, shape, dt, ph)

                def psem(name):
                    return sem("ro_" + name, ph)

                xh, lt = psb("xh", [P, 2, BLK]), psb("lt", [P, 2, BLK])
                gw, gb = psb("gw", [P, E]), psb("gb", [P, E])
                zero = psb("zero", [P, 4096])
                bits = psb("bits", [P, 30], I32)
                probs, oh1, oh2, aa, bb, wt = (psb(f"n8_{i}", [P, NT, E]) for i in range(6))
                n1 = psb("n1", [P, NT])
                wdest = psb("wdest", [P, NT, 2, E])
                thr, cand = psb("thr", [P, 1], I32), psb("cand", [P, 1], I32)
                take = psb("take", [P, 1], I32)
                count = psb("count", [P, 1])
                thr8, room = psb("thr8", [P, E]), psb("room", [P, E])
                pos_i = psb("pos_i", [P, NT, E], I32)
                iota_b = psb("iota_b", [P, P], BF16)
                pay = psb("pay", [P, TE, 2, SLOTS], BF16)
                oh_lo = psb("oh_lo", [P, 2, E, P], BF16)
                slot = psb("slot", [P, E, 2 * SLOTS])
                s_w, s_z, s_xh, s_tp, s_lt, s_lg, s_lo, s_c, s_row, s_yz = (
                    psem(n) for n in ("weights", "zero", "normed", "turned", "lt", "logits", "logits_out", "chain",
                                      "rows_stored", "y_zeroed"))
                s_st = [psem(f"stored{u}") for u in range(2)]
                ZC = 2 * T * P // (P * 4096)
                with nc.Block() as block:
                    @block.sync
                    def _(sp):
                        sp.dma_start(gw[:], a["gate_wT"]).then_inc(s_w, 16)
                        sp.dma_start(gb[:], a["gate_b"]).then_inc(s_w, 16)
                        sp.dma_start(bits[:], a["bits"]).then_inc(s_w, 16)
                        sp.wait_ge(s_w, 48)

                    @block.vector
                    def _(dve):
                        nc.vector.memset(zero[:], 0.0)

                with nc.Block() as block:
                    @block.vector
                    def _(dve):
                        def norm(i, u, k):
                            dve.wait_ge(s_st[u], k * 16 + 16)
                            for t in range(4):
                                ins = nc.vector.tensor_scalar(
                                    xh[:, u, t * P:(t + 1) * P], x2[:, bass.ds(i * BLK + t * P, P)],
                                    mean[:, bass.ds(i * 4 + t, 1)], rstd[:, bass.ds(i * 4 + t, 1)],
                                    ALU.subtract, ALU.mult)
                            ins.then_inc(s_xh, 1)

                        def logits(i, u):
                            dve.wait_ge(s_lg, i + 1)
                            dst = probs[:, bass.ds(i * 4, 4), :]
                            src = ps[:, 2 + u, 0:4 * E].rearrange("p (t e) -> p t e", e=E)
                            nc.vector.tensor_tensor(dst, src, gb[:].unsqueeze(1).broadcast_to((P, 4, E)), ALU.add)\
                                .then_inc(s_lo, 1)

                        norm(0, 0, 0)
                        with dve.Fori(0, NBLK // 2 - 1) as k:
                            norm(k * 2 + 1, 1, k)
                            logits(k * 2, 0)
                            norm(k * 2 + 2, 0, k + 1)
                            logits(k * 2 + 1, 1)
                        norm(NBLK - 1, 1, NBLK // 2 - 1)
                        logits(NBLK - 2, 0)
                        logits(NBLK - 1, 1)

                    @block.tensor
                    def _(pe):
                        def turn(i, u):
                            pe.wait_ge(s_xh, i + 1)
                            for t in range(4):
                                ins = nc.tensor.transpose(ps[:, u, t * P:(t + 1) * P], xh[:, u, t * P:(t + 1) * P], ident)
                            ins.then_inc(s_tp, 1)

                        def gate(i, u):
                            pe.wait_ge(s_lt, i + 1)
                            for t in range(4):
                                ins = nc.tensor.matmul(ps[:, 2 + u, t * E:(t + 1) * E], lt[:, u, t * P:(t + 1) * P], gw[:],
                                                       start=True, stop=True)
                            ins.then_inc(s_lg, 1)

                        turn(0, 0)
                        with pe.Fori(0, NBLK // 2 - 1) as k:
                            for u in range(2):
                                turn(k * 2 + u + 1, 1 - u)
                                gate(k * 2 + u, u)
                        turn(NBLK - 1, 1)
                        gate(NBLK - 2, 0)
                        gate(NBLK - 1, 1)

                    @block.scalar
                    def _(act):
                        with act.Fori(0, NBLK // 2) as k:
                            for u in range(2):
                                act.wait_ge(s_tp, k * 2 + u + 1)
                                nc.scalar.activation(lt[:, u, :], ps[:, u, :], ACT.Identity).then_inc(s_lt, 1)

                    @block.sync
                    def _(sp):
                        rows_v = rows_dram.rearrange("(i t p) w -> i p t w", t=4, p=P)
                        for u in range(2):
                            sp.sem_inc(s_st[u], 16)
                        with sp.Fori(0, NBLK // 2) as k:
                            for u in range(2):
                                i = k * 2 + u
                                sp.wait_ge(s_xh, i + 1)
                                sp.sem_inc(s_z, 1)
                                sp.dma_start(rows_v[bass.ds(i, 1), :, :, 0:P].rearrange("i p t w -> (i p) t w"),
                                             xh[:, u, :].rearrange("p (t w) -> p t w", t=4)).then_inc(s_st[u], 16)
                        for u in range(2):
                            sp.wait_ge(s_st[u], NBLK // 2 * 16 + 16)

                    @block.gpsimd
                    def _(pool):
                        for n in range(ZC):
                            nc.gpsimd.dma_start(y_dram[n * 4096:(n + 1) * 4096, :].rearrange("(p r) w -> p (r w)", p=P),
                                                zero[:]).then_inc(s_yz, 16)
                        pool.wait_ge(s_yz, ZC * 16)

                def per_tile(v):
                    return v.unsqueeze(2).broadcast_to((P, NT, E))

                def per_expert(v):
                    return v.unsqueeze(1).broadcast_to((P, NT, E))

                s_e, s_t, s_thr = psem("exp"), psem("turned2"), psem("thr")
                with nc.Block() as block:
                    @block.vector
                    def _(dve):
                        link = Chain(dve, s_c)
                        link(nc.vector.tensor_reduce(n1[:], probs[:], AX.X, ALU.max))
                        nc.vector.tensor_tensor(probs[:], probs[:], per_tile(n1[:]), ALU.subtract).then_inc(s_e, 1)
                        dve.wait_ge(s_e, 2)
                        link(nc.vector.tensor_reduce(n1[:], probs[:], AX.X, ALU.add))
                        link(nc.vector.reciprocal(n1[:], n1[:]))
                        link(nc.vector.tensor_tensor(probs[:], probs[:], per_tile(n1[:]), ALU.mult))
                        last = C("last")
                        for src, oh in ((probs, oh1), (bb, oh2)):
                            link(nc.vector.tensor_reduce(n1[:], src[:], AX.X, ALU.max))
                            link(nc.vector.tensor_tensor(aa[:], src[:], per_tile(n1[:]), ALU.is_equal))
                            link(nc.vector.tensor_tensor(aa[:], aa[:], per_expert(last), ALU.mult))
                            link(nc.vector.tensor_reduce(n1[:], aa[:], AX.X, ALU.max))
                            link(nc.vector.tensor_tensor(oh[:], per_expert(last), per_tile(n1[:]), ALU.is_equal))
                            if oh is oh1:
                                link(nc.vector.scalar_tensor_tensor(out=bb[:], in0=oh[:], scalar=-2.0, in1=probs[:],
                                                                    op0=ALU.mult, op1=ALU.add))
                        link(nc.vector.tensor_tensor(aa[:], oh1[:], oh2[:], ALU.add))
                        link(nc.vector.tensor_tensor(wt[:], aa[:], probs[:], ALU.mult))
                        link(nc.vector.tensor_copy(wdest[:, :, 0, :], wt[:]))
                        link(nc.vector.scalar_tensor_tensor(out=wdest[:, :, 1, :], in0=oh2[:], scalar=float(T),
                                                            in1=per_tile(C("token")), op0=ALU.mult, op1=ALU.add))
                        nc.vector.tensor_copy(iota_b[:], C("iota")).then_inc(s_e, 1)

                    @block.scalar
                    def _(act):
                        act.wait_ge(s_e, 1)
                        nc.scalar.activation(probs[:], probs[:], ACT.Exp).then_inc(s_e, 1)

                    @block.tensor
                    def _(pe):
                        pe.wait_ge(s_e, 3)
                        for n in range(4):
                            ins = nc.tensor.transpose(ps[:, 0, n * P:(n + 1) * P],
                                                      wt[:, n * 16:(n + 1) * 16, :].rearrange("p t e -> p (t e)"), ident)

                weights = aa[:].rearrange("p t e -> p (t e)")
                flags = bb[:].rearrange("p t e -> p (t e)")
                with nc.Block() as block:
                    @block.sync
                    def _(sp):
                        sp.dma_start(rows_dram.rearrange("(t p) w -> p t w", p=P)[:, :, P:XW],
                                     wdest[:].rearrange("p t k e -> p t (k e)")).then_inc(s_row, 16)
                        sp.wait_ge(s_row, 16)

                    @block.vector
                    def _(dve):
                        link = Chain(dve, s_t)
                        link(nc.vector.tensor_copy(weights, ps[:, 0, :]))
                        link(nc.vector.memset(thr[:], 0))
                        with dve.Fori(0, 30) as i:
                            link = Chain(dve, s_t, i * 4 + 2)
                            link(nc.vector.tensor_tensor(cand[:], thr[:], bits[:, bass.ds(i, 1)], ALU.bitwise_or))
                            link(nc.vector.tensor_scalar(flags, weights, cand[:].bitcast(F32), None, ALU.is_ge, ALU.add,
                                                         accum_out=count[:]))
                            dve.wait_ge(s_thr, i + 1)
                            link(nc.vector.tensor_scalar(take[:], ps[:, 1, 0:1], float(CAP), -1.0, ALU.is_ge, ALU.mult))
                            dve.sem_inc(s_z, 1)
                            link(nc.vector.copy_predicated(thr[:], take[:], cand[:]))

                    @block.tensor
                    def _(pe):
                        with pe.Fori(0, 30) as i:
                            pe.wait_ge(s_t, i * 4 + 4)
                            nc.tensor.matmul(ps[:, 1, 0:1], C("same_expert"), count[:], start=True, stop=True)\
                                .then_inc(s_thr, 1)

                s_p, s_q, s_pos = psem("prefix_in"), psem("prefix_out"), psem("pos")
                sel, incl, rank = oh1, oh2, probs
                ones_row = zero[:, 0:NT]
                hi, lo = aa, bb
                with nc.Block() as block:
                    @block.vector
                    def _(dve):
                        link = Chain(dve, s_pos)
                        link(nc.vector.memset(ones_row, 1.0))
                        nc.vector.tensor_scalar(flags[:, 0:P], C("ones"), thr[:].bitcast(F32), None, ALU.mult)\
                            .then_inc(s_p, 1)
                        dve.wait_ge(s_q, 1)
                        link(nc.vector.tensor_copy(thr8[:], ps[:, 0, 0:E]))
                        link(nc.vector.tensor_tensor(sel[:], wt[:], per_expert(thr8[:]), ALU.is_gt))
                        link(nc.vector.tensor_tensor(bb[:], wt[:], per_expert(thr8[:]), ALU.is_equal))
                        nc.vector.scalar_tensor_tensor(out=aa[:], in0=wt[:], scalar=0.0, in1=bb[:],
                                                       op0=ALU.is_gt, op1=ALU.mult).then_inc(s_p, 1)

                        def ranks():
                            tot = ps[:, 2, :].rearrange("p (t e) -> p t e", e=E)
                            for e in range(E):
                                link(nc.vector.tensor_tensor_scan(incl[:, :, e], ones_row, tot[:, :, e], 0.0, ALU.mult,
                                                                  ALU.add))
                            link(nc.vector.tensor_tensor(incl[:], incl[:], tot, ALU.subtract))
                            link(nc.vector.tensor_tensor(rank[:], incl[:], ps[:, 1, :].rearrange("p (t e) -> p t e", e=E),
                                                         ALU.add))

                        dve.wait_ge(s_q, 2)
                        ranks()
                        link(nc.vector.tensor_reduce(room[:], ps[:, 3, :].rearrange("p (t e) -> p e t", e=E), AX.X, ALU.add))
                        link(nc.vector.tensor_scalar(room[:], room[:], -1.0, float(CAP), ALU.mult, ALU.add))
                        link(nc.vector.tensor_tensor(rank[:], rank[:], per_expert(room[:]), ALU.is_lt))
                        link(nc.vector.tensor_tensor(rank[:], rank[:], aa[:], ALU.mult))
                        nc.vector.tensor_tensor(sel[:], sel[:], rank[:], ALU.add).then_inc(s_p, 1)
                        dve.wait_ge(s_q, 3)
                        ranks()
                        link(nc.vector.tensor_copy(pos_i[:], rank[:]))
                        link(nc.vector.tensor_single_scalar(pos_i[:], pos_i[:], 7, ALU.logical_shift_right))
                        link(nc.vector.tensor_copy(hi[:], pos_i[:]))
                        link(nc.vector.scalar_tensor_tensor(out=lo[:], in0=hi[:], scalar=-float(P), in1=rank[:],
                                                            op0=ALU.mult, op1=ALU.add))
                        link(nc.vector.scalar_tensor_tensor(out=lo[:], in0=lo[:], scalar=1.0, in1=sel[:],
                                                            op0=ALU.add, op1=ALU.mult))
                        link(nc.vector.tensor_scalar(lo[:], lo[:], -1.0, None, ALU.add))
                        link(nc.vector.tensor_tensor(pay[:, :, 0, :], C("iota")[:, 0:SLOTS].unsqueeze(1)
                                                     .broadcast_to((P, TE, SLOTS)),
                                                     hi[:].rearrange("p t e -> p (t e)").unsqueeze(2)
                                                     .broadcast_to((P, TE, SLOTS)), ALU.is_equal))
                        for t in range(NT):
                            nc.vector.tensor_scalar(pay[:, t * E:(t + 1) * E, 1, :], pay[:, t * E:(t + 1) * E, 0, :],
                                                    float(t), None, ALU.mult)
                        link(nc.vector.tensor_scalar(n1[:, 0:1], C("partition"), 1.0, None, ALU.add))
                        link(nc.vector.tensor_scalar(pay[:, :, 0, :], pay[:, :, 0, :], n1[:, 0:1], None, ALU.mult))

                    @block.tensor
                    def _(pe):
                        pe.wait_ge(s_p, 1)
                        nc.tensor.transpose(ps[:, 0, 0:P], flags[:, 0:P], ident).then_inc(s_q, 1)
                        pe.wait_ge(s_p, 2)
                        tied, over = aa[:].rearrange("p t e -> p (t e)"), sel[:].rearrange("p t e -> p (t e)")
                        nc.tensor.matmul(ps[:, 1, :], C("before"), tied, start=True, stop=True)
                        nc.tensor.matmul(ps[:, 2, :], C("ones"), tied, start=True, stop=True)
                        nc.tensor.matmul(ps[:, 3, :], C("ones"), over, start=True, stop=True).then_inc(s_q, 1)
                        pe.wait_ge(s_p, 3)
                        nc.tensor.matmul(ps[:, 1, :], C("before"), over, start=True, stop=True)
                        nc.tensor.matmul(ps[:, 2, :], C("ones"), over, start=True, stop=True).then_inc(s_q, 1)

                s_oh, s_li = psem("onehot"), psem("list")
                lo_f = lo[:].rearrange("p t e -> p (t e)")
                with nc.Block() as block:
                    @block.vector
                    def _(dve):
                        with dve.Fori(0, NT // 2) as k:
                            for u in range(2):
                                tile = k * 2 + u
                                dve.wait_ge(s_li, k + 1)
                                for e in range(E):
                                    ins = nc.vector.tensor_scalar(oh_lo[:, u, e, :], iota_b[:],
                                                                  lo_f[:, bass.ds(tile * E + e, 1)], None, ALU.is_equal)
                                ins.then_inc(s_oh, 1)

                    @block.tensor
                    def _(pe):
                        def collect(tile, u, start, stop):
                            pe.wait_ge(s_oh, tile + 1)
                            for e in range(E):
                                rhs = pay[:, bass.ds(tile * E + e, 1), :, :].rearrange("p x k s -> p (x k s)")
                                ins = nc.tensor.matmul(ps[:, e, 0:2 * SLOTS], oh_lo[:, u, e, :], rhs, start=start, stop=stop)
                            return ins

                        pe.sem_inc(s_li, 1)
                        collect(0, 0, True, False)
                        collect(1, 1, False, False).then_inc(s_li, 1)
                        with pe.Fori(1, NT // 2 - 1) as k:
                            collect(k * 2, 0, False, False)
                            collect(k * 2 + 1, 1, False, False).then_inc(s_li, 1)
                        collect(NT - 2, 0, False, False)
                        collect(NT - 1, 1, False, True).then_inc(s_li, 1)

                s_f = psem("final")
                with nc.Block() as block:
                    @block.vector
                    def _(dve):
                        link = Chain(dve, s_f)
                        link(nc.vector.tensor_copy(slot[:], ps[:, :, 0:2 * SLOTS]))
                        first, tile = slot[:, :, 0:SLOTS], slot[:, :, SLOTS:2 * SLOTS]
                        link(nc.vector.tensor_scalar(valid[:], first, 0.5, None, ALU.is_gt))
                        link(nc.vector.scalar_tensor_tensor(out=tile, in0=tile, scalar=float(P), in1=first,
                                                            op0=ALU.mult, op1=ALU.add))
                        link(nc.vector.tensor_scalar(gather_i[:], tile, -1.0, 0.0, ALU.add, ALU.max))
                        link(nc.vector.tensor_scalar(spare[:], valid[:], -1.0, 1.0, ALU.mult, ALU.add))
                        link(nc.vector.tensor_tensor(spare[:].rearrange("p e s -> p (e s)"),
                                                     spare[:].rearrange("p e s -> p (e s)"), C("spare_row"), ALU.mult))

        routing()

        def experts():
            with ExitStack() as ph:
                def psb(name, shape, dt=F32):
                    return sb("ex_" + name, shape, dt, ph)

                def psem(name):
                    return sem("ex_" + name, ph)

                NB2 = SLOTS // 2
                NBUF = 5
                BL = E * NB2
                we1, we2 = psb("we1", [P, 2, HID]), psb("we2", [P, 2, EC, P])
                be = psb("be", [P, E * EC])
                be2 = psb("be2", [P, E, P])
                bs = psb("bs", [P, 2, EC])
                xg = psb("xg", [P, NBUF, 2, XW])
                xt = psb("xt", [P, 2, S])
                ht = psb("ht", [P, EC, S])
                yw = psb("yw", [P, NBUF, 2, P])
                ycol = psb("ycol", [P, NBUF, 2])
                scat = psb("scat", [P, NBUF, 2], I32)
                s_b, s_tp, s_xt, s_h, s_ht, s_y, s_ys, s_c, s_bs = (
                    psem(n) for n in ("biases", "turned", "xt", "hidden", "gelu", "y", "y_ready", "chain", "bias_ready"))
                s_w = [psem(f"weights{u}") for u in range(2)]
                s_xg = [psem(f"gathered{u}") for u in range(NBUF)]
                s_sc = [psem(f"scattered{u}") for u in range(NBUF)]
                s_hold = psem("hold")

                with nc.Block() as block:
                    @block.sync
                    def _(sp):
                        sp.dma_start(be[:], a["eb1"]).then_inc(s_b, 16)
                        sp.dma_start(be2[:], a["eb2"]).then_inc(s_b, 16)
                        sp.wait_ge(s_b, 32)

                with nc.Block() as block:
                    @block.sync
                    def _(sp):
                        def load(e, u):
                            sp.dma_start(we1[:, u, :], a["ew1"][bass.ds(e, 1), :, :].rearrange("e p f -> (e p) f"))\
                                .then_inc(s_w[u], 16)
                            sp.dma_start(we2[:, u, :, :], a["ew2"][bass.ds(e, 1), :, :]
                                         .rearrange("e (c p) d -> (e p) c d", p=P)).then_inc(s_w[u], 16)

                        for u in range(2):
                            load(u, u)
                        with sp.Fori(1, E // 2) as k:
                            for u in range(2):
                                sp.wait_ge(s_y, (k * 2 + u - 1) * NB2)
                                sp.sem_inc(s_hold, 1)
                                load(k * 2 + u, u)

                    @block.gpsimd
                    def _(pool):
                        for n in range(BL + 3):
                            if n < BL:
                                if n >= NBUF:
                                    pool.wait_ge(s_ys, n - NBUF + 1)
                                for t in range(2):
                                    nc.gpsimd.indirect_dma_start(
                                        out=xg[:, n % NBUF, t, :], out_offset=None, in_=rows_dram,
                                        in_offset=bass.IndirectOffsetOnAxis(
                                            ap=gather_i[:, n // NB2, n % NB2 * 2 + t:n % NB2 * 2 + t + 1], axis=0),
                                    ).then_inc(s_xg[n % NBUF], 16)
                            m = n - 3
                            if m >= 0:
                                pool.wait_ge(s_ys, m + 1)
                                for t in range(2):
                                    nc.gpsimd.indirect_dma_start(
                                        out=y_dram, in_=yw[:, m % NBUF, t, :], in_offset=None,
                                        out_offset=bass.IndirectOffsetOnAxis(ap=scat[:, m % NBUF, t:t + 1], axis=0),
                                    ).then_inc(s_sc[m % NBUF], 16)
                        for u in range(NBUF):
                            pool.wait_ge(s_sc[u], 32 * (BL // NBUF))

                    @block.vector
                    def _(dve):
                        def evac(n, j):
                            dve.wait_ge(s_tp, n + 1)
                            nc.vector.tensor_copy(xt[:, j % 2, :], ps[:, j % 2, 0:S]).then_inc(s_xt, 1)

                        def weigh(k, j, first):
                            n, e, buf, s = k * 2 * NB2 + j, k * 2 + j // NB2, j % NBUF, j % NB2 * 2
                            link = Chain(dve, s_c, n * 2)
                            for t in range(2):
                                x = e * SLOTS + s + t
                                ins = nc.vector.scalar_tensor_tensor(
                                    out=ycol[:, buf, t:t + 1], in0=xg[:, buf, t, bass.ds(P + E + e, 1)],
                                    scalar=valid_f[:, bass.ds(x, 1)], in1=spare_f[:, bass.ds(x, 1)],
                                    op0=ALU.mult, op1=ALU.add)
                            link(ins)
                            dve.wait_ge(s_y, n + 1)
                            dve.sem_inc(s_hold, 1)
                            if not (first and j < NBUF):
                                dve.wait_ge(s_sc[buf], (k * 2 + j // NBUF) * 32)
                                dve.sem_inc(s_hold, 1)
                            link(nc.vector.tensor_tensor(yw[:, buf, :, :], ps[:, 6 + j % 2, 0:S].rearrange("p (t d) -> p t d", t=2),
                                                         be2[:, bass.ds(e, 1), :].broadcast_to((P, 2, P)), ALU.add))
                            nc.vector.tensor_copy(scat[:, buf, :], ycol[:, buf, :])
                            for t in range(2):
                                ins = nc.vector.tensor_scalar(yw[:, buf, t, :], yw[:, buf, t, :],
                                                              xg[:, buf, t, bass.ds(P + e, 1)], None, ALU.mult)
                            ins.then_inc(s_ys, 1)

                        valid_f = valid[:].rearrange("p e s -> p (e s)")
                        spare_f = spare[:].rearrange("p e s -> p (e s)")

                        def pair(k, first=False, final=False):
                            for j in range(2 * NB2):
                                if j % NB2 == 0:
                                    u = j // NB2
                                    nc.vector.tensor_copy(bs[:, u, :], be[:, bass.ds((k * 2 + u) * EC, EC)])\
                                        .then_inc(s_bs, 1)
                                if not (final and j == 2 * NB2 - 1):
                                    evac(k * 2 * NB2 + j + 1, j + 1)
                                weigh(k, j, first)

                        evac(0, 0)
                        pair(0, first=True)
                        with dve.Fori(1, E // 2 - 1) as k:
                            pair(k)
                        pair(E // 2 - 1, final=True)

                    @block.tensor
                    def _(pe):
                        def turn(k, j):
                            pe.wait_ge(s_xg[j % NBUF], 32 * (k * 2 + j // NBUF + 1))
                            for t in range(2):
                                ins = nc.tensor.transpose(ps[:, j % 2, t * P:(t + 1) * P], xg[:, j % NBUF, t, 0:P], ident)
                            ins.then_inc(s_tp, 1)

                        def hidden(k, j):
                            n, u = k * 2 * NB2 + j, j // NB2
                            pe.wait_ge(s_xt, n + 1)
                            if j % NB2 == 0:
                                pe.wait_ge(s_w[u], 32 * (k + 1))
                            for c in range(EC):
                                ins = nc.tensor.matmul(ps[:, 2 + c // 2, c % 2 * S:(c % 2 + 1) * S],
                                                       we1[:, u, c * P:(c + 1) * P], xt[:, j % 2, :], start=True, stop=True)
                                if c % 2:
                                    ins.then_inc(s_h, 1)

                        def output(k, j):
                            n, u = k * 2 * NB2 + j, j // NB2
                            pe.wait_ge(s_ht, (n + 1) * EC)
                            for t in range(2):
                                for c in range(EC):
                                    ins = nc.tensor.matmul(ps[:, 6 + j % 2, t * P:(t + 1) * P], ht[:, c, t * P:(t + 1) * P],
                                                           we2[:, u, c, :], start=(c == 0), stop=(c == EC - 1))
                            ins.then_inc(s_y, 1)

                        def pair(k, final):
                            for j in range(2 * NB2):
                                hidden(k, j)
                                if j < 2 * NB2 - 1:
                                    turn(k, j + 1)
                                elif not final:
                                    turn(k + 1, 0)
                                output(k, j)

                        turn(0, 0)
                        with pe.Fori(0, E // 2 - 1) as k:
                            pair(k, False)
                        pair(E // 2 - 1, True)

                    @block.scalar
                    def _(act):
                        nc.scalar.preload_act_table(ACT.Gelu)
                        with act.Fori(0, E // 2) as k:
                            for j in range(2 * NB2):
                                n, u = k * 2 * NB2 + j, j // NB2
                                if j % NB2 == 0:
                                    act.wait_ge(s_bs, k * 2 + u + 1)
                                    act.sem_inc(s_hold, 1)
                                for c in range(EC):
                                    act.wait_ge(s_h, n * 2 + c // 2 + 1)
                                    nc.scalar.activation(ht[:, c, :], ps[:, 2 + c // 2, c % 2 * S:(c % 2 + 1) * S], ACT.Gelu,
                                                         bias=bs[:, u, c:c + 1]).then_inc(s_ht, 1)

        experts()

        with ExitStack() as ph:
            CT = 8
            STEPS = NT // CT
            yy = sb("fin_y", [P, 2, 2, CT * P], c=ph)
            s_ld = [sem(f"fin_load{u}", ph) for u in range(2)]
            s_c, s_fin, s_out, s_hold = sem("fin_chain", ph), sem("fin_sum", ph), sem("fin_stored", ph), sem("fin_hold", ph)
            out_v = out.rearrange("b s d -> (b s) d").rearrange("(i t p) d -> i p t d", t=CT, p=P)
            y_v = y_dram[0:2 * T, :].rearrange("(c i t p) d -> c i p t d", c=2, t=CT, p=P)
            with nc.Block() as block:
                @block.sync
                def _(sp):
                    def load(i, u):
                        for c in range(2):
                            sp.dma_start(yy[:, u, c, :].rearrange("p (t d) -> p t d", t=CT),
                                         y_v[c, bass.ds(i, 1)].rearrange("i p t d -> (i p) t d")).then_inc(s_ld[u], 16)

                    load(0, 0)
                    load(1, 1)
                    with sp.Fori(1, STEPS // 2) as k:
                        for u in range(2):
                            sp.wait_ge(s_fin, k * 2 + u - 1)
                            sp.sem_inc(s_hold, 1)
                            load(k * 2 + u, u)

                @block.vector
                def _(dve):
                    with dve.Fori(0, STEPS // 2) as k:
                        for u in range(2):
                            i = k * 2 + u
                            link = Chain(dve, s_c, i)
                            xb = x2[:, bass.ds(i * CT * P, CT * P)]
                            dve.wait_ge(s_ld[u], 32 * (k + 1))
                            link(nc.vector.tensor_tensor(yy[:, u, 0, :], yy[:, u, 0, :], yy[:, u, 1, :], ALU.add))
                            nc.vector.tensor_tensor(xb, xb, yy[:, u, 0, :], ALU.add).then_inc(s_fin, 1)

                @block.scalar
                def _(act):
                    with act.Fori(0, STEPS) as i:
                        act.wait_ge(s_fin, i + 1)
                        act.sem_inc(s_hold, 1)
                        act.dma_start(out_v[bass.ds(i, 1)].rearrange("i p t d -> (i p) t d"),
                                      x2[:, bass.ds(i * CT * P, CT * P)].rearrange("p (t d) -> p t d", t=CT))\
                            .then_inc(s_out, 16)
                    act.wait_ge(s_out, 16 * STEPS)


def host_layout(x, **w):
    w = {k: np.ascontiguousarray(v) for k, v in w.items()}
    t = {k[7:]: v for k, v in w.items() if k.startswith("L0_tok_")}
    col = lambda v: v.reshape(-1, P).T
    rep = lambda v: np.broadcast_to(v[None], (P,) + v.shape)
    return {k: np.ascontiguousarray(v) for k, v in {
        "ids": np.asarray(x, np.int32).reshape(NT, P).T,
        "consts": shape_constants(),
        "emb": t["emb"], "pos": t["pos"], "Wqk": t["Wqk"], "Wv": t["Wv"], "Wo": t["Wo"], "rots": t["rots"],
        "W1": t["W1"], "W2": t["W2"], "ln1_b0": col(t["ln1_b"][0]),
        "b1c": t["b1"].reshape(2, FC, P).transpose(2, 0, 1), "b2r": rep(t["b2"]),
        "lncol": np.concatenate([col(v) for v in (t["ln1_s"][1], t["ln1_b"][1], t["ln2_s"][0], t["ln2_b"][0],
                                                  t["ln2_s"][1], t["ln2_b"][1], w["L0_attn_ln_gamma"],
                                                  w["L0_attn_ln_beta"])], 1),
        "W_gh": w["L0_attn_W_gh"], "gate_wT": w["L0_ffn_gate_w"].T, "gate_b": rep(w["L0_ffn_gate_b"]),
        "bits": np.broadcast_to(1 << np.arange(29, -1, -1, dtype=np.int32)[None], (P, 30)),
        "ew1": w["L0_ffn_w1"], "ew2": w["L0_ffn_w2"],
        "eb1": w["L0_ffn_b1"].reshape(E * EC, P).T, "eb2": rep(w["L0_ffn_b2"]),
    }.items()}


_OUTS = [((B, S, P), "float32")]


def kernel(**inputs):
    import numpy as _np
    import concourse.bacc as _bacc
    from concourse import mybir as _mybir
    from concourse.bass_utils import run_bass_kernel_spmd as _run

    nc = _bacc.Bacc("TRN2", target_bir_lowering=False, num_devices=1)
    arrays, args = {}, {}
    for name, v in host_layout(**inputs).items():
        arrays[f"in_{name}_dram"] = v
        args[name] = nc.dram_tensor(f"in_{name}_dram", v.shape, _mybir.dt.from_np(v.dtype), kind="ExternalInput").ap()
    shape, dtype = _OUTS[0]
    out = nc.dram_tensor("out_0_dram", shape, _mybir.dt.from_np(_np.dtype(dtype)), kind="ExternalOutput").ap()
    build(nc, args, out)
    r = _run(nc, [arrays], core_ids=[0])
    return r.results[0]["out_0_dram"]
```

```python
from contextlib import ExitStack

import numpy as np

import concourse.bass as bass
from concourse import mybir

ALU = mybir.AluOpType
ACT = mybir.ActivationFunctionType
AX = mybir.AxisListType
F32 = mybir.dt.float32
BF16 = mybir.dt.bfloat16
I32 = mybir.dt.int32

P = 128
B, S = 32, 256
T = B * S
NT = T // P
V = 8000
F = 512
FC = F // P
H, DH = 8, 16
NHASH, NBUCKET, CS = 4, 64, 64
NC_ = S // CS
NK = NBUCKET // 2
BLK = 512
NBLK = T // BLK
GB = 4
NG = B // GB
GT = GB * S
E, HID, EC = 8, 512, 4
CAP = int(1.2 * T / E)
SLOTS = -(-CAP // P)
LN_EPS = 1e-5
GRU_EPS = 1e-10

_COLS = {}
_WIDTH = 0
for _name, _n in (("ident", P), ("block_sum", P), ("window", 32), ("den_sum", P), ("before", P),
                  ("same_expert", P), ("iota", P), ("first_k", NK), ("guard", 1), ("guard_eps", 1), ("pair_rows", 2), ("head_rows", 4),
                  ("partition", 1), ("ranks", 3), ("ones", P), ("last", E),
                  ("token", NT), ("spare_row", E * SLOTS)):
    _COLS[_name] = (_WIDTH, _WIDTH + _n)
    _WIDTH += _n


def shape_constants():
    c = np.zeros((P, _WIDTH), np.float32)
    p, q = np.meshgrid(np.arange(P), np.arange(P), indexing="ij")

    def put(name, value):
        lo, hi = _COLS[name]
        c[:, lo:hi] = np.broadcast_to(value, (P, max(hi - lo, value.shape[1])))[:, :hi - lo]

    put("ident", p == q)
    put("block_sum", p // 32 == q // 32)
    same_head, same_hash = p // 16 == q // 16, p % 4 == q % 4
    cp, cq = p % 16 // 4, q % 16 // 4
    put("window", (p < 32) & same_head & same_hash & ((cp == cq) | (cp == (cq + 1) % NC_)))
    put("den_sum", NHASH * (same_head & same_hash))
    put("before", p < q)
    put("same_expert", p % E == q % E)
    put("iota", q)
    put("first_k", NK - np.arange(NK)[None, :])
    guard = np.arange(P)[:, None] % 32 == 16
    put("guard", guard)
    put("guard_eps", 1e-6 * guard)
    put("pair_rows", np.arange(P)[:, None] % 32 // 16 == np.arange(2)[None, :])
    put("head_rows", (np.arange(P)[:, None] // 32 == np.arange(4)[None, :]) * np.where(guard, -1.0, 1.0))
    put("partition", np.arange(P)[:, None])
    put("ranks", CS * np.arange(1, NC_)[None, :])
    put("ones", np.ones((P, P)))
    put("last", E - np.arange(E)[None, :])
    put("token", np.arange(NT)[None, :] * P + np.arange(P)[:, None])
    put("spare_row", 2 * T + np.arange(E * SLOTS)[None, :] * P + np.arange(P)[:, None])
    return c


class Chain:

    def __init__(self, eng, sem, base=0):
        self.eng, self.sem, self.base, self.n = eng, sem, base, 0

    def __call__(self, ins):
        self.n += 1
        ins.then_inc(self.sem, 1)
        self.eng.wait_ge(self.sem, self.base + self.n)


def build(nc, a, out):
    with ExitStack() as ctx:
        def sb(name, shape, dt=F32, c=ctx):
            return c.enter_context(nc.sbuf_tensor(name, shape, dt))

        def sem(name, c=ctx):
            return c.enter_context(nc.semaphore(name))

        ps = ctx.enter_context(nc.psum_tensor("ps", [P, 8, 512], F32))
        x1 = sb("x1", [P, NT * P])
        x2 = sb("x2", [P, NT * P])
        const = sb("const", [P, _WIDTH])
        stats = sb("stats", [P, NT, 6])
        mean = sb("mean", [P, NT])
        rstd = sb("rstd", [P, NT])
        tmp = sb("tmp", [P, 2, NT])
        b1c = sb("b1c", [P, 2, FC])
        b2r = sb("b2r", [P, 2, P])
        lncol = sb("lncol", [P, 8])
        s_load = sem("s_load")
        s_dv = sem("s_dv")
        s_sq = sem("s_sq")
        dv_count = [0]

        def C(name):
            return const[:, _COLS[name][0]:_COLS[name][1]]

        ident = C("ident")

        def finish_stats(dve, act_block_sem):
            link = Chain(dve, s_dv, dv_count[0])
            me, mo = stats[:, :, 1], stats[:, :, 4]
            link(nc.vector.tensor_tensor(mean[:], me, mo, ALU.add))
            link(nc.vector.tensor_tensor(tmp[:, 0, :], me, mo, ALU.subtract))
            link(nc.vector.tensor_scalar(mean[:], mean[:], 0.5, None, ALU.mult))
            link(nc.vector.scalar_tensor_tensor(out=tmp[:, 0, :], in0=tmp[:, 0, :], scalar=0.25, in1=tmp[:, 0, :],
                                                op0=ALU.mult, op1=ALU.mult))
            link(nc.vector.tensor_tensor(tmp[:, 1, :], stats[:, :, 2], stats[:, :, 5], ALU.add))
            link(nc.vector.scalar_tensor_tensor(out=tmp[:, 1, :], in0=tmp[:, 1, :], scalar=1.0 / P, in1=tmp[:, 0, :],
                                                op0=ALU.mult, op1=ALU.add))
            return link

        def rstd_phase(name, eps, gru=False):
            s_var = sem(f"{name}_var")
            s_root = sem(f"{name}_root")
            with nc.Block() as block:
                @block.vector
                def _(dve):
                    link = finish_stats(dve, s_var)
                    nc.vector.tensor_scalar(tmp[:, 0, :], tmp[:, 1, :], eps, None, ALU.add).then_inc(s_var, 1)
                    dve.wait_ge(s_root, 1)
                    link(nc.vector.reciprocal(rstd[:], rstd[:]))
                    if gru:
                        link(nc.vector.tensor_tensor(tmp[:, 0, :], rstd[:], rstd[:], ALU.mult))
                        link(nc.vector.tensor_tensor(tmp[:, 1, :], tmp[:, 1, :], tmp[:, 0, :], ALU.mult))
                        nc.vector.tensor_scalar(tmp[:, 0, :], tmp[:, 1, :], GRU_EPS, None, ALU.add).then_inc(s_var, 1)
                        dve.wait_ge(s_root, 2)
                        link(nc.vector.reciprocal(gru_r[:], gru_r[:]))
                    dv_count[0] += link.n

                @block.scalar
                def _(act):
                    act.wait_ge(s_var, 1)
                    nc.scalar.activation(rstd[:], tmp[:, 0, :], ACT.Sqrt).then_inc(s_root, 1)
                    if gru:
                        act.wait_ge(s_var, 2)
                        nc.scalar.activation(gru_r[:], tmp[:, 0, :], ACT.Sqrt).then_inc(s_root, 1)

        gru_r = sb("gru_r", [P, NT])

        with ExitStack() as ph:
            pos = sb("pos", [P, 2, P], c=ph)
            posc = sb("posc", [P, 2, P], c=ph)
            ids = sb("ids", [P, NT], I32, c=ph)
            idf = sb("idf", [P, 2, NT], c=ph)
            wv0 = sb("wv0", [P, P], c=ph)
            wo0 = sb("wo0", [P, P], c=ph)
            lb0 = sb("lb0", [P, 1], c=ph)
            t1 = sb("t1", [P, P], c=ph)
            GG = 8
            s_ids = sem("s_ids")
            s_idx = sem("s_idx")
            s_gather = [sem(f"s_gather{g}") for g in range(GG)]
            s_c0 = sem("s_c0")
            s_t1 = sem("s_t1")
            s_x = sem("s_x")
            NLOAD = 12
            with nc.Block() as block:
                @block.sync
                def _(sp):
                    sp.dma_start(ids[:], a["ids"]).then_inc(s_ids, 16)
                    sp.dma_start(const[:], a["consts"]).then_inc(s_load, 16)
                    sp.dma_start(pos[:], a["pos"][0, 0:S, :].rearrange("(t p) d -> p t d", p=P)).then_inc(s_load, 16)
                    sp.dma_start(wv0[:], a["Wv"][0]).then_inc(s_load, 16)
                    sp.dma_start(wo0[:], a["Wo"][0]).then_inc(s_load, 16)
                    sp.dma_start(lb0[:], a["ln1_b0"]).then_inc(s_load, 16)
                    sp.dma_start(b1c[:], a["b1c"]).then_inc(s_load, 16)
                    sp.dma_start(b2r[:], a["b2r"]).then_inc(s_load, 16)
                    sp.dma_start(lncol[:], a["lncol"]).then_inc(s_load, 16)
                    sp.wait_ge(s_load, 8 * 16)

                @block.vector
                def _(dve):
                    link = Chain(dve, s_dv, dv_count[0])
                    dve.wait_ge(s_ids, 16)
                    link(nc.vector.tensor_copy(idf[:, 0, :], ids[:]))
                    link(nc.vector.tensor_scalar(idf[:, 1, :], idf[:, 0, :], 0.0, float(V), ALU.is_lt, ALU.mult))
                    link(nc.vector.tensor_tensor(idf[:, 0, :], idf[:, 0, :], idf[:, 1, :], ALU.add))
                    nc.vector.tensor_scalar(ids[:], idf[:, 0, :], 0.0, float(V - 1), ALU.max, ALU.min).then_inc(s_idx, 1)
                    dve.wait_ge(s_c0, 1)
                    nc.vector.tensor_scalar(t1[:], C("ones"), ps[:, 0, 0:1], None, ALU.mult).then_inc(s_t1, 1)
                    dve.wait_ge(s_c0, 2)
                    for t in range(2):
                        link(nc.vector.tensor_tensor(posc[:, t, :], ps[:, 1, 0:P], pos[:, t, :], ALU.add))
                    for g in range(GG):
                        n = NT // GG
                        dve.wait_ge(s_gather[g], 16 * n)
                        for t in range(g * n, (g + 1) * n):
                            nc.vector.tensor_tensor(x1[:, t * P:(t + 1) * P], x1[:, t * P:(t + 1) * P], posc[:, t % 2, :],
                                                    ALU.add).then_inc(s_x, 1)
                        dve.wait_ge(s_x, (g + 1) * n)
                        for t in range(g * n, (g + 1) * n):
                            nc.vector.bn_stats(stats[:, t, :], x1[:, t * P:(t + 1) * P])
                    dv_count[0] += link.n

                @block.tensor
                def _(pe):
                    pe.wait_ge(s_load, 128)
                    nc.tensor.matmul(ps[:, 0, 0:1], wv0[:], lb0[:], start=True, stop=True).then_inc(s_c0, 1)
                    pe.wait_ge(s_t1, 1)
                    nc.tensor.matmul(ps[:, 1, 0:P], t1[:], wo0[:], start=True, stop=True).then_inc(s_c0, 1)

                @block.gpsimd
                def _(pool):
                    pool.wait_ge(s_idx, 1)
                    for t in range(NT):
                        nc.gpsimd.indirect_dma_start(
                            out=x1[:, t * P:(t + 1) * P], out_offset=None, in_=a["emb"],
                            in_offset=bass.IndirectOffsetOnAxis(ap=ids[:, t:t + 1], axis=0),
                        ).then_inc(s_gather[t // (NT // GG)], 16)

        rstd_phase("ln2_0", LN_EPS)

        def feed_forward(layer):
            with ExitStack() as ph:
                L = f"f{layer}_"
                xh = sb(L + "xh", [P, 2, BLK], c=ph)
                lt = sb(L + "lt", [P, 2, BLK], c=ph)
                ht = sb(L + "ht", [P, FC, BLK], c=ph)
                w1 = sb(L + "w1", [P, F], c=ph)
                w2 = sb(L + "w2", [P, FC, P], c=ph)
                s_w = sem(L + "weights")
                s_xh, s_tp, s_lt = sem(L + "normed"), sem(L + "turned"), sem(L + "lt_ready")
                s_h, s_ht, s_y = sem(L + "hidden"), sem(L + "gelu"), sem(L + "output")
                s_x2 = sem(L + "x2")
                lns, lnb = lncol[:, 2 + 2 * layer:3 + 2 * layer], lncol[:, 3 + 2 * layer:4 + 2 * layer]
                STEPS = 1 if layer == 0 else 4
                H0, Y0 = 2, 6

                with nc.Block() as block:
                    @block.sync
                    def _(sp):
                        sp.dma_start(w1[:], a["W1"][layer]).then_inc(s_w, 16)
                        sp.dma_start(w2[:], a["W2"][layer].rearrange("(c p) d -> p c d", p=P)).then_inc(s_w, 16)

                    @block.vector
                    def _(dve):
                        def norm(i, u):
                            for t in range(4):
                                ins = nc.vector.tensor_scalar(
                                    xh[:, u, t * P:(t + 1) * P], x1[:, bass.ds(i * BLK + t * P, P)],
                                    mean[:, bass.ds(i * 4 + t, 1)], rstd[:, bass.ds(i * 4 + t, 1)],
                                    ALU.subtract, ALU.mult)
                            ins.then_inc(s_xh, 1)

                        def residual(i, u):
                            link = Chain(dve, s_x2, i * STEPS)
                            x2b = x2[:, bass.ds(i * BLK, BLK)]
                            x2v = x2b.rearrange("p (t d) -> p t d", t=4)
                            bias = b2r[:, layer, :].unsqueeze(1).broadcast_to((P, 4, P))
                            dve.wait_ge(s_y, i + 1)
                            if layer == 0:
                                y = ps[:, Y0 + u, :].rearrange("p (t d) -> p t d", t=4)
                                link(nc.vector.tensor_tensor(x2v, y, bias, ALU.add))
                            else:
                                link(nc.vector.tensor_tensor(x2b, ps[:, Y0 + u, :], x2b, ALU.add))
                                link(nc.vector.tensor_tensor(x2v, x2v, bias, ALU.add))
                                link(nc.vector.tensor_tensor(x2b, x2b, x1[:, bass.ds(i * BLK, BLK)], ALU.add))
                                link(nc.vector.tensor_scalar(x2b, x2b, 0.5, None, ALU.mult))
                            for t in range(4):
                                nc.vector.bn_stats(stats[:, bass.ds(i * 4 + t, 1), :].rearrange("p a b -> p (a b)"),
                                                   x2[:, bass.ds(i * BLK + t * P, P)])

                        norm(0, 0)
                        with dve.Fori(0, NBLK // 2 - 1) as k:
                            for u in range(2):
                                norm(k * 2 + u + 1, 1 - u)
                                residual(k * 2 + u, u)
                        norm(NBLK - 1, 1)
                        residual(NBLK - 2, 0)
                        residual(NBLK - 1, 1)

                    @block.tensor
                    def _(pe):
                        def turn(i, u):
                            pe.wait_ge(s_xh, i + 1)
                            for t in range(4):
                                ins = nc.tensor.transpose(ps[:, u, t * P:(t + 1) * P], xh[:, u, t * P:(t + 1) * P], ident)
                            ins.then_inc(s_tp, 1)

                        def hidden(i, u):
                            pe.wait_ge(s_lt, i + 1)
                            for c in range(FC):
                                nc.tensor.matmul(ps[:, H0 + c, :], w1[:, c * P:(c + 1) * P], lt[:, u, :],
                                                 start=True, stop=True).then_inc(s_h, 1)

                        def output(i, u):
                            pe.wait_ge(s_ht, i * FC + FC)
                            for t in range(4):
                                for c in range(FC):
                                    ins = nc.tensor.matmul(ps[:, Y0 + u, t * P:(t + 1) * P],
                                                           ht[:, c, t * P:(t + 1) * P], w2[:, c, :],
                                                           start=(c == 0), stop=(c == FC - 1))
                            ins.then_inc(s_y, 1)

                        pe.wait_ge(s_w, 32)
                        turn(0, 0)
                        with pe.Fori(0, NBLK // 2 - 1) as k:
                            for u in range(2):
                                hidden(k * 2 + u, u)
                                turn(k * 2 + u + 1, 1 - u)
                                output(k * 2 + u, u)
                        hidden(NBLK - 2, 0)
                        turn(NBLK - 1, 1)
                        output(NBLK - 2, 0)
                        hidden(NBLK - 1, 1)
                        output(NBLK - 1, 1)

                    @block.scalar
                    def _(act):
                        nc.scalar.preload_act_table(ACT.Gelu_apprx_tanh)

                        def evac(i, u):
                            act.wait_ge(s_tp, i + 1)
                            nc.scalar.activation(lt[:, u, :], ps[:, u, :], ACT.Identity, scale=lns, bias=lnb)\
                                .then_inc(s_lt, 1)

                        def gelus(i):
                            for c in range(FC):
                                act.wait_ge(s_h, i * FC + c + 1)
                                nc.scalar.activation(ht[:, c, :], ps[:, H0 + c, :], ACT.Gelu_apprx_tanh,
                                                     bias=b1c[:, layer, c:c + 1]).then_inc(s_ht, 1)

                        evac(0, 0)
                        with act.Fori(0, NBLK // 2 - 1) as k:
                            for u in range(2):
                                gelus(k * 2 + u)
                                evac(k * 2 + u + 1, 1 - u)
                        gelus(NBLK - 2)
                        evac(NBLK - 1, 1)
                        gelus(NBLK - 1)

        feed_forward(0)
        rstd_phase("ln1_1", LN_EPS)

        def attention():
            with ExitStack() as ph:
                def psb(name, shape, dt=F32):
                    return sb("at_" + name, shape, dt, ph)

                def psem(name):
                    return sem("at_" + name, ph)

                QP = 32
                HS = 4
                NS = H // HS
                HP = H // 2
                W3 = 3 * 32
                wqk = psb("wqk", [P, NS, HS, QP])
                wv = psb("wv", [P, H, 32])
                wo = psb("wo", [P, P])
                rots = psb("rots", [P, NS, HS * NHASH * NK])
                xh = psb("xh", [P, 2, BLK])
                lt = psb("lt", [P, 2, BLK])
                sq = psb("sq", [P, NS, GT])
                nrm = psb("nrm", [P, NS, GT])
                qk_ = psb("qk", [P, 2, NS, GT])
                scale_ = psb("scale", [P, 2, NS * 8 * HS])
                vp_ = psb("vp", [P, 2, GT // P, H, 32])
                cn_ = psb("cn", [P, 2, 2, GB, P], BF16)
                qd = psb("qd", [P, 2, NS, HS, S])
                wd = psb("wd", [W3, HP, 2, S], BF16)
                ee = psb("ee", [P, 2, 2, H, S])
                cp = psb("cp", [P, 2, 2, H, 32])
                hi_ = psb("hi", [P, 2, H * NHASH])
                ext_ = psb("ext", [P, 2, H * NHASH])
                wins_ = psb("pos_wins", [P, 2, H * NHASH], I32)
                hit_ = [lt[:, i, :].bitcast(BF16).rearrange("p (x k) -> p x k", k=NK) for i in range(2)]
                identb = psb("identb", [P, P], BF16)
                windowb = psb("windowb", [W3, 32], BF16)
                fk = psb("fk", [P, NK], BF16)
                bt = psb("bt", [P, 2, GB, H * NHASH])
                rows, chunk = nrm[:, 0, 0:S], nrm[:, 0, S:2 * S]
                flags = nrm[:, 1, :].rearrange("p (k w) -> p k w", w=S)
                ct = psb("ct", [W3, HP, S], BF16)
                mt, xw, rc, ws, ot = (psb(n, [P, S]) for n in ("mt", "xw", "rc", "ws", "ot"))
                wb = psb("wb", [P, 3, S], BF16)
                thr = psb("thr", [P, 6, 3])
                ones = psb("ones", [P, S])
                ctb = ps[0:W3, 2, :].bitcast(BF16).rearrange("p (a w) -> p a w", w=S)
                s_cp = psem("cp")
                s_hold = psem("hold")
                s_zero, s_w = psem("zero"), psem("weights")
                s_xh, s_tp, s_lt, s_q, s_v, s_sq, s_vp, s_qc, s_n2, s_nrm, s_qk, s_kt, s_scale = (
                    psem(n) for n in ("normed", "turned", "lt", "q", "v", "squares", "vp", "q_copied", "norm2", "norm",
                                      "qk", "keys_turned", "scale"))
                s_rot, s_hit, s_hm, s_am, s_bt, s_chunk, s_chT, s_c = (
                    psem(n) for n in ("rot", "hit", "hit_index", "argmax", "buckets_turned", "chunk", "chunk_turned", "c"))
                s_qd, s_s, s_exp, s_ct, s_cts, s_mt, s_mts, s_d, s_xw, s_den, s_ws, s_sel, s_wd, s_g, s_a, s_o, s_ot, s_y, s_x1 = (
                    psem(n) for n in ("qd", "scores", "exp", "ct", "ct_out", "mt", "mt_out", "d", "xw", "den", "ws", "sel",
                                      "wd", "g", "a", "o", "ot", "y", "x1"))
                s_ch, s_cw = psem("chain"), psem("chain_w")
                KCH = 87
                KW = 5
                s_wload = psem("wload")
                HITS = (((0,), (1,)), ((2, 3), (4,)), ((5, 6), (7,)))

                with nc.Block() as block:
                    @block.gpsimd
                    def _(pool):
                        for t in (wqk, wv, rots, cp):
                            nc.gpsimd.memset(t[:], 0.0).then_inc(s_zero, 1)

                    @block.vector
                    def _(dve):
                        nc.vector.tensor_copy(fk[:], C("first_k")).then_inc(s_w, 1)
                        nc.vector.memset(ones[:], 1.0).then_inc(s_w, 1)
                        nc.vector.tensor_copy(identb[:], ident).then_inc(s_w, 1)
                        nc.vector.tensor_copy(windowb[:], C("window")[0:W3]).then_inc(s_w, 1)

                    @block.sync
                    def _(sp):
                        sp.wait_ge(s_zero, 4)
                        sp.dma_start(wo[:], a["Wo"][1]).then_inc(s_wload, 16)
                        n = 16
                        for s in range(NS):
                            sp.dma_start(wqk[:, s, :, 0:DH], a["Wqk"][1][:, s * 64:(s + 1) * 64]
                                         .rearrange("p (j d) -> p j d", j=HS)).then_inc(s_wload, 16)
                            n += 16
                            for j in range(HS):
                                dst = rots[32 * j:32 * j + DH, s, j * P:(j + 1) * P].rearrange("d (r k) -> d r k", r=NHASH)
                                sp.dma_start(dst, a["rots"][1, s * HS + j].rearrange("r d k -> d r k"))\
                                    .then_inc(s_wload, 16)
                                n += 16
                        wvv = wv[:].rearrange("p (j e) w -> p j e w", e=2)
                        src = a["Wv"][1].rearrange("p (j e d) -> p j e d", e=2, d=DH)
                        for e in range(2):
                            sp.dma_start(wvv[:, :, e, 16 * e:16 * e + DH], src[:, :, e, :]).then_inc(s_wload, 16)
                            n += 16
                        sp.wait_ge(s_wload, n)

                LASTG = NG - 1

                def bodies(eng, body):
                    with eng.Fori(0, (NG - 2) // 2) as k:
                        for u in range(2):
                            body(k * 2 + u, u, True, True)
                    body(NG - 2, 0, True, False)
                    body(LASTG, 1, False, False)

                with nc.Block() as block:
                    @block.vector
                    def _(dve):
                        def norm(g):
                            for n in range(2):
                                for t in range(4):
                                    tile = g * 8 + n * 4 + t
                                    ins = nc.vector.tensor_scalar(
                                        xh[:, n, t * P:(t + 1) * P], x2[:, bass.ds(tile * P, P)],
                                        mean[:, bass.ds(tile, 1)], rstd[:, bass.ds(tile, 1)], ALU.subtract, ALU.mult)
                                ins.then_inc(s_xh, 1)

                        def keys(g, v):
                            dve.wait_ge(s_qc, g * 4 + 4)
                            dve.wait_ge(s_nrm, g + 1)
                            for s in range(NS):
                                dst = qk_[:, v, s, :]
                                nc.vector.scalar_tensor_tensor(out=dst, in0=nrm[:, s, :], scalar=C("guard"), in1=dst,
                                                               op0=ALU.mult, op1=ALU.add).then_inc(s_qk, 1)

                        def scales(g, v, link):
                            dve.wait_ge(s_kt, g + 1)
                            src = ps[:, 4:8, :].rearrange("p b (x w) -> p (b x) w", w=32)[:, :, 16:17]
                            dst = scale_[:, v, :].unsqueeze(2)
                            link(nc.vector.reciprocal(dst, src))
                            nc.vector.tensor_scalar(dst, dst, 0.25, None, ALU.mult).then_inc(s_scale, 1)

                        def find(g, t, link):
                            pair = 4 + 2 * (t % 2)
                            hi, ext, pos_wins = hi_[:, t % 2, :], ext_[:, t % 2, :], wins_[:, t % 2, :]
                            rot = ps[:, pair:pair + 2, :].rearrange("p b (x k) -> p (b x) k", k=NK)
                            dve.wait_ge(s_rot, g * 8 + t + 1)
                            if t >= 2:
                                dve.wait_ge(s_am, g * 8 + t - 1)
                            nc.vector.tensor_reduce(hi, rot, AX.X, ALU.max)
                            link(nc.vector.tensor_reduce(ext, rot, AX.X, ALU.min))
                            link(nc.vector.scalar_tensor_tensor(out=pos_wins, in0=ext, scalar=-1.0, in1=hi,
                                                                op0=ALU.mult, op1=ALU.is_le))
                            dve.sem_inc(s_hold, 1)
                            link(nc.vector.copy_predicated(ext, pos_wins, hi))
                            nc.vector.tensor_tensor(hit_[t % 2], rot, ext.unsqueeze(2).broadcast_to((P, H * NHASH, NK)),
                                                    ALU.is_equal).then_inc(s_hit, 1)

                        def bucket(g, t, link):
                            hi, pos_wins = hi_[:, t % 2, :], wins_[:, t % 2, :]
                            dve.wait_ge(s_hm, g * 8 + t + 1)
                            link(nc.vector.tensor_reduce(hi, hit_[t % 2], AX.X, ALU.max))
                            link(nc.vector.scalar_tensor_tensor(out=hi, in0=pos_wins, scalar=float(NK), in1=hi,
                                                                op0=ALU.mult, op1=ALU.add))
                            nc.vector.tensor_scalar(bt[:, t % 2, t // 2, :], hi, -1.0, float(NBUCKET),
                                                    ALU.mult, ALU.add).then_inc(s_am, 1)

                        def chunks(g, v, link):
                            dve.wait_ge(s_bt, g + 1)
                            link(nc.vector.tensor_copy(rows, ps[:, 2, 0:S]))
                            low, cand, count, below, ok, rest = (thr[:, i, :] for i in range(6))
                            bit = NBUCKET // 2
                            nc.vector.memset(low, 0.0)
                            link(nc.vector.memset(below, 0.0))
                            while bit >= 1:
                                link(nc.vector.tensor_scalar(cand, low, float(bit), None, ALU.add))
                                for k in range(3):
                                    ins = nc.vector.tensor_scalar(flags[:, k, :], rows, cand[:, k:k + 1], None, ALU.is_lt,
                                                                  ALU.add, accum_out=count[:, k:k + 1])
                                link(ins)
                                link(nc.vector.tensor_tensor(ok, count, C("ranks"), ALU.is_le))
                                nc.vector.scalar_tensor_tensor(out=low, in0=ok, scalar=float(bit), in1=low,
                                                               op0=ALU.mult, op1=ALU.add)
                                link(nc.vector.tensor_tensor(count, count, ok, ALU.mult))
                                link(nc.vector.tensor_tensor(below, below, count, ALU.max))
                                bit //= 2
                            link(nc.vector.tensor_tensor(rest, C("ranks"), below, ALU.subtract))
                            for k in range(3):
                                same, run, at = flags[:, 0, :], flags[:, 1, :], flags[:, 2, :]
                                link(nc.vector.tensor_scalar(same, rows, low[:, k:k + 1], None, ALU.is_equal))
                                link(nc.vector.tensor_tensor_scan(run, ones[:], same, 0.0, ALU.mult, ALU.add))
                                link(nc.vector.scalar_tensor_tensor(out=at, in0=run, scalar=rest[:, k:k + 1], in1=same,
                                                                    op0=ALU.is_gt, op1=ALU.mult))
                                link(nc.vector.scalar_tensor_tensor(out=(chunk if k == 0 else flags[:, 3, :]), in0=rows,
                                                                    scalar=low[:, k:k + 1], in1=at, op0=ALU.is_gt, op1=ALU.add))
                                if k == 1:
                                    link(nc.vector.tensor_tensor(chunk, chunk, flags[:, 3, :], ALU.add))
                                elif k == 2:
                                    nc.vector.tensor_tensor(chunk, chunk, flags[:, 3, :], ALU.add).then_inc(s_chunk, 1)
                            dve.wait_ge(s_chT, g + 1)
                            for t in range(2):
                                src = ps[:, 2, S + t * P:S + (t + 1) * P].rearrange("p (x r) -> p x r", r=NHASH)
                                dst = cn_[:, v, t, :, :].rearrange("p b (h c r) -> p (b h) c r", c=NC_, r=NHASH)
                                for c in range(NC_):
                                    ins = nc.vector.tensor_scalar(dst[:, :, c, :], src, float(c), None, ALU.is_equal)
                            ins.then_inc(s_c, 1)

                        def window_sum(n):
                            dve.wait_ge(s_d, n + 1)
                            nc.vector.tensor_tensor(xw[:], ps[:, 2, 0:S], mt[:], ALU.mult).then_inc(s_xw, 1)

                        def weights(n):
                            link = Chain(dve, s_cw, n * KW)
                            dve.wait_ge(s_den, n + 1)
                            link(nc.vector.reciprocal(rc[:], ps[:, 2, S:2 * S]))
                            link(nc.vector.tensor_tensor(ws[:], rc[:], mt[:], ALU.mult))
                            link(nc.vector.tensor_copy(wb[:, 0, :], ws[:]))
                            link(nc.vector.tensor_tensor(rc[:], ws[:], wb[:, 0, :], ALU.subtract))
                            link(nc.vector.tensor_copy(wb[:, 1, :], rc[:]))
                            nc.vector.tensor_tensor(wb[:, 2, :], rc[:], wb[:, 1, :], ALU.subtract).then_inc(s_ws, 1)

                        def weigh(n, b, half_way=None):
                            for k in range(8):
                                t, pr = k // 4, k % 4
                                if k == 4 and half_way:
                                    half_way()
                                dve.wait_ge(s_g, n * 8 + k + 1)
                                e2 = ee[:, b % 2, t, 2 * pr:2 * pr + 2, :]
                                nc.vector.tensor_tensor(e2, ps[:, k % 2, :].rearrange("p (h w) -> p h w", h=2), e2,
                                                        ALU.mult).then_inc(s_a, 1)

                        def residual(n):
                            dve.wait_ge(s_y, n + 1)
                            xb = x1[:, bass.ds(n * S, S)]
                            nc.vector.tensor_tensor(xb, ps[:, 3, S:2 * S], xb, ALU.add).then_inc(s_x1, 1)
                            dve.wait_ge(s_x1, n + 1)
                            for t in range(2):
                                nc.vector.bn_stats(stats[:, bass.ds(n * 2 + t, 1), :].rearrange("p a b -> p (a b)"),
                                                   x1[:, bass.ds(n * S + t * P, P)])

                        def hash_tiles(g, tiles, link):
                            for t in tiles:
                                find(g, t, link)
                                if t:
                                    bucket(g, t - 1, link)

                        def body(g, u, more, front):
                            link = Chain(dve, s_ch, (g + 1) * KCH)
                            for b in range(GB):
                                n = g * GB + b
                                if more and b == 0:
                                    scales(g + 1, 1 - u, link)
                                weigh(n, b, (lambda: bucket(g + 1, 7, link)) if more and b == 3 else None)
                                if more and b < 3:
                                    hash_tiles(g + 1, HITS[b][0], link)
                                if front and b == 3:
                                    norm(g + 2)
                                if more and b == 3:
                                    chunks(g + 1, 1 - u, link)
                                    residual(n)
                                    window_sum(n + 1)
                                else:
                                    if b < 3:
                                        window_sum(n + 1)
                                    residual(n)
                                if more or b < 3:
                                    weights(n + 1)
                                if more and b < 3:
                                    hash_tiles(g + 1, HITS[b][1], link)
                            if front:
                                keys(g + 2, u)
                            if more:
                                assert link.n == KCH, link.n

                        link = Chain(dve, s_ch, 0)
                        norm(0)
                        keys(0, 0)
                        scales(0, 0, link)
                        hash_tiles(0, range(8), link)
                        bucket(0, 7, link)
                        norm(1)
                        chunks(0, 0, link)
                        window_sum(0)
                        weights(0)
                        keys(1, 1)
                        bodies(dve, body)

                    @block.tensor
                    def _(pe):
                        def turn_in(g):
                            for n in range(2):
                                pe.wait_ge(s_xh, g * 2 + n + 1)
                                for t in range(4):
                                    ins = nc.tensor.transpose(ps[:, 4 + n, t * P:(t + 1) * P], xh[:, n, t * P:(t + 1) * P], ident)
                                ins.then_inc(s_tp, 1)

                        def project_q(g, n):
                            if n == 0:
                                pe.wait_ge(s_lt, g * 2 + 2)
                            else:
                                pe.wait_ge(s_qc, g * 4 + 2)
                                pe.wait_ge(s_sq, g * 4 + 2)
                            for s in range(NS):
                                nc.tensor.matmul(ps[:, 6 + s, :], wqk[:, s, :, :].rearrange("p j d -> p (j d)"),
                                                 lt[:, n, :], start=True, stop=True).then_inc(s_q, 1)

                        def project_v(g, n):
                            if n:
                                pe.wait_ge(s_vp, g * 2 + 1)
                            for t in range(4):
                                ins = nc.tensor.matmul(ps[:, 4 + t // 2, (t % 2) * S:(t % 2 + 1) * S],
                                                       lt[:, n, t * P:(t + 1) * P], wv[:].rearrange("p h d -> p (h d)"),
                                                       start=True, stop=True)
                            ins.then_inc(s_v, 1)

                        def norms(g):
                            pe.wait_ge(s_sq, g * 4 + 4)
                            pe.wait_ge(s_qc, g * 4 + 4)
                            pe.wait_ge(s_vp, g * 2 + 2)
                            for s in range(NS):
                                for n in range(2):
                                    ins = nc.tensor.matmul(ps[:, 4 + 2 * s + n, :], C("block_sum"),
                                                           sq[:, s, n * BLK:(n + 1) * BLK], start=True, stop=True)
                            ins.then_inc(s_n2, 1)

                        def turn_keys(g, v):
                            pe.wait_ge(s_qk, g * 2 + 2)
                            pe.wait_ge(s_nrm, g + 1)
                            for s in range(NS):
                                for t in range(8):
                                    x = s * 8 + t
                                    ins = nc.tensor.transpose(ps[:, 4 + x // 4, x % 4 * P:(x % 4 + 1) * P],
                                                              qk_[:, v, s, t * P:(t + 1) * P], ident)
                            ins.then_inc(s_kt, 1)

                        def rotate(g, v, t):
                            if t < 2:
                                pe.wait_ge(s_scale, g + 1)
                            else:
                                pe.wait_ge(s_hit, g * 8 + t - 1)
                            for s in range(NS):
                                ins = nc.tensor.matmul(ps[:, 4 + 2 * (t % 2) + s, :], qk_[:, v, s, t * P:(t + 1) * P],
                                                       rots[:, s, :], start=True, stop=True)
                            ins.then_inc(s_rot, 1)

                        def turn_buckets(g):
                            pe.wait_ge(s_am, g * 8 + 8)
                            for t in range(2):
                                ins = nc.tensor.transpose(ps[:, 2, t * P:(t + 1) * P],
                                                          bt[:, t, :, :].rearrange("p b x -> p (b x)"), ident)
                            ins.then_inc(s_bt, 1)

                        def turn_chunks(g):
                            pe.wait_ge(s_chunk, g + 1)
                            for t in range(2):
                                ins = nc.tensor.transpose(ps[:, 2, S + t * P:S + (t + 1) * P], chunk[:, t * P:(t + 1) * P], ident)
                            ins.then_inc(s_chT, 1)

                        def scores(n, v, b, first=False, sums_of=None):
                            pe.wait_ge(s_qd, n * NS + 2)
                            for k in range(8):
                                t, s, pr = k // 4, k // 2 % 2, k % 2
                                if k == 4 and sums_of is not None:
                                    denominators(sums_of)
                                if k >= 2:
                                    pe.wait_ge(s_exp, n * 8 + k - 1)
                                elif not first:
                                    pe.wait_ge(s_a, (n - 2) * 8 + 8)
                                nc.tensor.matmul(ps[:, k % 2, :], qk_[:, v, s, b * S + t * P:b * S + (t + 1) * P],
                                                 qd[:, b % 2, s, 2 * pr:2 * pr + 2, :].rearrange("p j w -> p (j w)"),
                                                 start=True, stop=True).then_inc(s_s, 1)

                        def turn_c(u, b):
                            for t in range(2):
                                for pr in range(HP):
                                    for s in range(3):
                                        ins = nc.tensor.transpose(ctb[32 * s:32 * s + 32, pr, t * P:(t + 1) * P],
                                                                  cn_[:, u, t, b, 32 * pr:32 * pr + 32], identb[:])
                            ins.then_inc(s_ct, 1)

                        def windows(n):
                            pe.wait_ge(s_cts, n + 1)
                            for pr in range(HP):
                                ins = nc.tensor.matmul(ps[32 * pr:32 * pr + 32, 2, 0:S], windowb[:], ct[:, pr, :],
                                                       start=True, stop=True)
                            ins.then_inc(s_mt, 1)

                        def sums(n, b):
                            pe.wait_ge(s_exp, n * 8 + 8)
                            pe.wait_ge(s_cp, n * 2 + 2)
                            pe.wait_ge(s_mts, n + 1)
                            for i, (e, t) in enumerate(((0, 0), (0, 1), (1, 0), (1, 1))):
                                for j in range(4):
                                    h = 2 * j + e
                                    ins = nc.tensor.matmul(ps[32 * j:32 * j + 32, 2, 0:S], cp[:, b % 2, t, h, :],
                                                           ee[:, b % 2, t, h, :], start=(i == 0), stop=(i == 3))
                            ins.then_inc(s_d, 1)

                        def denominators(n):
                            pe.wait_ge(s_xw, n + 1)
                            nc.tensor.matmul(ps[:, 2, S:2 * S], C("den_sum"), xw[:], start=True, stop=True)\
                                .then_inc(s_den, 1)

                        def place_w(n, scored):
                            pe.wait_ge(s_ws, n + 1)
                            if scored:
                                pe.wait_ge(s_exp, n * 8 + 16)
                            for pr in range(HP):
                                for s in range(3):
                                    ins = nc.tensor.matmul(ps[32 * s:32 * s + 32, pr // 2, pr % 2 * S:(pr % 2 + 1) * S],
                                                           identb[:, 32 * pr:32 * pr + 32], wb[:, s, :], start=True, stop=True)
                            ins.then_inc(s_sel, 1)

                        def products(n, between):
                            for k in range(8):
                                t, pr = k // 4, k % 4
                                if k in between:
                                    between[k]()
                                if k >= 2:
                                    pe.wait_ge(s_a, n * 8 + k - 1)
                                else:
                                    pe.wait_ge(s_wd, n * 2 + 2)
                                nc.tensor.matmul(ps[:, k % 2, :], ct[:, pr, t * P:(t + 1) * P],
                                                 wd[:, pr, :, :].rearrange("p h w -> p (h w)"),
                                                 start=True, stop=True).then_inc(s_g, 1)

                        def attend(n, u, b):
                            pe.wait_ge(s_a, n * 8 + 8)
                            for i, (e, t) in enumerate(((0, 0), (0, 1), (1, 0), (1, 1))):
                                for j in range(4):
                                    h = 2 * j + e
                                    ins = nc.tensor.matmul(ps[32 * j:32 * j + 32, 3, 0:S], vp_[:, u, 2 * b + t, h, :],
                                                           ee[:, b % 2, t, h, :], start=(i == 0), stop=(i == 3))
                            ins.then_inc(s_o, 1)

                        def output(n):
                            pe.wait_ge(s_ot, n + 1)
                            for t in range(2):
                                ins = nc.tensor.matmul(ps[:, 3, S + t * P:S + (t + 1) * P], ot[:, t * P:(t + 1) * P],
                                                       wo[:], start=True, stop=True)
                            ins.then_inc(s_y, 1)

                        def body(g, u, more, front):
                            v = 1 - u
                            for b in range(GB):
                                n = g * GB + b
                                place_w(n, more or b < 3)
                                if more and b == 0:
                                    turn_keys(g + 1, v)
                                between = {}
                                if b < 3:
                                    between[4] = lambda: turn_c(u, b + 1)
                                if more and b < 3:
                                    first, second = (0, 1) if b == 0 else HITS[b][0]
                                    between[2] = lambda: rotate(g + 1, v, first)
                                    between[6] = lambda: rotate(g + 1, v, second)
                                if more and b == 3:
                                    between[6] = lambda: turn_buckets(g + 1)
                                products(n, between)
                                attend(n, u, b)
                                if b < 3:
                                    windows(n + 1)
                                elif front:
                                    turn_in(g + 2)
                                output(n)
                                if b < 3:
                                    sums(n + 1, b + 1)
                                    if more and b:
                                        rotate(g + 1, v, HITS[b][1][0])
                                if b < 2:
                                    scores(n + 2, u, b + 2, sums_of=n + 1)
                                elif more:
                                    scores(n + 2, v, b - 2, sums_of=n + 1 if b < 3 else None)
                                elif b < 3:
                                    denominators(n + 1)
                                if more and b == 3:
                                    if front:
                                        for i in range(2):
                                            project_q(g + 2, i)
                                            project_v(g + 2, i)
                                        norms(g + 2)
                                    turn_chunks(g + 1)
                                    pe.wait_ge(s_c, g + 2)
                                    turn_c(v, 0)
                                    windows(n + 1)
                                    sums(n + 1, 0)
                                    denominators(n + 1)

                        turn_in(0)
                        for n in range(2):
                            project_q(0, n)
                            project_v(0, n)
                        norms(0)
                        turn_keys(0, 0)
                        rotate(0, 0, 0)
                        rotate(0, 0, 1)
                        scores(0, 0, 0, first=True)
                        pe.wait_ge(s_exp, 8)
                        scores(1, 0, 1, first=True)
                        for t in range(2, 8):
                            rotate(0, 0, t)
                        turn_buckets(0)
                        turn_in(1)
                        for n in range(2):
                            project_q(1, n)
                            project_v(1, n)
                        turn_chunks(0)
                        pe.wait_ge(s_c, 1)
                        turn_c(0, 0)
                        windows(0)
                        sums(0, 0)
                        denominators(0)
                        norms(1)
                        bodies(pe, body)

                    @block.scalar
                    def _(act):
                        def front_in(g):
                            for n in range(2):
                                act.wait_ge(s_tp, g * 2 + n + 1)
                                nc.scalar.activation(lt[:, n, :], ps[:, 4 + n, :], ACT.Identity, scale=lncol[:, 0:1],
                                                     bias=lncol[:, 1:2]).then_inc(s_lt, 1)

                        def take_q(g, v, n):
                            for s in range(NS):
                                act.wait_ge(s_q, g * 4 + n * 2 + s + 1)
                                nc.scalar.activation(qk_[:, v, s, n * BLK:(n + 1) * BLK], ps[:, 6 + s, :], ACT.Identity,
                                                     bias=C("guard_eps")).then_inc(s_qc, 1)
                                nc.scalar.activation(sq[:, s, n * BLK:(n + 1) * BLK], ps[:, 6 + s, :], ACT.Square)\
                                    .then_inc(s_sq, 1)

                        def take_v(g, v, n):
                            act.wait_ge(s_v, g * 2 + n + 1)
                            dst = vp_[:, v, 4 * n:4 * n + 4, :, :].rearrange("p t h d -> p (t h d)")
                            nc.scalar.activation(dst, ps[:, 4:6, :].rearrange("p b w -> p (b w)"), ACT.Identity)\
                                .then_inc(s_vp, 1)

                        def roots(g, first=False):
                            act.wait_ge(s_n2, g + 1)
                            if not first:
                                act.wait_ge(s_chT, g)
                            nc.scalar.activation(nrm[:].rearrange("p s w -> p (s w)"),
                                                 ps[:, 4:8, :].rearrange("p b w -> p (b w)"), ACT.Sqrt).then_inc(s_nrm, 1)

                        def exps(g, n, v, b):
                            act.wait_ge(s_scale, g + 1)
                            for k in range(8):
                                t, s, pr = k // 4, k // 2 % 2, k % 2
                                act.wait_ge(s_s, n * 8 + k + 1)
                                for j in range(2):
                                    col = (s * 8 + 2 * b + t) * HS + 2 * pr + j
                                    ins = nc.scalar.activation(ee[:, b % 2, t, s * HS + 2 * pr + j, :],
                                                               ps[:, k % 2, j * S:(j + 1) * S], ACT.Exp,
                                                               scale=scale_[:, v, col:col + 1])
                                ins.then_inc(s_exp, 1)

                        def take_c(n, first=False):
                            act.wait_ge(s_ct, n + 1)
                            if not first:
                                act.wait_ge(s_g, n * 8)
                            nc.scalar.activation(ct[:].rearrange("p a w -> p (a w)"),
                                                 ctb.rearrange("p a w -> p (a w)"), ACT.Identity).then_inc(s_cts, 1)

                        def take_windows(n):
                            act.wait_ge(s_mt, n + 1)
                            nc.scalar.activation(mt[:], ps[:, 2, 0:S], ACT.Identity).then_inc(s_mts, 1)

                        def take_w(n):
                            act.wait_ge(s_sel, n + 1)
                            for e in range(2):
                                nc.scalar.activation(wd[:, :, e, :], ps[0:W3, 0:2, :].rearrange("p b (a w) -> p (b a) w", w=S),
                                                     ACT.Identity, scale=C("pair_rows")[0:W3, e:e + 1]).then_inc(s_wd, 1)

                        def take_o(n):
                            act.wait_ge(s_o, n + 1)
                            nc.scalar.activation(ot[:], ps[:, 3, 0:S], ACT.Identity).then_inc(s_ot, 1)

                        def body(g, u, more, front):
                            v = 1 - u
                            for b in range(GB):
                                n = g * GB + b
                                take_w(n)
                                if b < 3:
                                    take_c(n + 1)
                                take_o(n)
                                if b < 3:
                                    take_windows(n + 1)
                                elif front:
                                    front_in(g + 2)
                                if b < 2:
                                    exps(g, n + 2, u, b + 2)
                                elif more:
                                    exps(g + 1, n + 2, v, b - 2)
                                if front and b == 3:
                                    for i in range(2):
                                        take_q(g + 2, u, i)
                                        take_v(g + 2, u, i)
                                if more and b == 3:
                                    take_c(n + 1)
                                    take_windows(n + 1)
                            if front:
                                roots(g + 2)

                        front_in(0)
                        for n in range(2):
                            take_q(0, 0, n)
                            take_v(0, 0, n)
                        roots(0, first=True)
                        exps(0, 0, 0, 0)
                        exps(0, 1, 0, 1)
                        front_in(1)
                        for n in range(2):
                            take_q(1, 1, n)
                            take_v(1, 1, n)
                        take_c(0, first=True)
                        take_windows(0)
                        roots(1)
                        bodies(act, body)

                    @block.gpsimd
                    def _(pool):
                        def place_q(g, v, n, b, first=False):
                            if not first:
                                pool.wait_ge(s_s, (n - 2) * 8 + 8)
                                pool.sem_inc(s_hold, 1)
                            pool.wait_ge(s_qk, g * 2 + 2)
                            pool.sem_inc(s_hold, 1)
                            for s in range(NS):
                                src = qk_[:, v, s, b * S:(b + 1) * S].unsqueeze(1).broadcast_to((P, HS, S))
                                nc.gpsimd.tensor_tensor(qd[:, b % 2, s, :, :], src,
                                                        C("head_rows").unsqueeze(2).broadcast_to((P, HS, S)), ALU.mult)\
                                    .then_inc(s_qd, 1)

                        def index_hits(g, tiles):
                            for t in tiles:
                                pool.wait_ge(s_hit, g * 8 + t + 1)
                                pool.sem_inc(s_hold, 1)
                                nc.gpsimd.tensor_tensor(hit_[t % 2], hit_[t % 2], fk[:].unsqueeze(1)
                                                        .broadcast_to((P, H * NHASH, NK)), ALU.mult).then_inc(s_hm, 1)

                        def place_c(g, u, n, b, first=False):
                            if b == 0:
                                pool.wait_ge(s_c, g + 1)
                                pool.sem_inc(s_hold, 1)
                            if not first:
                                pool.wait_ge(s_d, n - 1)
                                pool.sem_inc(s_hold, 1)
                            src = cn_[:, u, :, b, :].rearrange("p t (j e d) -> p t j e d", e=2, d=16)
                            dst = cp[:, b % 2].rearrange("p t (j e) w -> p t j e w", e=2)
                            for e in range(2):
                                nc.gpsimd.tensor_copy(dst[:, :, :, e, 16 * e:16 * e + 16], src[:, :, :, e, :]).then_inc(s_cp, 1)

                        def body(g, u, more, front):
                            v = 1 - u
                            for b in range(GB):
                                n = g * GB + b
                                if b < 2:
                                    place_q(g, u, n + 2, b + 2)
                                    place_c(g, u, n + 2, b + 2)
                                elif more:
                                    place_q(g + 1, v, n + 2, b - 2)
                                if more and b < 3:
                                    index_hits(g + 1, HITS[b][0] + HITS[b][1])
                                if more and b == 3:
                                    place_c(g + 1, v, n + 1, 0)
                                    place_c(g + 1, v, n + 2, 1)

                        place_q(0, 0, 0, 0, first=True)
                        place_q(0, 0, 1, 1, first=True)
                        index_hits(0, range(8))
                        place_c(0, 0, 0, 0, first=True)
                        place_c(0, 0, 1, 1, first=True)
                        bodies(pool, body)

        attention()
        rstd_phase("ln2_1", LN_EPS)
        feed_forward(1)
        rstd_phase("gru", LN_EPS, gru=True)

        def recurrence():
            with ExitStack() as ph:
                def psb(name, shape, dt=F32):
                    return sb("re_" + name, shape, dt, ph)

                def psem(name):
                    return sem("re_" + name, ph)

                xh, lt = psb("xh", [P, 2, BLK]), psb("lt", [P, 2, BLK])
                wgh = psb("wgh", [P, 2 * P])
                rr = psb("rr", [P, 3, NT])
                gate = psb("gate", [P, 3, BLK])
                g_, st = psb("g", [P, BLK]), psb("state", [P, 2, BLK])
                s_w, s_rr = psem("weights"), psem("factors")
                s_xh, s_tp, s_lt, s_gh, s_sig, s_st, s_bk, s_c = (
                    psem(n) for n in ("normed", "turned", "lt", "gates", "sigmoids", "states", "back", "chain"))
                K = 7
                with nc.Block() as block:
                    @block.sync
                    def _(sp):
                        sp.dma_start(wgh[:], a["W_gh"]).then_inc(s_w, 16)
                        sp.wait_ge(s_w, 16)

                    @block.vector
                    def _(dve):
                        link = Chain(dve, s_rr)
                        link(nc.vector.tensor_tensor(rr[:, 0, :], rstd[:], gru_r[:], ALU.mult))
                        link(nc.vector.tensor_scalar(rr[:, 1, :], rstd[:], 1.0, None, ALU.add))
                        link(nc.vector.scalar_tensor_tensor(out=rr[:, 2, :], in0=mean[:], scalar=-1.0, in1=rstd[:],
                                                            op0=ALU.mult, op1=ALU.mult))

                with nc.Block() as block:
                    @block.vector
                    def _(dve):
                        def norm(i, u):
                            for t in range(4):
                                ins = nc.vector.tensor_scalar(
                                    xh[:, u, t * P:(t + 1) * P], x2[:, bass.ds(i * BLK + t * P, P)],
                                    mean[:, bass.ds(i * 4 + t, 1)], rr[:, 0, bass.ds(i * 4 + t, 1)],
                                    ALU.subtract, ALU.mult)
                            ins.then_inc(s_xh, 1)

                        def mix(i, u):
                            link = Chain(dve, s_c, i * K)
                            for t in range(4):
                                h = x2[:, bass.ds(i * BLK + t * P, P)]
                                link(nc.vector.tensor_scalar(h, h, rr[:, 1, bass.ds(i * 4 + t, 1)],
                                                             rr[:, 2, bass.ds(i * 4 + t, 1)], ALU.mult, ALU.add))
                            dve.wait_ge(s_sig, i * 3 + 3)
                            link(nc.vector.tensor_scalar(g_[:], ps[:, 3 + 2 * u, :], 0.0, None, ALU.max))
                            link(nc.vector.scalar_tensor_tensor(out=g_[:], in0=gate[:, 2, :], scalar=0.5, in1=g_[:],
                                                                op0=ALU.min, op1=ALU.add))
                            link(nc.vector.tensor_tensor(g_[:], g_[:], gate[:, 0, :], ALU.mult))
                            for t in range(2):
                                w = slice(t * S, (t + 1) * S)
                                nc.vector.tensor_tensor_scan(st[:, u, w], gate[:, 1, w], g_[:, w], 0.0, ALU.mult, ALU.add)\
                                    .then_inc(s_st, 1)
                            assert link.n == K

                        def residual(i, u):
                            dve.wait_ge(s_bk, i + 1)
                            x2b = x2[:, bass.ds(i * BLK, BLK)]
                            nc.vector.tensor_tensor(x2b, ps[:, 6 + u, :], x2b, ALU.add).then_inc(s_rr, 1)
                            dve.wait_ge(s_rr, 3 + i + 1)
                            for t in range(4):
                                nc.vector.bn_stats(stats[:, bass.ds(i * 4 + t, 1), :].rearrange("p a b -> p (a b)"),
                                                   x2[:, bass.ds(i * BLK + t * P, P)])

                        norm(0, 0)
                        with dve.Fori(0, NBLK // 2 - 1) as k:
                            for u in range(2):
                                norm(k * 2 + u + 1, 1 - u)
                                mix(k * 2 + u, u)
                                residual(k * 2 + u, u)
                        norm(NBLK - 1, 1)
                        mix(NBLK - 2, 0)
                        residual(NBLK - 2, 0)
                        mix(NBLK - 1, 1)
                        residual(NBLK - 1, 1)

                    @block.tensor
                    def _(pe):
                        def turn(i, u):
                            pe.wait_ge(s_xh, i + 1)
                            for t in range(4):
                                ins = nc.tensor.transpose(ps[:, u, t * P:(t + 1) * P], xh[:, u, t * P:(t + 1) * P], ident)
                            ins.then_inc(s_tp, 1)

                        def gates(i, u):
                            pe.wait_ge(s_lt, i + 1)
                            for c in range(2):
                                ins = nc.tensor.matmul(ps[:, 2 + 2 * u + c, :], wgh[:, c * P:(c + 1) * P], lt[:, u, :],
                                                       start=True, stop=True)
                            ins.then_inc(s_gh, 1)

                        def back(i, u):
                            pe.wait_ge(s_st, i * 2 + 2)
                            for t in range(4):
                                ins = nc.tensor.transpose(ps[:, 6 + u, t * P:(t + 1) * P], st[:, u, t * P:(t + 1) * P], ident)
                            ins.then_inc(s_bk, 1)

                        turn(0, 0)
                        with pe.Fori(0, NBLK // 2 - 1) as k:
                            for u in range(2):
                                gates(k * 2 + u, u)
                                turn(k * 2 + u + 1, 1 - u)
                                back(k * 2 + u, u)
                        gates(NBLK - 2, 0)
                        turn(NBLK - 1, 1)
                        back(NBLK - 2, 0)
                        gates(NBLK - 1, 1)
                        back(NBLK - 1, 1)

                    @block.scalar
                    def _(act):
                        nc.scalar.preload_act_table(ACT.Sigmoid)

                        def evac(i, u):
                            act.wait_ge(s_tp, i + 1)
                            nc.scalar.activation(lt[:, u, :], ps[:, u, :], ACT.Identity, scale=lncol[:, 6:7],
                                                 bias=lncol[:, 7:8]).then_inc(s_lt, 1)

                        def sigmoids(i, u):
                            act.wait_ge(s_gh, i + 1)
                            for c, (bank, scale) in enumerate(((0, 1.0), (0, -1.0), (1, 1.0))):
                                nc.scalar.activation(gate[:, c, :], ps[:, 2 + 2 * u + bank, :], ACT.Sigmoid, scale=scale)\
                                    .then_inc(s_sig, 1)

                        evac(0, 0)
                        with act.Fori(0, NBLK // 2 - 1) as k:
                            for u in range(2):
                                sigmoids(k * 2 + u, u)
                                evac(k * 2 + u + 1, 1 - u)
                        sigmoids(NBLK - 2, 0)
                        evac(NBLK - 1, 1)
                        sigmoids(NBLK - 1, 1)

        recurrence()
        rstd_phase("ln3", LN_EPS)

        XW = P + 2 * E
        rows_dram = nc.dram_tensor("expert_rows", [T, XW], F32, kind="Internal").ap()
        y_dram = nc.dram_tensor("expert_out", [2 * T + E * SLOTS * P, P], F32, kind="Internal").ap()
        TE = NT * E
        gather_i = sb("gather_i", [P, E, SLOTS], I32)
        valid = sb("valid", [P, E, SLOTS])
        spare = sb("spare", [P, E, SLOTS])

        def routing():
            with ExitStack() as ph:
                def psb(name, shape, dt=F32):
                    return sb("ro_" + name, shape, dt, ph)

                def psem(name):
                    return sem("ro_" + name, ph)

                xh, lt = psb("xh", [P, 2, BLK]), psb("lt", [P, 2, BLK])
                gw, gb = psb("gw", [P, E]), psb("gb", [P, E])
                zero = psb("zero", [P, 4096])
                bits = psb("bits", [P, 30], I32)
                probs, oh1, oh2, aa, bb, wt = (psb(f"n8_{i}", [P, NT, E]) for i in range(6))
                n1 = psb("n1", [P, NT])
                wdest = psb("wdest", [P, NT, 2, E])
                thr, cand = psb("thr", [P, 1], I32), psb("cand", [P, 1], I32)
                take = psb("take", [P, 1], I32)
                count = psb("count", [P, 1])
                thr8, room = psb("thr8", [P, E]), psb("room", [P, E])
                pos_i = psb("pos_i", [P, NT, E], I32)
                iota_b = psb("iota_b", [P, P], BF16)
                pay = psb("pay", [P, TE, 2, SLOTS], BF16)
                oh_lo = psb("oh_lo", [P, 2, E, P], BF16)
                slot = psb("slot", [P, E, 2 * SLOTS])
                s_w, s_z, s_xh, s_tp, s_lt, s_lg, s_lo, s_c, s_row, s_yz = (
                    psem(n) for n in ("weights", "zero", "normed", "turned", "lt", "logits", "logits_out", "chain",
                                      "rows_stored", "y_zeroed"))
                s_st = [psem(f"stored{u}") for u in range(2)]
                ZC = 2 * T * P // (P * 4096)
                with nc.Block() as block:
                    @block.sync
                    def _(sp):
                        sp.dma_start(gw[:], a["gate_wT"]).then_inc(s_w, 16)
                        sp.dma_start(gb[:], a["gate_b"]).then_inc(s_w, 16)
                        sp.dma_start(bits[:], a["bits"]).then_inc(s_w, 16)
                        sp.wait_ge(s_w, 48)

                    @block.vector
                    def _(dve):
                        nc.vector.memset(zero[:], 0.0)

                with nc.Block() as block:
                    @block.vector
                    def _(dve):
                        def norm(i, u, k):
                            dve.wait_ge(s_st[u], k * 16 + 16)
                            for t in range(4):
                                ins = nc.vector.tensor_scalar(
                                    xh[:, u, t * P:(t + 1) * P], x2[:, bass.ds(i * BLK + t * P, P)],
                                    mean[:, bass.ds(i * 4 + t, 1)], rstd[:, bass.ds(i * 4 + t, 1)],
                                    ALU.subtract, ALU.mult)
                            ins.then_inc(s_xh, 1)

                        def logits(i, u):
                            dve.wait_ge(s_lg, i + 1)
                            dst = probs[:, bass.ds(i * 4, 4), :]
                            src = ps[:, 2 + u, 0:4 * E].rearrange("p (t e) -> p t e", e=E)
                            nc.vector.tensor_tensor(dst, src, gb[:].unsqueeze(1).broadcast_to((P, 4, E)), ALU.add)\
                                .then_inc(s_lo, 1)

                        norm(0, 0, 0)
                        with dve.Fori(0, NBLK // 2 - 1) as k:
                            norm(k * 2 + 1, 1, k)
                            logits(k * 2, 0)
                            norm(k * 2 + 2, 0, k + 1)
                            logits(k * 2 + 1, 1)
                        norm(NBLK - 1, 1, NBLK // 2 - 1)
                        logits(NBLK - 2, 0)
                        logits(NBLK - 1, 1)

                    @block.tensor
                    def _(pe):
                        def turn(i, u):
                            pe.wait_ge(s_xh, i + 1)
                            for t in range(4):
                                ins = nc.tensor.transpose(ps[:, u, t * P:(t + 1) * P], xh[:, u, t * P:(t + 1) * P], ident)
                            ins.then_inc(s_tp, 1)

                        def gate(i, u):
                            pe.wait_ge(s_lt, i + 1)
                            for t in range(4):
                                ins = nc.tensor.matmul(ps[:, 2 + u, t * E:(t + 1) * E], lt[:, u, t * P:(t + 1) * P], gw[:],
                                                       start=True, stop=True)
                            ins.then_inc(s_lg, 1)

                        turn(0, 0)
                        with pe.Fori(0, NBLK // 2 - 1) as k:
                            for u in range(2):
                                turn(k * 2 + u + 1, 1 - u)
                                gate(k * 2 + u, u)
                        turn(NBLK - 1, 1)
                        gate(NBLK - 2, 0)
                        gate(NBLK - 1, 1)

                    @block.scalar
                    def _(act):
                        with act.Fori(0, NBLK // 2) as k:
                            for u in range(2):
                                act.wait_ge(s_tp, k * 2 + u + 1)
                                nc.scalar.activation(lt[:, u, :], ps[:, u, :], ACT.Identity).then_inc(s_lt, 1)

                    @block.sync
                    def _(sp):
                        rows_v = rows_dram.rearrange("(i t p) w -> i p t w", t=4, p=P)
                        for u in range(2):
                            sp.sem_inc(s_st[u], 16)
                        with sp.Fori(0, NBLK // 2) as k:
                            for u in range(2):
                                i = k * 2 + u
                                sp.wait_ge(s_xh, i + 1)
                                sp.sem_inc(s_z, 1)
                                sp.dma_start(rows_v[bass.ds(i, 1), :, :, 0:P].rearrange("i p t w -> (i p) t w"),
                                             xh[:, u, :].rearrange("p (t w) -> p t w", t=4)).then_inc(s_st[u], 16)
                        for u in range(2):
                            sp.wait_ge(s_st[u], NBLK // 2 * 16 + 16)

                    @block.gpsimd
                    def _(pool):
                        for n in range(ZC):
                            nc.gpsimd.dma_start(y_dram[n * 4096:(n + 1) * 4096, :].rearrange("(p r) w -> p (r w)", p=P),
                                                zero[:]).then_inc(s_yz, 16)
                        pool.wait_ge(s_yz, ZC * 16)

                def per_tile(v):
                    return v.unsqueeze(2).broadcast_to((P, NT, E))

                def per_expert(v):
                    return v.unsqueeze(1).broadcast_to((P, NT, E))

                s_e, s_t, s_thr = psem("exp"), psem("turned2"), psem("thr")
                with nc.Block() as block:
                    @block.vector
                    def _(dve):
                        link = Chain(dve, s_c)
                        link(nc.vector.tensor_reduce(n1[:], probs[:], AX.X, ALU.max))
                        nc.vector.tensor_tensor(probs[:], probs[:], per_tile(n1[:]), ALU.subtract).then_inc(s_e, 1)
                        dve.wait_ge(s_e, 2)
                        link(nc.vector.tensor_reduce(n1[:], probs[:], AX.X, ALU.add))
                        link(nc.vector.reciprocal(n1[:], n1[:]))
                        link(nc.vector.tensor_tensor(probs[:], probs[:], per_tile(n1[:]), ALU.mult))
                        last = C("last")
                        for src, oh in ((probs, oh1), (bb, oh2)):
                            link(nc.vector.tensor_reduce(n1[:], src[:], AX.X, ALU.max))
                            link(nc.vector.tensor_tensor(aa[:], src[:], per_tile(n1[:]), ALU.is_equal))
                            link(nc.vector.tensor_tensor(aa[:], aa[:], per_expert(last), ALU.mult))
                            link(nc.vector.tensor_reduce(n1[:], aa[:], AX.X, ALU.max))
                            link(nc.vector.tensor_tensor(oh[:], per_expert(last), per_tile(n1[:]), ALU.is_equal))
                            if oh is oh1:
                                link(nc.vector.scalar_tensor_tensor(out=bb[:], in0=oh[:], scalar=-2.0, in1=probs[:],
                                                                    op0=ALU.mult, op1=ALU.add))
                        link(nc.vector.tensor_tensor(aa[:], oh1[:], oh2[:], ALU.add))
                        link(nc.vector.tensor_tensor(wt[:], aa[:], probs[:], ALU.mult))
                        link(nc.vector.tensor_copy(wdest[:, :, 0, :], wt[:]))
                        link(nc.vector.scalar_tensor_tensor(out=wdest[:, :, 1, :], in0=oh2[:], scalar=float(T),
                                                            in1=per_tile(C("token")), op0=ALU.mult, op1=ALU.add))
                        nc.vector.tensor_copy(iota_b[:], C("iota")).then_inc(s_e, 1)

                    @block.scalar
                    def _(act):
                        act.wait_ge(s_e, 1)
                        nc.scalar.activation(probs[:], probs[:], ACT.Exp).then_inc(s_e, 1)

                    @block.tensor
                    def _(pe):
                        pe.wait_ge(s_e, 3)
                        for n in range(4):
                            ins = nc.tensor.transpose(ps[:, 0, n * P:(n + 1) * P],
                                                      wt[:, n * 16:(n + 1) * 16, :].rearrange("p t e -> p (t e)"), ident)

                weights = aa[:].rearrange("p t e -> p (t e)")
                flags = bb[:].rearrange("p t e -> p (t e)")
                with nc.Block() as block:
                    @block.sync
                    def _(sp):
                        sp.dma_start(rows_dram.rearrange("(t p) w -> p t w", p=P)[:, :, P:XW],
                                     wdest[:].rearrange("p t k e -> p t (k e)")).then_inc(s_row, 16)
                        sp.wait_ge(s_row, 16)

                    @block.vector
                    def _(dve):
                        link = Chain(dve, s_t)
                        link(nc.vector.tensor_copy(weights, ps[:, 0, :]))
                        link(nc.vector.memset(thr[:], 0))
                        with dve.Fori(0, 30) as i:
                            link = Chain(dve, s_t, i * 4 + 2)
                            link(nc.vector.tensor_tensor(cand[:], thr[:], bits[:, bass.ds(i, 1)], ALU.bitwise_or))
                            link(nc.vector.tensor_scalar(flags, weights, cand[:].bitcast(F32), None, ALU.is_ge, ALU.add,
                                                         accum_out=count[:]))
                            dve.wait_ge(s_thr, i + 1)
                            link(nc.vector.tensor_scalar(take[:], ps[:, 1, 0:1], float(CAP), -1.0, ALU.is_ge, ALU.mult))
                            dve.sem_inc(s_z, 1)
                            link(nc.vector.copy_predicated(thr[:], take[:], cand[:]))

                    @block.tensor
                    def _(pe):
                        with pe.Fori(0, 30) as i:
                            pe.wait_ge(s_t, i * 4 + 4)
                            nc.tensor.matmul(ps[:, 1, 0:1], C("same_expert"), count[:], start=True, stop=True)\
                                .then_inc(s_thr, 1)

                s_p, s_q, s_pos = psem("prefix_in"), psem("prefix_out"), psem("pos")
                sel, incl, rank = oh1, oh2, probs
                ones_row = zero[:, 0:NT]
                hi, lo = aa, bb
                with nc.Block() as block:
                    @block.vector
                    def _(dve):
                        link = Chain(dve, s_pos)
                        link(nc.vector.memset(ones_row, 1.0))
                        nc.vector.tensor_scalar(flags[:, 0:P], C("ones"), thr[:].bitcast(F32), None, ALU.mult)\
                            .then_inc(s_p, 1)
                        dve.wait_ge(s_q, 1)
                        link(nc.vector.tensor_copy(thr8[:], ps[:, 0, 0:E]))
                        link(nc.vector.tensor_tensor(sel[:], wt[:], per_expert(thr8[:]), ALU.is_gt))
                        link(nc.vector.tensor_tensor(bb[:], wt[:], per_expert(thr8[:]), ALU.is_equal))
                        nc.vector.scalar_tensor_tensor(out=aa[:], in0=wt[:], scalar=0.0, in1=bb[:],
                                                       op0=ALU.is_gt, op1=ALU.mult).then_inc(s_p, 1)

                        def ranks():
                            tot = ps[:, 2, :].rearrange("p (t e) -> p t e", e=E)
                            for e in range(E):
                                link(nc.vector.tensor_tensor_scan(incl[:, :, e], ones_row, tot[:, :, e], 0.0, ALU.mult,
                                                                  ALU.add))
                            link(nc.vector.tensor_tensor(incl[:], incl[:], tot, ALU.subtract))
                            link(nc.vector.tensor_tensor(rank[:], incl[:], ps[:, 1, :].rearrange("p (t e) -> p t e", e=E),
                                                         ALU.add))

                        dve.wait_ge(s_q, 2)
                        ranks()
                        link(nc.vector.tensor_reduce(room[:], ps[:, 3, :].rearrange("p (t e) -> p e t", e=E), AX.X, ALU.add))
                        link(nc.vector.tensor_scalar(room[:], room[:], -1.0, float(CAP), ALU.mult, ALU.add))
                        link(nc.vector.tensor_tensor(rank[:], rank[:], per_expert(room[:]), ALU.is_lt))
                        link(nc.vector.tensor_tensor(rank[:], rank[:], aa[:], ALU.mult))
                        nc.vector.tensor_tensor(sel[:], sel[:], rank[:], ALU.add).then_inc(s_p, 1)
                        dve.wait_ge(s_q, 3)
                        ranks()
                        link(nc.vector.tensor_copy(pos_i[:], rank[:]))
                        link(nc.vector.tensor_single_scalar(pos_i[:], pos_i[:], 7, ALU.logical_shift_right))
                        link(nc.vector.tensor_copy(hi[:], pos_i[:]))
                        link(nc.vector.scalar_tensor_tensor(out=lo[:], in0=hi[:], scalar=-float(P), in1=rank[:],
                                                            op0=ALU.mult, op1=ALU.add))
                        link(nc.vector.scalar_tensor_tensor(out=lo[:], in0=lo[:], scalar=1.0, in1=sel[:],
                                                            op0=ALU.add, op1=ALU.mult))
                        link(nc.vector.tensor_scalar(lo[:], lo[:], -1.0, None, ALU.add))
                        link(nc.vector.tensor_tensor(pay[:, :, 0, :], C("iota")[:, 0:SLOTS].unsqueeze(1)
                                                     .broadcast_to((P, TE, SLOTS)),
                                                     hi[:].rearrange("p t e -> p (t e)").unsqueeze(2)
                                                     .broadcast_to((P, TE, SLOTS)), ALU.is_equal))
                        for t in range(NT):
                            nc.vector.tensor_scalar(pay[:, t * E:(t + 1) * E, 1, :], pay[:, t * E:(t + 1) * E, 0, :],
                                                    float(t), None, ALU.mult)
                        link(nc.vector.tensor_scalar(n1[:, 0:1], C("partition"), 1.0, None, ALU.add))
                        link(nc.vector.tensor_scalar(pay[:, :, 0, :], pay[:, :, 0, :], n1[:, 0:1], None, ALU.mult))

                    @block.tensor
                    def _(pe):
                        pe.wait_ge(s_p, 1)
                        nc.tensor.transpose(ps[:, 0, 0:P], flags[:, 0:P], ident).then_inc(s_q, 1)
                        pe.wait_ge(s_p, 2)
                        tied, over = aa[:].rearrange("p t e -> p (t e)"), sel[:].rearrange("p t e -> p (t e)")
                        nc.tensor.matmul(ps[:, 1, :], C("before"), tied, start=True, stop=True)
                        nc.tensor.matmul(ps[:, 2, :], C("ones"), tied, start=True, stop=True)
                        nc.tensor.matmul(ps[:, 3, :], C("ones"), over, start=True, stop=True).then_inc(s_q, 1)
                        pe.wait_ge(s_p, 3)
                        nc.tensor.matmul(ps[:, 1, :], C("before"), over, start=True, stop=True)
                        nc.tensor.matmul(ps[:, 2, :], C("ones"), over, start=True, stop=True).then_inc(s_q, 1)

                s_oh, s_li = psem("onehot"), psem("list")
                lo_f = lo[:].rearrange("p t e -> p (t e)")
                with nc.Block() as block:
                    @block.vector
                    def _(dve):
                        with dve.Fori(0, NT // 2) as k:
                            for u in range(2):
                                tile = k * 2 + u
                                dve.wait_ge(s_li, k + 1)
                                for e in range(E):
                                    ins = nc.vector.tensor_scalar(oh_lo[:, u, e, :], iota_b[:],
                                                                  lo_f[:, bass.ds(tile * E + e, 1)], None, ALU.is_equal)
                                ins.then_inc(s_oh, 1)

                    @block.tensor
                    def _(pe):
                        def collect(tile, u, start, stop):
                            pe.wait_ge(s_oh, tile + 1)
                            for e in range(E):
                                rhs = pay[:, bass.ds(tile * E + e, 1), :, :].rearrange("p x k s -> p (x k s)")
                                ins = nc.tensor.matmul(ps[:, e, 0:2 * SLOTS], oh_lo[:, u, e, :], rhs, start=start, stop=stop)
                            return ins

                        pe.sem_inc(s_li, 1)
                        collect(0, 0, True, False)
                        collect(1, 1, False, False).then_inc(s_li, 1)
                        with pe.Fori(1, NT // 2 - 1) as k:
                            collect(k * 2, 0, False, False)
                            collect(k * 2 + 1, 1, False, False).then_inc(s_li, 1)
                        collect(NT - 2, 0, False, False)
                        collect(NT - 1, 1, False, True).then_inc(s_li, 1)

                s_f = psem("final")
                with nc.Block() as block:
                    @block.vector
                    def _(dve):
                        link = Chain(dve, s_f)
                        link(nc.vector.tensor_copy(slot[:], ps[:, :, 0:2 * SLOTS]))
                        first, tile = slot[:, :, 0:SLOTS], slot[:, :, SLOTS:2 * SLOTS]
                        link(nc.vector.tensor_scalar(valid[:], first, 0.5, None, ALU.is_gt))
                        link(nc.vector.scalar_tensor_tensor(out=tile, in0=tile, scalar=float(P), in1=first,
                                                            op0=ALU.mult, op1=ALU.add))
                        link(nc.vector.tensor_scalar(gather_i[:], tile, -1.0, 0.0, ALU.add, ALU.max))
                        link(nc.vector.tensor_scalar(spare[:], valid[:], -1.0, 1.0, ALU.mult, ALU.add))
                        link(nc.vector.tensor_tensor(spare[:].rearrange("p e s -> p (e s)"),
                                                     spare[:].rearrange("p e s -> p (e s)"), C("spare_row"), ALU.mult))

        routing()

        def experts():
            with ExitStack() as ph:
                def psb(name, shape, dt=F32):
                    return sb("ex_" + name, shape, dt, ph)

                def psem(name):
                    return sem("ex_" + name, ph)

                NB2 = SLOTS // 2
                NBUF = 5
                BL = E * NB2
                we1, we2 = psb("we1", [P, 2, HID]), psb("we2", [P, 2, EC, P])
                be = psb("be", [P, E * EC])
                be2 = psb("be2", [P, E, P])
                bs = psb("bs", [P, 2, EC])
                xg = psb("xg", [P, NBUF, 2, XW])
                xt = psb("xt", [P, 2, S])
                ht = psb("ht", [P, EC, S])
                yw = psb("yw", [P, NBUF, 2, P])
                ycol = psb("ycol", [P, NBUF, 2])
                scat = psb("scat", [P, NBUF, 2], I32)
                s_b, s_tp, s_xt, s_h, s_ht, s_y, s_ys, s_c, s_bs = (
                    psem(n) for n in ("biases", "turned", "xt", "hidden", "gelu", "y", "y_ready", "chain", "bias_ready"))
                s_w = [psem(f"weights{u}") for u in range(2)]
                s_xg = [psem(f"gathered{u}") for u in range(NBUF)]
                s_sc = [psem(f"scattered{u}") for u in range(NBUF)]
                s_hold = psem("hold")

                with nc.Block() as block:
                    @block.sync
                    def _(sp):
                        sp.dma_start(be[:], a["eb1"]).then_inc(s_b, 16)
                        sp.dma_start(be2[:], a["eb2"]).then_inc(s_b, 16)
                        sp.wait_ge(s_b, 32)

                with nc.Block() as block:
                    @block.sync
                    def _(sp):
                        def load(e, u):
                            sp.dma_start(we1[:, u, :], a["ew1"][bass.ds(e, 1), :, :].rearrange("e p f -> (e p) f"))\
                                .then_inc(s_w[u], 16)
                            sp.dma_start(we2[:, u, :, :], a["ew2"][bass.ds(e, 1), :, :]
                                         .rearrange("e (c p) d -> (e p) c d", p=P)).then_inc(s_w[u], 16)

                        for u in range(2):
                            load(u, u)
                        with sp.Fori(1, E // 2) as k:
                            for u in range(2):
                                sp.wait_ge(s_y, (k * 2 + u - 1) * NB2)
                                sp.sem_inc(s_hold, 1)
                                load(k * 2 + u, u)

                    @block.gpsimd
                    def _(pool):
                        for n in range(BL + 3):
                            if n < BL:
                                if n >= NBUF:
                                    pool.wait_ge(s_ys, n - NBUF + 1)
                                for t in range(2):
                                    nc.gpsimd.indirect_dma_start(
                                        out=xg[:, n % NBUF, t, :], out_offset=None, in_=rows_dram,
                                        in_offset=bass.IndirectOffsetOnAxis(
                                            ap=gather_i[:, n // NB2, n % NB2 * 2 + t:n % NB2 * 2 + t + 1], axis=0),
                                    ).then_inc(s_xg[n % NBUF], 16)
                            m = n - 3
                            if m >= 0:
                                pool.wait_ge(s_ys, m + 1)
                                for t in range(2):
                                    nc.gpsimd.indirect_dma_start(
                                        out=y_dram, in_=yw[:, m % NBUF, t, :], in_offset=None,
                                        out_offset=bass.IndirectOffsetOnAxis(ap=scat[:, m % NBUF, t:t + 1], axis=0),
                                    ).then_inc(s_sc[m % NBUF], 16)
                        for u in range(NBUF):
                            pool.wait_ge(s_sc[u], 32 * (BL // NBUF))

                    @block.vector
                    def _(dve):
                        def evac(n, j):
                            dve.wait_ge(s_tp, n + 1)
                            nc.vector.tensor_copy(xt[:, j % 2, :], ps[:, j % 2, 0:S]).then_inc(s_xt, 1)

                        def weigh(k, j, first):
                            n, e, buf, s = k * 2 * NB2 + j, k * 2 + j // NB2, j % NBUF, j % NB2 * 2
                            link = Chain(dve, s_c, n * 2)
                            for t in range(2):
                                x = e * SLOTS + s + t
                                ins = nc.vector.scalar_tensor_tensor(
                                    out=ycol[:, buf, t:t + 1], in0=xg[:, buf, t, bass.ds(P + E + e, 1)],
                                    scalar=valid_f[:, bass.ds(x, 1)], in1=spare_f[:, bass.ds(x, 1)],
                                    op0=ALU.mult, op1=ALU.add)
                            link(ins)
                            dve.wait_ge(s_y, n + 1)
                            dve.sem_inc(s_hold, 1)
                            if not (first and j < NBUF):
                                dve.wait_ge(s_sc[buf], (k * 2 + j // NBUF) * 32)
                                dve.sem_inc(s_hold, 1)
                            link(nc.vector.tensor_tensor(yw[:, buf, :, :], ps[:, 6 + j % 2, 0:S].rearrange("p (t d) -> p t d", t=2),
                                                         be2[:, bass.ds(e, 1), :].broadcast_to((P, 2, P)), ALU.add))
                            nc.vector.tensor_copy(scat[:, buf, :], ycol[:, buf, :])
                            for t in range(2):
                                ins = nc.vector.tensor_scalar(yw[:, buf, t, :], yw[:, buf, t, :],
                                                              xg[:, buf, t, bass.ds(P + e, 1)], None, ALU.mult)
                            ins.then_inc(s_ys, 1)

                        valid_f = valid[:].rearrange("p e s -> p (e s)")
                        spare_f = spare[:].rearrange("p e s -> p (e s)")

                        def pair(k, first=False, final=False):
                            for j in range(2 * NB2):
                                if j % NB2 == 0:
                                    u = j // NB2
                                    nc.vector.tensor_copy(bs[:, u, :], be[:, bass.ds((k * 2 + u) * EC, EC)])\
                                        .then_inc(s_bs, 1)
                                if not (final and j == 2 * NB2 - 1):
                                    evac(k * 2 * NB2 + j + 1, j + 1)
                                weigh(k, j, first)

                        evac(0, 0)
                        pair(0, first=True)
                        with dve.Fori(1, E // 2 - 1) as k:
                            pair(k)
                        pair(E // 2 - 1, final=True)

                    @block.tensor
                    def _(pe):
                        def turn(k, j):
                            pe.wait_ge(s_xg[j % NBUF], 32 * (k * 2 + j // NBUF + 1))
                            for t in range(2):
                                ins = nc.tensor.transpose(ps[:, j % 2, t * P:(t + 1) * P], xg[:, j % NBUF, t, 0:P], ident)
                            ins.then_inc(s_tp, 1)

                        def hidden(k, j):
                            n, u = k * 2 * NB2 + j, j // NB2
                            pe.wait_ge(s_xt, n + 1)
                            if j % NB2 == 0:
                                pe.wait_ge(s_w[u], 32 * (k + 1))
                            for c in range(EC):
                                ins = nc.tensor.matmul(ps[:, 2 + c // 2, c % 2 * S:(c % 2 + 1) * S],
                                                       we1[:, u, c * P:(c + 1) * P], xt[:, j % 2, :], start=True, stop=True)
                                if c % 2:
                                    ins.then_inc(s_h, 1)

                        def output(k, j):
                            n, u = k * 2 * NB2 + j, j // NB2
                            pe.wait_ge(s_ht, (n + 1) * EC)
                            for t in range(2):
                                for c in range(EC):
                                    ins = nc.tensor.matmul(ps[:, 6 + j % 2, t * P:(t + 1) * P], ht[:, c, t * P:(t + 1) * P],
                                                           we2[:, u, c, :], start=(c == 0), stop=(c == EC - 1))
                            ins.then_inc(s_y, 1)

                        def pair(k, final):
                            for j in range(2 * NB2):
                                hidden(k, j)
                                if j < 2 * NB2 - 1:
                                    turn(k, j + 1)
                                elif not final:
                                    turn(k + 1, 0)
                                output(k, j)

                        turn(0, 0)
                        with pe.Fori(0, E // 2 - 1) as k:
                            pair(k, False)
                        pair(E // 2 - 1, True)

                    @block.scalar
                    def _(act):
                        nc.scalar.preload_act_table(ACT.Gelu)
                        with act.Fori(0, E // 2) as k:
                            for j in range(2 * NB2):
                                n, u = k * 2 * NB2 + j, j // NB2
                                if j % NB2 == 0:
                                    act.wait_ge(s_bs, k * 2 + u + 1)
                                    act.sem_inc(s_hold, 1)
                                for c in range(EC):
                                    act.wait_ge(s_h, n * 2 + c // 2 + 1)
                                    nc.scalar.activation(ht[:, c, :], ps[:, 2 + c // 2, c % 2 * S:(c % 2 + 1) * S], ACT.Gelu,
                                                         bias=bs[:, u, c:c + 1]).then_inc(s_ht, 1)

        experts()

        with ExitStack() as ph:
            CT = 8
            STEPS = NT // CT
            yy = sb("fin_y", [P, 2, 2, CT * P], c=ph)
            s_ld = [sem(f"fin_load{u}", ph) for u in range(2)]
            s_c, s_fin, s_out, s_hold = sem("fin_chain", ph), sem("fin_sum", ph), sem("fin_stored", ph), sem("fin_hold", ph)
            out_v = out.rearrange("b s d -> (b s) d").rearrange("(i t p) d -> i p t d", t=CT, p=P)
            y_v = y_dram[0:2 * T, :].rearrange("(c i t p) d -> c i p t d", c=2, t=CT, p=P)
            with nc.Block() as block:
                @block.sync
                def _(sp):
                    def load(i, u):
                        for c in range(2):
                            sp.dma_start(yy[:, u, c, :].rearrange("p (t d) -> p t d", t=CT),
                                         y_v[c, bass.ds(i, 1)].rearrange("i p t d -> (i p) t d")).then_inc(s_ld[u], 16)

                    load(0, 0)
                    load(1, 1)
                    with sp.Fori(1, STEPS // 2) as k:
                        for u in range(2):
                            sp.wait_ge(s_fin, k * 2 + u - 1)
                            sp.sem_inc(s_hold, 1)
                            load(k * 2 + u, u)

                @block.vector
                def _(dve):
                    with dve.Fori(0, STEPS // 2) as k:
                        for u in range(2):
                            i = k * 2 + u
                            link = Chain(dve, s_c, i)
                            xb = x2[:, bass.ds(i * CT * P, CT * P)]
                            dve.wait_ge(s_ld[u], 32 * (k + 1))
                            link(nc.vector.tensor_tensor(yy[:, u, 0, :], yy[:, u, 0, :], yy[:, u, 1, :], ALU.add))
                            nc.vector.tensor_tensor(xb, xb, yy[:, u, 0, :], ALU.add).then_inc(s_fin, 1)

                @block.scalar
                def _(act):
                    with act.Fori(0, STEPS) as i:
                        act.wait_ge(s_fin, i + 1)
                        act.sem_inc(s_hold, 1)
                        act.dma_start(out_v[bass.ds(i, 1)].rearrange("i p t d -> (i p) t d"),
                                      x2[:, bass.ds(i * CT * P, CT * P)].rearrange("p (t d) -> p t d", t=CT))\
                            .then_inc(s_out, 16)
                    act.wait_ge(s_out, 16 * STEPS)


def host_layout(x, **w):
    w = {k: np.ascontiguousarray(v) for k, v in w.items()}
    t = {k[7:]: v for k, v in w.items() if k.startswith("L0_tok_")}
    col = lambda v: v.reshape(-1, P).T
    rep = lambda v: np.broadcast_to(v[None], (P,) + v.shape)
    return {k: np.ascontiguousarray(v) for k, v in {
        "ids": np.asarray(x, np.int32).reshape(NT, P).T,
        "consts": shape_constants(),
        "emb": t["emb"], "pos": t["pos"], "Wqk": t["Wqk"], "Wv": t["Wv"], "Wo": t["Wo"], "rots": t["rots"],
        "W1": t["W1"], "W2": t["W2"], "ln1_b0": col(t["ln1_b"][0]),
        "b1c": t["b1"].reshape(2, FC, P).transpose(2, 0, 1), "b2r": rep(t["b2"]),
        "lncol": np.concatenate([col(v) for v in (t["ln1_s"][1], t["ln1_b"][1], t["ln2_s"][0], t["ln2_b"][0],
                                                  t["ln2_s"][1], t["ln2_b"][1], w["L0_attn_ln_gamma"],
                                                  w["L0_attn_ln_beta"])], 1),
        "W_gh": w["L0_attn_W_gh"], "gate_wT": w["L0_ffn_gate_w"].T, "gate_b": rep(w["L0_ffn_gate_b"]),
        "bits": np.broadcast_to(1 << np.arange(29, -1, -1, dtype=np.int32)[None], (P, 30)),
        "ew1": w["L0_ffn_w1"], "ew2": w["L0_ffn_w2"],
        "eb1": w["L0_ffn_b1"].reshape(E * EC, P).T, "eb2": rep(w["L0_ffn_b2"]),
    }.items()}


_OUTS = [((B, S, P), "float32")]


def kernel(**inputs):
    import numpy as _np
    import concourse.bacc as _bacc
    from concourse import mybir as _mybir
    from concourse.bass_utils import run_bass_kernel_spmd as _run

    nc = _bacc.Bacc("TRN2", target_bir_lowering=False, num_devices=1)
    arrays, args = {}, {}
    for name, v in host_layout(**inputs).items():
        arrays[f"in_{name}_dram"] = v
        args[name] = nc.dram_tensor(f"in_{name}_dram", v.shape, _mybir.dt.from_np(v.dtype), kind="ExternalInput").ap()
    shape, dtype = _OUTS[0]
    out = nc.dram_tensor("out_0_dram", shape, _mybir.dt.from_np(_np.dtype(dtype)), kind="ExternalOutput").ap()
    build(nc, args, out)
    r = _run(nc, [arrays], core_ids=[0])
    return r.results[0]["out_0_dram"]
```

```python
from contextlib import ExitStack

import numpy as np

import concourse.bass as bass
from concourse import mybir

ALU = mybir.AluOpType
ACT = mybir.ActivationFunctionType
AX = mybir.AxisListType
F32 = mybir.dt.float32
BF16 = mybir.dt.bfloat16
I32 = mybir.dt.int32

P = 128
B, S = 32, 256
T = B * S
NT = T // P
V = 8000
F = 512
FC = F // P
H, DH = 8, 16
NHASH, NBUCKET, CS = 4, 64, 64
NC_ = S // CS
NK = NBUCKET // 2
BLK = 512
NBLK = T // BLK
GB = 4
NG = B // GB
GT = GB * S
E, HID, EC = 8, 512, 4
CAP = int(1.2 * T / E)
SLOTS = -(-CAP // P)
LN_EPS = 1e-5
GRU_EPS = 1e-10

_COLS = {}
_WIDTH = 0
for _name, _n in (("ident", P), ("block_sum", P), ("window", 32), ("den_sum", P), ("before", P),
                  ("same_expert", P), ("iota", P), ("first_k", NK), ("guard", 1), ("guard_eps", 1), ("pair_rows", 2), ("head_rows", 4),
                  ("partition", 1), ("half", 1), ("ranks", 3), ("ones", P), ("last", E),
                  ("token", NT), ("spare_row", E * SLOTS)):
    _COLS[_name] = (_WIDTH, _WIDTH + _n)
    _WIDTH += _n


def shape_constants():
    c = np.zeros((P, _WIDTH), np.float32)
    p, q = np.meshgrid(np.arange(P), np.arange(P), indexing="ij")

    def put(name, value):
        lo, hi = _COLS[name]
        c[:, lo:hi] = np.broadcast_to(value, (P, max(hi - lo, value.shape[1])))[:, :hi - lo]

    put("ident", p == q)
    put("block_sum", p // 32 == q // 32)
    same_head, same_hash = p // 16 == q // 16, p % 4 == q % 4
    cp, cq = p % 16 // 4, q % 16 // 4
    put("window", (p < 32) & same_head & same_hash & ((cp == cq) | (cp == (cq + 1) % NC_)))
    put("den_sum", NHASH * (same_head & same_hash))
    put("before", p < q)
    put("same_expert", p % E == q % E)
    put("iota", q)
    put("first_k", NK - np.arange(NK)[None, :])
    guard = np.arange(P)[:, None] % 32 == 16
    put("guard", guard)
    put("guard_eps", 1e-6 * guard)
    put("pair_rows", np.arange(P)[:, None] % 32 // 16 == np.arange(2)[None, :])
    put("head_rows", (np.arange(P)[:, None] // 32 == np.arange(4)[None, :]) * np.where(guard, -1.0, 1.0))
    put("half", np.full((P, 1), 0.5))
    put("partition", np.arange(P)[:, None])
    put("ranks", CS * np.arange(1, NC_)[None, :])
    put("ones", np.ones((P, P)))
    put("last", E - np.arange(E)[None, :])
    put("token", np.arange(NT)[None, :] * P + np.arange(P)[:, None])
    put("spare_row", 2 * T + np.arange(E * SLOTS)[None, :] * P + np.arange(P)[:, None])
    return c


class Chain:

    def __init__(self, eng, sem, base=0):
        self.eng, self.sem, self.base, self.n = eng, sem, base, 0

    def __call__(self, ins):
        self.n += 1
        ins.then_inc(self.sem, 1)
        self.eng.wait_ge(self.sem, self.base + self.n)


def build(nc, a, out):
    with ExitStack() as ctx:
        def sb(name, shape, dt=F32, c=ctx):
            return c.enter_context(nc.sbuf_tensor(name, shape, dt))

        def sem(name, c=ctx):
            return c.enter_context(nc.semaphore(name))

        ps = ctx.enter_context(nc.psum_tensor("ps", [P, 8, 512], F32))
        x1 = sb("x1", [P, NT * P])
        x2 = sb("x2", [P, NT * P])
        const = sb("const", [P, _WIDTH])
        stats = sb("stats", [P, NT, 6])
        mean = sb("mean", [P, NT])
        rstd = sb("rstd", [P, NT])
        tmp = sb("tmp", [P, 2, NT])
        b1c = sb("b1c", [P, 2, FC])
        b2r = sb("b2r", [P, 2, P])
        lncol = sb("lncol", [P, 8])
        s_load = sem("s_load")
        s_dv = sem("s_dv")
        s_sq = sem("s_sq")
        dv_count = [0]
        s_var, s_root = sem("s_var"), sem("s_root")
        root_count = [0]

        def C(name):
            return const[:, _COLS[name][0]:_COLS[name][1]]

        ident = C("ident")

        def finish_stats(dve, w):
            link = Chain(dve, s_dv, dv_count[0])
            me, mo = stats[:, w, 1], stats[:, w, 4]
            link(nc.vector.tensor_tensor(mean[:, w], me, mo, ALU.add))
            link(nc.vector.tensor_tensor(tmp[:, 0, w], me, mo, ALU.subtract))
            link(nc.vector.tensor_scalar(mean[:, w], mean[:, w], 0.5, None, ALU.mult))
            link(nc.vector.scalar_tensor_tensor(out=tmp[:, 0, w], in0=tmp[:, 0, w], scalar=0.25, in1=tmp[:, 0, w],
                                                op0=ALU.mult, op1=ALU.mult))
            link(nc.vector.tensor_tensor(tmp[:, 1, w], stats[:, w, 2], stats[:, w, 5], ALU.add))
            link(nc.vector.scalar_tensor_tensor(out=tmp[:, 1, w], in0=tmp[:, 1, w], scalar=1.0 / P, in1=tmp[:, 0, w],
                                                op0=ALU.mult, op1=ALU.add))
            return link

        def rstd_phase(eps, gru=False, w=slice(0, NT)):
            done = root_count[0]
            root_count[0] += 2 if gru else 1
            with nc.Block() as block:
                @block.vector
                def _(dve):
                    link = finish_stats(dve, w)
                    nc.vector.tensor_scalar(tmp[:, 0, w], tmp[:, 1, w], eps, None, ALU.add).then_inc(s_var, 1)
                    dve.wait_ge(s_root, done + 1)
                    link(nc.vector.reciprocal(rstd[:, w], rstd[:, w]))
                    if gru:
                        link(nc.vector.tensor_tensor(tmp[:, 0, :], rstd[:], rstd[:], ALU.mult))
                        link(nc.vector.tensor_tensor(tmp[:, 1, :], tmp[:, 1, :], tmp[:, 0, :], ALU.mult))
                        nc.vector.tensor_scalar(tmp[:, 0, :], tmp[:, 1, :], GRU_EPS, None, ALU.add).then_inc(s_var, 1)
                        dve.wait_ge(s_root, done + 2)
                        link(nc.vector.reciprocal(gru_r[:], gru_r[:]))
                    dv_count[0] += link.n

                @block.scalar
                def _(act):
                    act.wait_ge(s_var, done + 1)
                    nc.scalar.activation(rstd[:, w], tmp[:, 0, w], ACT.Sqrt).then_inc(s_root, 1)
                    if gru:
                        act.wait_ge(s_var, done + 2)
                        nc.scalar.activation(gru_r[:], tmp[:, 0, :], ACT.Sqrt).then_inc(s_root, 1)

        gru_r = sb("gru_r", [P, NT])

        GG = 8
        first_layer = ctx.enter_context(ExitStack())
        ids = sb("ids", [P, NT], I32, first_layer)
        posc = sb("posc", [P, 2, P], c=first_layer)
        s_gather = [sem(f"s_gather{g}") for g in range(2)]
        s_added = sem("s_added")
        PARTS = ((0, 1), (1, 4), (4, NT // GG))

        def gather(pool, lo, hi, first=False):
            for g in range(lo, hi + 1):
                if g < hi:
                    for t in range(g * GG, (g + 1) * GG):
                        nc.gpsimd.indirect_dma_start(
                            out=x1[:, t * P:(t + 1) * P], out_offset=None, in_=a["emb"],
                            in_offset=bass.IndirectOffsetOnAxis(ap=ids[:, t:t + 1], axis=0),
                        ).then_inc(s_gather[g % 2], 16)
                if g > lo:
                    x1g = x1[:, (g - 1) * GG * P:g * GG * P].rearrange("p (t w) -> p t w", w=2 * P)
                    pool.wait_ge(s_gather[(g - 1) % 2], 16 * GG * ((g - 1) // 2 + 1))
                    if first:
                        pool.wait_ge(s_t1, 3)
                    nc.gpsimd.tensor_tensor(x1g, x1g, posc[:].rearrange("p t d -> p (t d)").unsqueeze(1)
                                            .broadcast_to((P, GG // 2, 2 * P)), ALU.add).then_inc(s_added, 1)

        def gathered_stats(dve, lo, hi):
            for g in range(lo, hi):
                dve.wait_ge(s_added, g + 1)
                for t in range(g * GG, (g + 1) * GG):
                    nc.vector.bn_stats(stats[:, t, :], x1[:, t * P:(t + 1) * P])

        with ExitStack() as ph:
            pos = sb("pos", [P, 2, P], c=ph)
            idf = sb("idf", [P, 2, NT], c=ph)
            wv0 = sb("wv0", [P, P], c=ph)
            wo0 = sb("wo0", [P, P], c=ph)
            lb0 = sb("lb0", [P, 1], c=ph)
            t1 = sb("t1", [P, P], c=ph)
            s_ids = sem("s_ids")
            s_idx = sem("s_idx")
            s_c0 = sem("s_c0")
            s_t1 = sem("s_t1")
            with nc.Block() as block:
                @block.sync
                def _(sp):
                    sp.dma_start(ids[:], a["ids"]).then_inc(s_ids, 16)
                    sp.dma_start(const[:], a["consts"]).then_inc(s_load, 16)
                    sp.dma_start(pos[:], a["pos"][0, 0:S, :].rearrange("(t p) d -> p t d", p=P)).then_inc(s_load, 16)
                    sp.dma_start(wv0[:], a["Wv"][0]).then_inc(s_load, 16)
                    sp.dma_start(wo0[:], a["Wo"][0]).then_inc(s_load, 16)
                    sp.dma_start(lb0[:], a["ln1_b0"]).then_inc(s_load, 16)
                    sp.dma_start(b1c[:], a["b1c"]).then_inc(s_load, 16)
                    sp.dma_start(b2r[:], a["b2r"]).then_inc(s_load, 16)
                    sp.dma_start(lncol[:], a["lncol"]).then_inc(s_load, 16)
                    sp.wait_ge(s_load, 8 * 16)

                @block.vector
                def _(dve):
                    link = Chain(dve, s_dv, dv_count[0])
                    dve.wait_ge(s_ids, 16)
                    link(nc.vector.tensor_copy(idf[:, 0, :], ids[:]))
                    link(nc.vector.tensor_scalar(idf[:, 1, :], idf[:, 0, :], 0.0, float(V), ALU.is_lt, ALU.mult))
                    link(nc.vector.tensor_tensor(idf[:, 0, :], idf[:, 0, :], idf[:, 1, :], ALU.add))
                    nc.vector.tensor_scalar(ids[:], idf[:, 0, :], 0.0, float(V - 1), ALU.max, ALU.min).then_inc(s_idx, 1)
                    dve.wait_ge(s_c0, 1)
                    nc.vector.tensor_scalar(t1[:], C("ones"), ps[:, 0, 0:1], None, ALU.mult).then_inc(s_t1, 1)
                    dve.wait_ge(s_c0, 2)
                    for t in range(2):
                        ins = nc.vector.tensor_tensor(posc[:, t, :], ps[:, 1, 0:P], pos[:, t, :], ALU.add)
                        ins.then_inc(s_t1, 1)
                    gathered_stats(dve, *PARTS[0])
                    dv_count[0] += link.n

                @block.tensor
                def _(pe):
                    pe.wait_ge(s_load, 128)
                    nc.tensor.matmul(ps[:, 0, 0:1], wv0[:], lb0[:], start=True, stop=True).then_inc(s_c0, 1)
                    pe.wait_ge(s_t1, 1)
                    nc.tensor.matmul(ps[:, 1, 0:P], t1[:], wo0[:], start=True, stop=True).then_inc(s_c0, 1)

                @block.gpsimd
                def _(pool):
                    pool.wait_ge(s_idx, 1)
                    gather(pool, *PARTS[0], first=True)


        def feed_forward(layer):
            with ExitStack() as ph:
                w1 = sb(f"f{layer}_w1", [P, F], c=ph)
                w2 = sb(f"f{layer}_w2", [P, FC, P], c=ph)
                s_w = sem(f"f{layer}_weights")
                if layer:
                    rstd_phase(LN_EPS)
                    blocks_of(layer, 0, NBLK, w1, w2, s_w)
                else:
                    for n, (lo, hi) in enumerate(PARTS):
                        rstd_phase(LN_EPS, w=slice(lo * GG, hi * GG))
                        ahead = PARTS[n + 1] if n + 1 < len(PARTS) else None
                        blocks_of(0, lo * GG // 4, hi * GG // 4, w1, w2, s_w, ahead)

        def blocks_of(layer, lo, hi, w1, w2, s_w, ahead=None):
            with ExitStack() as ph:
                L = f"f{layer}_{lo}_"
                N = hi - lo
                sum_sems = [sem(L + "sum", ph), sem(L + "hold", ph)] if layer == 1 else None
                xh = sb(L + "xh", [P, 2, BLK], c=ph)
                lt = sb(L + "lt", [P, 2, BLK], c=ph)
                ht = sb(L + "ht", [P, 2, FC, BLK], c=ph)
                s_xh, s_tp, s_lt = sem(L + "normed"), sem(L + "turned"), sem(L + "lt_ready")
                s_h, s_ht, s_y = sem(L + "hidden"), sem(L + "gelu"), sem(L + "output")
                s_x2 = sem(L + "x2")
                lns, lnb = lncol[:, 2 + 2 * layer:3 + 2 * layer], lncol[:, 3 + 2 * layer:4 + 2 * layer]
                H0, Y0 = 2, 6

                with nc.Block() as block:
                    @block.sync
                    def _(sp):
                        if lo == 0:
                            sp.dma_start(w1[:], a["W1"][layer]).then_inc(s_w, 16)
                            sp.dma_start(w2[:], a["W2"][layer].rearrange("(c p) d -> p c d", p=P)).then_inc(s_w, 16)

                    @block.vector
                    def _(dve):
                        def norm(i, u):
                            for t in range(4):
                                ins = nc.vector.tensor_scalar(
                                    xh[:, u, t * P:(t + 1) * P], x1[:, bass.ds((i + lo) * BLK + t * P, P)],
                                    mean[:, bass.ds((i + lo) * 4 + t, 1)], rstd[:, bass.ds((i + lo) * 4 + t, 1)],
                                    ALU.subtract, ALU.mult)
                            ins.then_inc(s_xh, 1)

                        def residual(i, u):
                            x2b = x2[:, bass.ds((i + lo) * BLK, BLK)]
                            if layer == 0:
                                bias = b2r[:, layer, :].unsqueeze(1).broadcast_to((P, 4, P))
                                dve.wait_ge(s_y, i + 1)
                                nc.vector.tensor_tensor(x2b.rearrange("p (t d) -> p t d", t=4),
                                                        ps[:, Y0 + u, :].rearrange("p (t d) -> p t d", t=4), bias, ALU.add)\
                                    .then_inc(s_x2, 1)
                            else:
                                dve.wait_ge(sum_sems[0], i * 3 + 3)
                                dve.wait_ge(s_y, i + 1)
                                nc.vector.scalar_tensor_tensor(out=x2b, in0=ps[:, Y0 + u, :], scalar=0.5, in1=x2b,
                                                               op0=ALU.mult, op1=ALU.add).then_inc(s_x2, 1)

                        def statistics(i):
                            dve.wait_ge(s_x2, i + 1)
                            for t in range(4):
                                nc.vector.bn_stats(stats[:, bass.ds((i + lo) * 4 + t, 1), :].rearrange("p a b -> p (a b)"),
                                                   x2[:, bass.ds((i + lo) * BLK + t * P, P)])

                        def next_norm(i, u):
                            dve.wait_ge(s_tp, i - 1)
                            norm(i, u)

                        def body(i, u, more=True):
                            residual(i, u)
                            if more:
                                next_norm(i + 3, 1 - u)
                            statistics(i)

                        norm(0, 0)
                        norm(1, 1)
                        if N > 2:
                            next_norm(2, 0)
                            with dve.Fori(0, N // 2 - 2) as k:
                                for u in range(2):
                                    body(k * 2 + u, u)
                            body(N - 4, 0)
                            body(N - 3, 1, more=False)
                        if ahead:
                            gathered_stats(dve, *ahead)
                        body(N - 2, 0, more=False)
                        body(N - 1, 1, more=False)

                    @block.gpsimd
                    def _(pool):
                        if ahead:
                            gather(pool, *ahead)
                        if layer == 1:
                            s_sum, s_hold = sum_sems
                            bias = b2r[:, layer, :].unsqueeze(1).broadcast_to((P, 4, P))
                            with pool.Fori(0, NBLK) as i:
                                link = Chain(pool, s_sum, i * 3)
                                x2b = x2[:, bass.ds(i * BLK, BLK)]
                                x2v = x2b.rearrange("p (t d) -> p t d", t=4)
                                link(nc.gpsimd.tensor_tensor(x2b, x2b, x1[:, bass.ds(i * BLK, BLK)], ALU.add))
                                pool.sem_inc(s_hold, 1)
                                link(nc.gpsimd.tensor_tensor(x2v, x2v, bias, ALU.add))
                                pool.sem_inc(s_hold, 1)
                                nc.gpsimd.tensor_tensor(x2b, x2b, C("half").broadcast_to((P, BLK)), ALU.mult)\
                                    .then_inc(s_sum, 1)

                    @block.tensor
                    def _(pe):
                        def turn(i, u):
                            pe.wait_ge(s_xh, i + 1)
                            for t in range(4):
                                ins = nc.tensor.transpose(ps[:, u, t * P:(t + 1) * P], xh[:, u, t * P:(t + 1) * P], ident)
                            ins.then_inc(s_tp, 1)

                        def hidden(i, u, first=False):
                            pe.wait_ge(s_lt, i + 1)
                            for c in range(FC):
                                if not first:
                                    pe.wait_ge(s_ht, (i - 1) * FC + c + 1)
                                nc.tensor.matmul(ps[:, H0 + c, :], w1[:, c * P:(c + 1) * P], lt[:, u, :],
                                                 start=True, stop=True).then_inc(s_h, 1)

                        def output(i, u, first=False):
                            pe.wait_ge(s_ht, i * FC + FC)
                            if not first:
                                pe.wait_ge(s_x2, i - 1)
                            for t in range(4):
                                for c in range(FC):
                                    ins = nc.tensor.matmul(ps[:, Y0 + u, t * P:(t + 1) * P],
                                                           ht[:, u, c, t * P:(t + 1) * P], w2[:, c, :],
                                                           start=(c == 0), stop=(c == FC - 1))
                            ins.then_inc(s_y, 1)

                        def body(i, u, first=False):
                            hidden(i + 1, 1 - u)
                            turn(i + 2, u)
                            output(i, u, first)

                        pe.wait_ge(s_w, 32)
                        turn(0, 0)
                        hidden(0, 0, first=True)
                        turn(1, 1)
                        if N > 2:
                            body(0, 0, first=True)
                            body(1, 1, first=True)
                        if N > 4:
                            with pe.Fori(1, N // 2 - 1) as k:
                                for u in range(2):
                                    body(k * 2 + u, u)
                        hidden(N - 1, 1)
                        output(N - 2, 0, first=(N == 2))
                        output(N - 1, 1, first=(N == 2))

                    @block.scalar
                    def _(act):
                        nc.scalar.preload_act_table(ACT.Gelu_apprx_tanh)

                        def evac(i, u):
                            act.wait_ge(s_tp, i + 1)
                            nc.scalar.activation(lt[:, u, :], ps[:, u, :], ACT.Identity, scale=lns, bias=lnb)\
                                .then_inc(s_lt, 1)

                        def gelus(i, u):
                            for c in range(FC):
                                act.wait_ge(s_h, i * FC + c + 1)
                                nc.scalar.activation(ht[:, u, c, :], ps[:, H0 + c, :], ACT.Gelu_apprx_tanh,
                                                     bias=b1c[:, layer, c:c + 1]).then_inc(s_ht, 1)

                        evac(0, 0)
                        gelus(0, 0)
                        evac(1, 1)
                        if N > 2:
                            with act.Fori(0, N // 2 - 1) as k:
                                for u in range(2):
                                    gelus(k * 2 + u + 1, 1 - u)
                                    evac(k * 2 + u + 2, u)
                        gelus(N - 1, 1)

        feed_forward(0)
        first_layer.close()
        rstd_phase(LN_EPS)

        def attention():
            with ExitStack() as ph:
                def psb(name, shape, dt=F32):
                    return sb("at_" + name, shape, dt, ph)

                def psem(name):
                    return sem("at_" + name, ph)

                QP = 32
                HS = 4
                NS = H // HS
                HP = H // 2
                W3 = 3 * 32
                wqk = psb("wqk", [P, NS, HS, QP])
                wv = psb("wv", [P, H, 32])
                wo = psb("wo", [P, P])
                rots = psb("rots", [P, NS, HS * NHASH * NK])
                xh = psb("xh", [P, 2, BLK])
                lt = psb("lt", [P, 2, BLK])
                sq = psb("sq", [P, NS, GT])
                nrm = psb("nrm", [P, NS, GT])
                qk_ = psb("qk", [P, 2, NS, GT])
                scale_ = psb("scale", [P, 2, NS * 8 * HS])
                vp_ = psb("vp", [P, 2, GT // P, H, 32])
                cn_ = psb("cn", [P, 2, 2, GB, P], BF16)
                qd = psb("qd", [P, 2, NS, HS, S])
                wd = psb("wd", [W3, HP, 2, S], BF16)
                ee = psb("ee", [P, 2, 2, H, S])
                cp = psb("cp", [P, 2, 2, H, 32])
                hi_ = psb("hi", [P, 2, H * NHASH])
                ext_ = psb("ext", [P, 2, H * NHASH])
                wins_ = psb("pos_wins", [P, 2, H * NHASH], I32)
                hit_ = [lt[:, i, :].bitcast(BF16).rearrange("p (x k) -> p x k", k=NK) for i in range(2)]
                identb = psb("identb", [P, P], BF16)
                windowb = psb("windowb", [W3, 32], BF16)
                fk = psb("fk", [P, NK], BF16)
                bt = psb("bt", [P, 2, GB, H * NHASH])
                rows, chunk = (psb(n, [P, S], BF16)[:] for n in ("rows", "chunk"))
                flags = psb("flags", [P, 4, S], BF16)
                ct = psb("ct", [W3, HP, S], BF16)
                mt, ot = psb("mt", [P, S]), psb("ot", [P, S])
                ws = psb("ws", [P, S])
                wb = psb("wb", [P, 3, S], BF16)
                thr = psb("thr", [P, 6, 3])
                chunk_t = ps[:, 2, S:2 * S].bitcast(BF16)[:, 0:S]
                ctb = ps[0:W3, 2, :].bitcast(BF16).rearrange("p (a w) -> p a w", w=S)
                s_cp = psem("cp")
                s_hold = psem("hold")
                s_zero, s_w = psem("zero"), psem("weights")
                s_xh, s_tp, s_lt, s_q, s_v, s_sq, s_vp, s_qc, s_n2, s_nrm, s_qk, s_kt, s_scale = (
                    psem(n) for n in ("normed", "turned", "lt", "q", "v", "squares", "vp", "q_copied", "norm2", "norm",
                                      "qk", "keys_turned", "scale"))
                s_rot, s_hit, s_hm, s_am, s_bt, s_chunk, s_chT, s_c = (
                    psem(n) for n in ("rot", "hit", "hit_index", "argmax", "buckets_turned", "chunk", "chunk_turned", "c"))
                s_qd, s_s, s_exp, s_ct, s_cts, s_mt, s_mts, s_d, s_xw, s_den, s_ws, s_sel, s_wd, s_g, s_a, s_o, s_ot, s_y, s_x1 = (
                    psem(n) for n in ("qd", "scores", "exp", "ct", "ct_out", "mt", "mt_out", "d", "xw", "den", "ws", "sel",
                                      "wd", "g", "a", "o", "ot", "y", "x1"))
                s_ch, s_cw = psem("chain"), psem("chain_w")
                KCH = 87
                HEAD = 4
                KW = 5
                s_wload = psem("wload")
                HITS = (((1, 2), (3,)), ((4, 5), (6,)), ((7,), ()))
                ROTS = (((2,), (3,)), ((4, 5), (6,)), ((7,), ()))

                LASTG = NG - 1

                def bodies(eng, body):
                    with eng.Fori(0, (NG - 2) // 2) as k:
                        for u in range(2):
                            body(k * 2 + u, u, True, True)
                    body(NG - 2, 0, True, False)
                    body(LASTG, 1, False, False)

                WLOADS = 16 * (3 + NS * (1 + HS))

                with nc.Block() as block:
                    @block.sync
                    def _(sp):
                        sp.wait_ge(s_zero, 4)
                        sp.dma_start(wo[:], a["Wo"][1]).then_inc(s_wload, 16)
                        n = 16
                        for s in range(NS):
                            sp.dma_start(wqk[:, s, :, 0:DH], a["Wqk"][1][:, s * 64:(s + 1) * 64]
                                         .rearrange("p (j d) -> p j d", j=HS)).then_inc(s_wload, 16)
                            n += 16
                            for j in range(HS):
                                dst = rots[32 * j:32 * j + DH, s, j * P:(j + 1) * P].rearrange("d (r k) -> d r k", r=NHASH)
                                sp.dma_start(dst, a["rots"][1, s * HS + j].rearrange("r d k -> d r k"))\
                                    .then_inc(s_wload, 16)
                                n += 16
                        wvv = wv[:].rearrange("p (j e) w -> p j e w", e=2)
                        src = a["Wv"][1].rearrange("p (j e d) -> p j e d", e=2, d=DH)
                        for e in range(2):
                            sp.dma_start(wvv[:, :, e, 16 * e:16 * e + DH], src[:, :, e, :]).then_inc(s_wload, 16)
                            n += 16
                        assert n == WLOADS, n

                    @block.vector
                    def _(dve):
                        def norm(g):
                            for n in range(2):
                                for t in range(4):
                                    tile = g * 8 + n * 4 + t
                                    ins = nc.vector.tensor_scalar(
                                        xh[:, n, t * P:(t + 1) * P], x2[:, bass.ds(tile * P, P)],
                                        mean[:, bass.ds(tile, 1)], rstd[:, bass.ds(tile, 1)], ALU.subtract, ALU.mult)
                                ins.then_inc(s_xh, 1)

                        def keys(g, v):
                            dve.wait_ge(s_qc, g * 4 + 4)
                            dve.wait_ge(s_nrm, g + 1)
                            for s in range(NS):
                                dst = qk_[:, v, s, :]
                                nc.vector.scalar_tensor_tensor(out=dst, in0=nrm[:, s, :], scalar=C("guard"), in1=dst,
                                                               op0=ALU.mult, op1=ALU.add).then_inc(s_qk, 1)

                        def scales(g, v, link):
                            dve.wait_ge(s_kt, g + 1)
                            src = ps[:, 4:8, :].rearrange("p b (x w) -> p (b x) w", w=32)[:, :, 16:17]
                            dst = scale_[:, v, :].unsqueeze(2)
                            link(nc.vector.reciprocal(dst, src))
                            nc.vector.tensor_scalar(dst, dst, 0.25, None, ALU.mult).then_inc(s_scale, 1)

                        def find(g, t, link):
                            pair = 4 + 2 * (t % 2)
                            hi, ext, pos_wins = hi_[:, t % 2, :], ext_[:, t % 2, :], wins_[:, t % 2, :]
                            rot = ps[:, pair:pair + 2, :].rearrange("p b (x k) -> p (b x) k", k=NK)
                            dve.wait_ge(s_rot, g * 8 + t + 1)
                            if t >= 2:
                                dve.wait_ge(s_am, g * 8 + t - 1)
                            nc.vector.tensor_reduce(hi, rot, AX.X, ALU.max)
                            link(nc.vector.tensor_reduce(ext, rot, AX.X, ALU.min))
                            link(nc.vector.scalar_tensor_tensor(out=pos_wins, in0=ext, scalar=-1.0, in1=hi,
                                                                op0=ALU.mult, op1=ALU.is_le))
                            dve.sem_inc(s_hold, 1)
                            link(nc.vector.copy_predicated(ext, pos_wins, hi))
                            nc.vector.tensor_tensor(hit_[t % 2], rot, ext.unsqueeze(2).broadcast_to((P, H * NHASH, NK)),
                                                    ALU.is_equal).then_inc(s_hit, 1)

                        def bucket(g, t, link):
                            hi, pos_wins = hi_[:, t % 2, :], wins_[:, t % 2, :]
                            dve.wait_ge(s_hm, g * 8 + t + 1)
                            link(nc.vector.tensor_reduce(hi, hit_[t % 2], AX.X, ALU.max))
                            link(nc.vector.scalar_tensor_tensor(out=hi, in0=pos_wins, scalar=float(NK), in1=hi,
                                                                op0=ALU.mult, op1=ALU.add))
                            nc.vector.tensor_scalar(bt[:, t % 2, t // 2, :], hi, -1.0, float(NBUCKET),
                                                    ALU.mult, ALU.add).then_inc(s_am, 1)

                        def chunks(g, v, link):
                            dve.wait_ge(s_bt, g + 1)
                            link(nc.vector.tensor_copy(rows, ps[:, 2, 0:S]))
                            low, cand, count, below, ok, rest = (thr[:, i, :] for i in range(6))
                            bit = NBUCKET // 2
                            nc.vector.memset(low, 0.0)
                            link(nc.vector.memset(below, 0.0))
                            while bit >= 1:
                                link(nc.vector.tensor_scalar(cand, low, float(bit), None, ALU.add))
                                for k in range(3):
                                    ins = nc.vector.tensor_scalar(flags[:, k, :], rows, cand[:, k:k + 1], None, ALU.is_lt,
                                                                  ALU.add, accum_out=count[:, k:k + 1])
                                link(ins)
                                link(nc.vector.tensor_tensor(ok, count, C("ranks"), ALU.is_le))
                                nc.vector.scalar_tensor_tensor(out=low, in0=ok, scalar=float(bit), in1=low,
                                                               op0=ALU.mult, op1=ALU.add)
                                link(nc.vector.tensor_tensor(count, count, ok, ALU.mult))
                                link(nc.vector.tensor_tensor(below, below, count, ALU.max))
                                bit //= 2
                            link(nc.vector.tensor_tensor(rest, C("ranks"), below, ALU.subtract))
                            for k in range(3):
                                same, run, at = flags[:, 0, :], flags[:, 1, :], flags[:, 2, :]
                                link(nc.vector.tensor_scalar(same, rows, low[:, k:k + 1], None, ALU.is_equal))
                                link(nc.vector.tensor_tensor_scan(run, C("ones")[:, 0:1].broadcast_to((P, S)), same, 0.0, ALU.mult, ALU.add))
                                link(nc.vector.scalar_tensor_tensor(out=at, in0=run, scalar=rest[:, k:k + 1], in1=same,
                                                                    op0=ALU.is_gt, op1=ALU.mult))
                                link(nc.vector.scalar_tensor_tensor(out=(chunk if k == 0 else flags[:, 3, :]), in0=rows,
                                                                    scalar=low[:, k:k + 1], in1=at, op0=ALU.is_gt, op1=ALU.add))
                                if k == 1:
                                    link(nc.vector.tensor_tensor(chunk, chunk, flags[:, 3, :], ALU.add))
                                elif k == 2:
                                    nc.vector.tensor_tensor(chunk, chunk, flags[:, 3, :], ALU.add).then_inc(s_chunk, 1)
                            dve.wait_ge(s_chT, g + 1)
                            for t in range(2):
                                src = chunk_t[:, t * P:(t + 1) * P].rearrange("p (x r) -> p x r", r=NHASH)
                                dst = cn_[:, v, t, :, :].rearrange("p b (h c r) -> p (b h) c r", c=NC_, r=NHASH)
                                for c in range(NC_):
                                    ins = nc.vector.tensor_scalar(dst[:, :, c, :], src, float(c), None, ALU.is_equal)
                            ins.then_inc(s_c, 1)

                        def window_sum(n):
                            dve.wait_ge(s_d, n + 1)
                            nc.vector.tensor_tensor(ws[:], ps[:, 2, 0:S], mt[:], ALU.mult).then_inc(s_xw, 1)

                        def weights(n):
                            link = Chain(dve, s_cw, n * KW)
                            dve.wait_ge(s_den, n + 1)
                            link(nc.vector.reciprocal(ws[:], ps[:, 2, S:2 * S]))
                            link(nc.vector.tensor_tensor(ws[:], ws[:], mt[:], ALU.mult))
                            link(nc.vector.tensor_copy(wb[:, 0, :], ws[:]))
                            link(nc.vector.tensor_tensor(ws[:], ws[:], wb[:, 0, :], ALU.subtract))
                            link(nc.vector.tensor_copy(wb[:, 1, :], ws[:]))
                            nc.vector.tensor_tensor(wb[:, 2, :], ws[:], wb[:, 1, :], ALU.subtract).then_inc(s_ws, 1)

                        def weigh(n, b, half_way=None):
                            for k in range(8):
                                t, pr = k // 4, k % 4
                                if k == 4 and half_way:
                                    half_way()
                                dve.wait_ge(s_g, n * 8 + k + 1)
                                e2 = ee[:, b % 2, t, 2 * pr:2 * pr + 2, :]
                                nc.vector.tensor_tensor(e2, ps[:, k % 2, :].rearrange("p (h w) -> p h w", h=2), e2,
                                                        ALU.mult).then_inc(s_a, 1)

                        def residual(n):
                            dve.wait_ge(s_y, n + 1)
                            xb = x1[:, bass.ds(n * S, S)]
                            nc.vector.tensor_tensor(xb, ps[:, 3, S:2 * S], xb, ALU.add).then_inc(s_x1, 1)
                            dve.wait_ge(s_x1, n + 1)
                            for t in range(2):
                                nc.vector.bn_stats(stats[:, bass.ds(n * 2 + t, 1), :].rearrange("p a b -> p (a b)"),
                                                   x1[:, bass.ds(n * S + t * P, P)])

                        def hash_tiles(g, tiles, link):
                            for t in tiles:
                                find(g, t, link)
                                if t:
                                    bucket(g, t - 1, link)

                        def next_keys(g, v):
                            link = Chain(dve, s_ch, g * KCH)
                            keys(g, v)
                            return link

                        def body(g, u, more, front):
                            link = Chain(dve, s_ch, (g + 1) * KCH)
                            link.n = HEAD
                            for b in range(GB):
                                n = g * GB + b
                                weigh(n, b)
                                if more and b < 3:
                                    hash_tiles(g + 1, HITS[b][0], link)
                                if more and b == 3:
                                    chunks(g + 1, 1 - u, link)
                                    assert link.n == KCH, link.n
                                if front and b == 3:
                                    ahead = next_keys(g + 2, u)
                                if b < 3:
                                    window_sum(n + 1)
                                residual(n)
                                if more and b == 3:
                                    window_sum(n + 1)
                                if front and b == 3:
                                    scales(g + 2, u, ahead)
                                if more or b < 3:
                                    weights(n + 1)
                                if more and b < 3:
                                    hash_tiles(g + 1, HITS[b][1], link)
                                if more and b == 2:
                                    bucket(g + 1, 7, link)
                                if front and b == 2:
                                    norm(g + 2)
                                if front and b == 3:
                                    find(g + 2, 0, ahead)
                                    assert ahead.n == HEAD, ahead.n

                        for t in (wqk, wv, rots, cp):
                            nc.vector.memset(t[:], 0.0).then_inc(s_zero, 1)
                        link = Chain(dve, s_ch, 0)
                        norm(0)
                        nc.vector.tensor_copy(fk[:], C("first_k")).then_inc(s_w, 1)
                        nc.vector.tensor_copy(identb[:], ident).then_inc(s_w, 1)
                        nc.vector.tensor_copy(windowb[:], C("window")[0:W3]).then_inc(s_w, 1)
                        keys(0, 0)
                        scales(0, 0, link)
                        hash_tiles(0, range(8), link)
                        bucket(0, 7, link)
                        norm(1)
                        chunks(0, 0, link)
                        ahead = next_keys(1, 1)
                        window_sum(0)
                        scales(1, 1, ahead)
                        weights(0)
                        find(1, 0, ahead)
                        bodies(dve, body)

                    @block.tensor
                    def _(pe):
                        def turn_in(g):
                            for n in range(2):
                                pe.wait_ge(s_xh, g * 2 + n + 1)
                                for t in range(4):
                                    ins = nc.tensor.transpose(ps[:, 4 + n, t * P:(t + 1) * P], xh[:, n, t * P:(t + 1) * P], ident)
                                ins.then_inc(s_tp, 1)

                        def project_q(g, n):
                            if n == 0:
                                pe.wait_ge(s_lt, g * 2 + 2)
                            else:
                                pe.wait_ge(s_qc, g * 4 + 2)
                                pe.wait_ge(s_sq, g * 4 + 2)
                            for s in range(NS):
                                nc.tensor.matmul(ps[:, 6 + s, :], wqk[:, s, :, :].rearrange("p j d -> p (j d)"),
                                                 lt[:, n, :], start=True, stop=True).then_inc(s_q, 1)

                        def project_v(g, n):
                            if n:
                                pe.wait_ge(s_vp, g * 2 + 1)
                            for t in range(4):
                                ins = nc.tensor.matmul(ps[:, 4 + t // 2, (t % 2) * S:(t % 2 + 1) * S],
                                                       lt[:, n, t * P:(t + 1) * P], wv[:].rearrange("p h d -> p (h d)"),
                                                       start=True, stop=True)
                            ins.then_inc(s_v, 1)

                        def norms(g):
                            pe.wait_ge(s_sq, g * 4 + 4)
                            pe.wait_ge(s_qc, g * 4 + 4)
                            pe.wait_ge(s_vp, g * 2 + 2)
                            for s in range(NS):
                                for n in range(2):
                                    ins = nc.tensor.matmul(ps[:, 4 + 2 * s + n, :], C("block_sum"),
                                                           sq[:, s, n * BLK:(n + 1) * BLK], start=True, stop=True)
                            ins.then_inc(s_n2, 1)

                        def turn_keys(g, v):
                            pe.wait_ge(s_qk, g * 2 + 2)
                            pe.wait_ge(s_nrm, g + 1)
                            for s in range(NS):
                                for t in range(8):
                                    x = s * 8 + t
                                    ins = nc.tensor.transpose(ps[:, 4 + x // 4, x % 4 * P:(x % 4 + 1) * P],
                                                              qk_[:, v, s, t * P:(t + 1) * P], ident)
                            ins.then_inc(s_kt, 1)

                        def rotate(g, v, t):
                            if t < 2:
                                pe.wait_ge(s_scale, g + 1)
                            else:
                                pe.wait_ge(s_hit, g * 8 + t - 1)
                            for s in range(NS):
                                ins = nc.tensor.matmul(ps[:, 4 + 2 * (t % 2) + s, :], qk_[:, v, s, t * P:(t + 1) * P],
                                                       rots[:, s, :], start=True, stop=True)
                            ins.then_inc(s_rot, 1)

                        def turn_buckets(g):
                            pe.wait_ge(s_am, g * 8 + 8)
                            for t in range(2):
                                ins = nc.tensor.transpose(ps[:, 2, t * P:(t + 1) * P],
                                                          bt[:, t, :, :].rearrange("p b x -> p (b x)"), ident)
                            ins.then_inc(s_bt, 1)

                        def turn_chunks(g):
                            pe.wait_ge(s_chunk, g + 1)
                            for t in range(2):
                                ins = nc.tensor.transpose(chunk_t[:, t * P:(t + 1) * P], chunk[:, t * P:(t + 1) * P], identb[:])
                            ins.then_inc(s_chT, 1)

                        def scores(n, v, b, first=False, sums_of=None):
                            pe.wait_ge(s_qd, n * NS + 2)
                            for k in range(8):
                                t, s, pr = k // 4, k // 2 % 2, k % 2
                                if k == 3 and sums_of is not None:
                                    denominators(sums_of)
                                if k >= 2:
                                    pe.wait_ge(s_exp, n * 8 + k - 1)
                                elif not first:
                                    pe.wait_ge(s_a, (n - 2) * 8 + 8)
                                nc.tensor.matmul(ps[:, k % 2, :], qk_[:, v, s, b * S + t * P:b * S + (t + 1) * P],
                                                 qd[:, b % 2, s, 2 * pr:2 * pr + 2, :].rearrange("p j w -> p (j w)"),
                                                 start=True, stop=True).then_inc(s_s, 1)

                        def turn_c(u, b):
                            for t in range(2):
                                for pr in range(HP):
                                    for s in range(3):
                                        ins = nc.tensor.transpose(ctb[32 * s:32 * s + 32, pr, t * P:(t + 1) * P],
                                                                  cn_[:, u, t, b, 32 * pr:32 * pr + 32], identb[:])
                            ins.then_inc(s_ct, 1)

                        def windows(n):
                            pe.wait_ge(s_cts, n + 1)
                            for pr in range(HP):
                                ins = nc.tensor.matmul(ps[32 * pr:32 * pr + 32, 2, 0:S], windowb[:], ct[:, pr, :],
                                                       start=True, stop=True)
                            ins.then_inc(s_mt, 1)

                        def sums(n, b):
                            pe.wait_ge(s_exp, n * 8 + 8)
                            pe.wait_ge(s_cp, n * 2 + 2)
                            pe.wait_ge(s_mts, n + 1)
                            for i, (e, t) in enumerate(((0, 0), (0, 1), (1, 0), (1, 1))):
                                for j in range(4):
                                    h = 2 * j + e
                                    ins = nc.tensor.matmul(ps[32 * j:32 * j + 32, 2, 0:S], cp[:, b % 2, t, h, :],
                                                           ee[:, b % 2, t, h, :], start=(i == 0), stop=(i == 3))
                            ins.then_inc(s_d, 1)

                        def denominators(n):
                            pe.wait_ge(s_xw, n + 1)
                            nc.tensor.matmul(ps[:, 2, S:2 * S], C("den_sum"), ws[:], start=True, stop=True)\
                                .then_inc(s_den, 1)

                        def place_w(n, scored):
                            pe.wait_ge(s_ws, n + 1)
                            if scored:
                                pe.wait_ge(s_exp, n * 8 + 16)
                            for pr in range(HP):
                                for s in range(3):
                                    ins = nc.tensor.matmul(ps[32 * s:32 * s + 32, pr // 2, pr % 2 * S:(pr % 2 + 1) * S],
                                                           identb[:, 32 * pr:32 * pr + 32], wb[:, s, :], start=True, stop=True)
                            ins.then_inc(s_sel, 1)

                        def products(n, between):
                            for k in range(8):
                                t, pr = k // 4, k % 4
                                if k in between:
                                    between[k]()
                                if k >= 2:
                                    pe.wait_ge(s_a, n * 8 + k - 1)
                                else:
                                    pe.wait_ge(s_wd, n * 2 + 2)
                                nc.tensor.matmul(ps[:, k % 2, :], ct[:, pr, t * P:(t + 1) * P],
                                                 wd[:, pr, :, :].rearrange("p h w -> p (h w)"),
                                                 start=True, stop=True).then_inc(s_g, 1)

                        def attend(n, u, b):
                            pe.wait_ge(s_a, n * 8 + 8)
                            for i, (e, t) in enumerate(((0, 0), (0, 1), (1, 0), (1, 1))):
                                for j in range(4):
                                    h = 2 * j + e
                                    ins = nc.tensor.matmul(ps[32 * j:32 * j + 32, 3, 0:S], vp_[:, u, 2 * b + t, h, :],
                                                           ee[:, b % 2, t, h, :], start=(i == 0), stop=(i == 3))
                            ins.then_inc(s_o, 1)

                        def output(n):
                            pe.wait_ge(s_ot, n + 1)
                            for t in range(2):
                                ins = nc.tensor.matmul(ps[:, 3, S + t * P:S + (t + 1) * P], ot[:, t * P:(t + 1) * P],
                                                       wo[:], start=True, stop=True)
                            ins.then_inc(s_y, 1)

                        def body(g, u, more, front):
                            v = 1 - u
                            for b in range(GB):
                                n = g * GB + b
                                place_w(n, more or b < 3)
                                between = {}
                                if b < 3:
                                    between[4] = lambda: turn_c(u, b + 1)
                                if more and b < 3:
                                    for at, t in zip((2, 6), ROTS[b][0]):
                                        between[at] = lambda t=t: rotate(g + 1, v, t)
                                elif more:
                                    between[2] = lambda: turn_buckets(g + 1)
                                products(n, between)
                                if front and b == 3:
                                    turn_in(g + 2)
                                attend(n, u, b)
                                if b < 3:
                                    windows(n + 1)
                                output(n)
                                if b < 3:
                                    sums(n + 1, b + 1)
                                    if more:
                                        for t in ROTS[b][1]:
                                            rotate(g + 1, v, t)
                                if b < 2:
                                    scores(n + 2, u, b + 2, sums_of=n + 1)
                                elif more:
                                    scores(n + 2, v, b - 2, sums_of=n + 1 if b < 3 else None)
                                elif b < 3:
                                    denominators(n + 1)
                                if more and b == 3:
                                    start_chunks(g + 2, v, n + 1, u if front else None)

                        def start_chunks(g, v, n, keys_of):
                            if keys_of is not None:
                                project_q(g, 0)
                                project_v(g, 0)
                                project_q(g, 1)
                            turn_chunks(g - 1)
                            if keys_of is not None:
                                project_v(g, 1)
                            pe.wait_ge(s_c, g)
                            turn_c(v, 0)
                            if keys_of is not None:
                                norms(g)
                            windows(n)
                            sums(n, 0)
                            if keys_of is not None:
                                turn_keys(g, keys_of)
                            denominators(n)
                            if keys_of is not None:
                                rotate(g, keys_of, 0)
                                rotate(g, keys_of, 1)

                        turn_in(0)
                        pe.wait_ge(s_wload, WLOADS)
                        pe.wait_ge(s_w, 3)
                        for n in range(2):
                            project_q(0, n)
                            project_v(0, n)
                        norms(0)
                        turn_keys(0, 0)
                        rotate(0, 0, 0)
                        rotate(0, 0, 1)
                        scores(0, 0, 0, first=True)
                        pe.wait_ge(s_exp, 8)
                        scores(1, 0, 1, first=True)
                        for t in range(2, 8):
                            rotate(0, 0, t)
                        turn_buckets(0)
                        turn_in(1)
                        start_chunks(1, 0, 0, 1)
                        bodies(pe, body)

                    @block.scalar
                    def _(act):
                        def front_in(g):
                            for n in range(2):
                                act.wait_ge(s_tp, g * 2 + n + 1)
                                nc.scalar.activation(lt[:, n, :], ps[:, 4 + n, :], ACT.Identity, scale=lncol[:, 0:1],
                                                     bias=lncol[:, 1:2]).then_inc(s_lt, 1)

                        def take_q(g, v, n):
                            for s in range(NS):
                                act.wait_ge(s_q, g * 4 + n * 2 + s + 1)
                                nc.scalar.activation(qk_[:, v, s, n * BLK:(n + 1) * BLK], ps[:, 6 + s, :], ACT.Identity,
                                                     bias=C("guard_eps")).then_inc(s_qc, 1)
                                nc.scalar.activation(sq[:, s, n * BLK:(n + 1) * BLK], ps[:, 6 + s, :], ACT.Square)\
                                    .then_inc(s_sq, 1)

                        def take_v(g, v, n):
                            act.wait_ge(s_v, g * 2 + n + 1)
                            dst = vp_[:, v, 4 * n:4 * n + 4, :, :].rearrange("p t h d -> p (t h d)")
                            nc.scalar.activation(dst, ps[:, 4:6, :].rearrange("p b w -> p (b w)"), ACT.Identity)\
                                .then_inc(s_vp, 1)

                        def roots(g):
                            act.wait_ge(s_n2, g + 1)
                            nc.scalar.activation(nrm[:].rearrange("p s w -> p (s w)"),
                                                 ps[:, 4:8, :].rearrange("p b w -> p (b w)"), ACT.Sqrt).then_inc(s_nrm, 1)

                        def exps(g, n, v, b):
                            act.wait_ge(s_scale, g + 1)
                            for k in range(8):
                                t, s, pr = k // 4, k // 2 % 2, k % 2
                                act.wait_ge(s_s, n * 8 + k + 1)
                                for j in range(2):
                                    col = (s * 8 + 2 * b + t) * HS + 2 * pr + j
                                    ins = nc.scalar.activation(ee[:, b % 2, t, s * HS + 2 * pr + j, :],
                                                               ps[:, k % 2, j * S:(j + 1) * S], ACT.Exp,
                                                               scale=scale_[:, v, col:col + 1])
                                ins.then_inc(s_exp, 1)

                        def take_c(n, first=False):
                            act.wait_ge(s_ct, n + 1)
                            if not first:
                                act.wait_ge(s_g, n * 8)
                            nc.scalar.activation(ct[:].rearrange("p a w -> p (a w)"),
                                                 ctb.rearrange("p a w -> p (a w)"), ACT.Identity).then_inc(s_cts, 1)

                        def take_windows(n):
                            act.wait_ge(s_mt, n + 1)
                            nc.scalar.activation(mt[:], ps[:, 2, 0:S], ACT.Identity).then_inc(s_mts, 1)

                        def take_w(n):
                            act.wait_ge(s_sel, n + 1)
                            for e in range(2):
                                nc.scalar.activation(wd[:, :, e, :], ps[0:W3, 0:2, :].rearrange("p b (a w) -> p (b a) w", w=S),
                                                     ACT.Identity, scale=C("pair_rows")[0:W3, e:e + 1]).then_inc(s_wd, 1)

                        def take_o(n):
                            act.wait_ge(s_o, n + 1)
                            nc.scalar.activation(ot[:], ps[:, 3, 0:S], ACT.Identity).then_inc(s_ot, 1)

                        def body(g, u, more, front):
                            v = 1 - u
                            for b in range(GB):
                                n = g * GB + b
                                take_w(n)
                                if front and b == 3:
                                    front_in(g + 2)
                                if b < 3:
                                    take_c(n + 1)
                                take_o(n)
                                if b < 3:
                                    take_windows(n + 1)
                                if b < 2:
                                    exps(g, n + 2, u, b + 2)
                                elif more:
                                    exps(g + 1, n + 2, v, b - 2)
                                if front and b == 3:
                                    for i in range(2):
                                        take_q(g + 2, u, i)
                                        take_v(g + 2, u, i)
                                if more and b == 3:
                                    take_c(n + 1)
                                if front and b == 3:
                                    roots(g + 2)
                                if more and b == 3:
                                    take_windows(n + 1)

                        front_in(0)
                        for n in range(2):
                            take_q(0, 0, n)
                            take_v(0, 0, n)
                        roots(0)
                        exps(0, 0, 0, 0)
                        exps(0, 1, 0, 1)
                        front_in(1)
                        for n in range(2):
                            take_q(1, 1, n)
                            take_v(1, 1, n)
                        take_c(0, first=True)
                        roots(1)
                        take_windows(0)
                        bodies(act, body)

                    @block.gpsimd
                    def _(pool):
                        def place_q(g, v, n, b, first=False):
                            if not first:
                                pool.wait_ge(s_s, (n - 2) * 8 + 8)
                                pool.sem_inc(s_hold, 1)
                            pool.wait_ge(s_qk, g * 2 + 2)
                            pool.sem_inc(s_hold, 1)
                            for s in range(NS):
                                src = qk_[:, v, s, b * S:(b + 1) * S].unsqueeze(1).broadcast_to((P, HS, S))
                                nc.gpsimd.tensor_tensor(qd[:, b % 2, s, :, :], src,
                                                        C("head_rows").unsqueeze(2).broadcast_to((P, HS, S)), ALU.mult)\
                                    .then_inc(s_qd, 1)

                        def index_hits(g, tiles):
                            for t in tiles:
                                pool.wait_ge(s_hit, g * 8 + t + 1)
                                pool.sem_inc(s_hold, 1)
                                nc.gpsimd.tensor_tensor(hit_[t % 2], hit_[t % 2], fk[:].unsqueeze(1)
                                                        .broadcast_to((P, H * NHASH, NK)), ALU.mult).then_inc(s_hm, 1)

                        def place_c(g, u, n, b, first=False):
                            if b == 0:
                                pool.wait_ge(s_c, g + 1)
                                pool.sem_inc(s_hold, 1)
                            if not first:
                                pool.wait_ge(s_d, n - 1)
                                pool.sem_inc(s_hold, 1)
                            src = cn_[:, u, :, b, :].rearrange("p t (j e d) -> p t j e d", e=2, d=16)
                            dst = cp[:, b % 2].rearrange("p t (j e) w -> p t j e w", e=2)
                            for e in range(2):
                                nc.gpsimd.tensor_copy(dst[:, :, :, e, 16 * e:16 * e + 16], src[:, :, :, e, :]).then_inc(s_cp, 1)

                        def body(g, u, more, front):
                            v = 1 - u
                            for b in range(GB):
                                n = g * GB + b
                                if b < 2:
                                    place_q(g, u, n + 2, b + 2)
                                    place_c(g, u, n + 2, b + 2)
                                elif more:
                                    place_q(g + 1, v, n + 2, b - 2)
                                if more and b < 3:
                                    index_hits(g + 1, HITS[b][0] + HITS[b][1])
                                if more and b == 3:
                                    place_c(g + 1, v, n + 1, 0)
                                    place_c(g + 1, v, n + 2, 1)
                                if front and b == 3:
                                    index_hits(g + 2, (0,))

                        pool.wait_ge(s_zero, 4)
                        pool.wait_ge(s_w, 3)
                        place_q(0, 0, 0, 0, first=True)
                        place_q(0, 0, 1, 1, first=True)
                        index_hits(0, range(8))
                        place_c(0, 0, 0, 0, first=True)
                        place_c(0, 0, 1, 1, first=True)
                        index_hits(1, (0,))
                        bodies(pool, body)

        attention()
        feed_forward(1)
        rstd_phase(LN_EPS, gru=True)

        XW = P + 2 * E
        rows_dram = nc.dram_tensor("expert_rows", [T, XW], F32, kind="Internal").ap()
        y_dram = nc.dram_tensor("expert_out", [2 * T + E * SLOTS * P, P], F32, kind="Internal").ap()

        def recurrence():
            with ExitStack() as ph:
                def psb(name, shape, dt=F32):
                    return sb("re_" + name, shape, dt, ph)

                def psem(name):
                    return sem("re_" + name, ph)

                xh, lt = psb("xh", [P, 2, BLK]), psb("lt", [P, 2, BLK])
                wgh = psb("wgh", [P, 2 * P])
                rr = psb("rr", [P, 3, NT])
                gate = psb("gate", [P, 2, 4, BLK])
                ZW = 2048
                zero = psb("zero", [P, ZW])
                ZC = 2 * T // ZW
                s_yz = psem("y_zeroed")
                g_, st = psb("g", [P, 2, BLK]), psb("state", [P, 2, BLK])
                s_w, s_rr = psem("weights"), psem("factors")
                s_xh, s_tp, s_lt, s_gh, s_sig, s_st, s_bk, s_c, s_h, s_hold = (
                    psem(n) for n in ("normed", "turned", "lt", "gates", "sigmoids", "states", "back", "chain",
                                      "h_plus_norm", "hold"))
                K = 2
                def factors(dve):
                    link = Chain(dve, s_rr)
                    link(nc.vector.memset(zero[:], 0.0))
                    link(nc.vector.tensor_tensor(rr[:, 0, :], rstd[:], gru_r[:], ALU.mult))
                    link(nc.vector.tensor_scalar(rr[:, 1, :], rstd[:], 1.0, None, ALU.add))
                    link(nc.vector.scalar_tensor_tensor(out=rr[:, 2, :], in0=mean[:], scalar=-1.0, in1=rstd[:],
                                                        op0=ALU.mult, op1=ALU.mult))

                with nc.Block() as block:
                    @block.sync
                    def _(sp):
                        sp.dma_start(wgh[:], a["W_gh"]).then_inc(s_w, 16)
                        sp.wait_ge(s_rr, 1)
                        for n in range(ZC):
                            sp.dma_start(y_dram[n * ZW:(n + 1) * ZW, :].rearrange("(p r) w -> p (r w)", p=P),
                                         zero[:]).then_inc(s_yz, 16)
                        sp.wait_ge(s_yz, ZC * 16)

                    @block.vector
                    def _(dve):
                        def norm(i, u):
                            for t in range(4):
                                ins = nc.vector.tensor_scalar(
                                    xh[:, u, t * P:(t + 1) * P], x2[:, bass.ds(i * BLK + t * P, P)],
                                    mean[:, bass.ds(i * 4 + t, 1)], rr[:, 0, bass.ds(i * 4 + t, 1)],
                                    ALU.subtract, ALU.mult)
                            ins.then_inc(s_xh, 1)

                        def mix(i, u):
                            link = Chain(dve, s_c, i * K)
                            dve.wait_ge(s_sig, i * 4 + 4)
                            link(nc.vector.scalar_tensor_tensor(out=g_[:, u], in0=gate[:, u, 2, :], scalar=0.5,
                                                                in1=gate[:, u, 3, :], op0=ALU.min, op1=ALU.add))
                            link(nc.vector.tensor_tensor(g_[:, u], g_[:, u], gate[:, u, 0, :], ALU.mult))
                            for t in range(2):
                                w = slice(t * S, (t + 1) * S)
                                nc.vector.tensor_tensor_scan(st[:, u, w], gate[:, u, 1, w], g_[:, u, w], 0.0, ALU.mult, ALU.add)\
                                    .then_inc(s_st, 1)
                            assert link.n == K

                        def residual(i, u):
                            dve.wait_ge(s_h, i * 2 + 2)
                            dve.wait_ge(s_bk, i + 1)
                            x2b = x2[:, bass.ds(i * BLK, BLK)]
                            nc.vector.tensor_tensor(x2b, ps[:, 6 + u, :], x2b, ALU.add).then_inc(s_rr, 1)
                            dve.wait_ge(s_rr, 4 + i + 1)
                            for t in range(4):
                                nc.vector.bn_stats(stats[:, bass.ds(i * 4 + t, 1), :].rearrange("p a b -> p (a b)"),
                                                   x2[:, bass.ds(i * BLK + t * P, P)])

                        def body(i, u):
                            if not isinstance(i, int) or i + 2 < NBLK:
                                dve.wait_ge(s_tp, i + 1)
                                norm(i + 2, u)
                            mix(i, u)
                            residual(i - 1, 1 - u)

                        factors(dve)
                        norm(0, 0)
                        norm(1, 1)
                        dve.wait_ge(s_tp, 1)
                        norm(2, 0)
                        mix(0, 0)
                        with dve.Fori(0, NBLK // 2 - 2) as k:
                            body(k * 2 + 1, 1)
                            body(k * 2 + 2, 0)
                        for i in range(NBLK - 3, NBLK):
                            body(i, i % 2)
                        residual(NBLK - 1, 1)

                    @block.gpsimd
                    def _(pool):
                        with pool.Fori(0, NBLK) as i:
                            pool.wait_ge(s_xh, i + 1)
                            pool.sem_inc(s_hold, 1)
                            h = x2[:, bass.ds(i * BLK, BLK)].rearrange("p (t d) -> p t d", t=4)
                            for row, op in ((1, ALU.mult), (2, ALU.add)):
                                by_tile = rr[:, row, bass.ds(i * 4, 4)].unsqueeze(2).broadcast_to((P, 4, P))
                                ins = nc.gpsimd.tensor_tensor(h, h, by_tile, op)
                                ins.then_inc(s_h, 1)
                                if row == 1:
                                    pool.wait_ge(s_h, i * 2 + 1)
                                    pool.sem_inc(s_hold, 1)

                    @block.tensor
                    def _(pe):
                        def turn(i, u):
                            pe.wait_ge(s_xh, i + 1)
                            for t in range(4):
                                ins = nc.tensor.transpose(ps[:, u, t * P:(t + 1) * P], xh[:, u, t * P:(t + 1) * P], ident)
                            ins.then_inc(s_tp, 1)

                        def gates(i, u):
                            pe.wait_ge(s_lt, i + 1)
                            for c in range(2):
                                ins = nc.tensor.matmul(ps[:, 2 + 2 * u + c, :], wgh[:, c * P:(c + 1) * P], lt[:, u, :],
                                                       start=True, stop=True)
                            ins.then_inc(s_gh, 1)

                        def back(i, u):
                            pe.wait_ge(s_st, i * 2 + 2)
                            for t in range(4):
                                ins = nc.tensor.transpose(ps[:, 6 + u, t * P:(t + 1) * P], st[:, u, t * P:(t + 1) * P], ident)
                            ins.then_inc(s_bk, 1)

                        pe.wait_ge(s_w, 16)
                        turn(0, 0)
                        gates(0, 0)
                        turn(1, 1)
                        with pe.Fori(0, NBLK // 2 - 1) as k:
                            for u in range(2):
                                gates(k * 2 + u + 1, 1 - u)
                                turn(k * 2 + u + 2, u)
                                back(k * 2 + u, u)
                        gates(NBLK - 1, 1)
                        back(NBLK - 2, 0)
                        back(NBLK - 1, 1)

                    @block.scalar
                    def _(act):
                        nc.scalar.preload_act_table(ACT.Sigmoid)

                        def evac(i, u):
                            act.wait_ge(s_tp, i + 1)
                            nc.scalar.activation(lt[:, u, :], ps[:, u, :], ACT.Identity, scale=lncol[:, 6:7],
                                                 bias=lncol[:, 7:8]).then_inc(s_lt, 1)

                        def sigmoids(i, u):
                            act.wait_ge(s_gh, i + 1)
                            for c, (bank, scale, f) in enumerate(((0, 1.0, ACT.Sigmoid), (0, -1.0, ACT.Sigmoid),
                                                                  (1, 1.0, ACT.Sigmoid), (1, 1.0, ACT.Relu))):
                                nc.scalar.activation(gate[:, u, c, :], ps[:, 2 + 2 * u + bank, :], f, scale=scale)\
                                    .then_inc(s_sig, 1)

                        evac(0, 0)
                        evac(1, 1)
                        sigmoids(0, 0)
                        with act.Fori(0, NBLK // 2 - 1) as k:
                            for u in range(2):
                                evac(k * 2 + u + 2, u)
                                sigmoids(k * 2 + u + 1, 1 - u)
                        sigmoids(NBLK - 1, 1)

        recurrence()
        rstd_phase(LN_EPS)

        TE = NT * E
        gather_i = sb("gather_i", [P, E, SLOTS], I32)
        valid = sb("valid", [P, E, SLOTS])
        spare = sb("spare", [P, E, SLOTS])

        def routing():
            with ExitStack() as ph:
                def psb(name, shape, dt=F32):
                    return sb("ro_" + name, shape, dt, ph)

                def psem(name):
                    return sem("ro_" + name, ph)

                xh, lt = psb("xh", [P, 4, BLK]), psb("lt", [P, 2, BLK])
                gw, gb = psb("gw", [P, E]), psb("gb", [P, E])
                ones_t = psb("ones_t", [P, NT])
                BITS = 2
                CANDS = 2 ** BITS - 1
                bits = psb("bits", [P, 30 // BITS * CANDS], I32)
                probs, oh1, oh2, aa, bb, wt = (psb(f"n8_{i}", [P, NT, E]) for i in range(6))
                n1 = psb("n1", [P, NT])
                wdest = psb("wdest", [P, NT, 2, E])
                thr, cand = psb("thr", [P, 1], I32), psb("cand", [P, CANDS], I32)
                take = psb("take", [P, CANDS], I32)
                count = psb("count", [P, CANDS])
                above = psb("above", [P, CANDS, TE], BF16)
                thr8, room = psb("thr8", [P, E]), psb("room", [P, E])
                pos_i = psb("pos_i", [P, NT, E], I32)
                iota_b = psb("iota_b", [P, P], BF16)
                neg_lo, one = psb("neg_lo", [P, TE]), psb("one", [P, 1])
                tile_b = psb("tile_b", [P, NT, E], BF16)
                tile_te = tile_b[:].rearrange("p t e -> p (t e)")
                is_hi = psb("is_hi", [P, TE, SLOTS], BF16)
                pay = psb("pay", [P, TE, 2, SLOTS], BF16)
                NO = 4
                oh_lo = psb("oh_lo", [P, NO, E, P], BF16)
                slot = psb("slot", [P, E, 2 * SLOTS])
                s_w, s_z, s_xh, s_tp, s_lt, s_lg, s_lo, s_c, s_row = (
                    psem(n) for n in ("weights", "zero", "normed", "turned", "lt", "logits", "logits_out", "chain",
                                      "rows_stored"))
                NB = 4
                s_st = [psem(f"stored{u}") for u in range(NB)]
                with nc.Block() as block:
                    @block.vector
                    def _(dve):
                        def norm(i, v, k):
                            dve.wait_ge(s_st[v], k * 16 + 16)
                            for t in range(4):
                                ins = nc.vector.tensor_scalar(
                                    xh[:, v, t * P:(t + 1) * P], x2[:, bass.ds(i * BLK + t * P, P)],
                                    mean[:, bass.ds(i * 4 + t, 1)], rstd[:, bass.ds(i * 4 + t, 1)],
                                    ALU.subtract, ALU.mult)
                            ins.then_inc(s_xh, 1)

                        def logits(i, u):
                            dve.wait_ge(s_lg, i + 1)
                            dst = probs[:, bass.ds(i * 4, 4), :]
                            src = ps[:, 2 + u, 0:4 * E].rearrange("p (t e) -> p t e", e=E)
                            nc.vector.tensor_tensor(dst, src, gb[:].unsqueeze(1).broadcast_to((P, 4, E)), ALU.add)\
                                .then_inc(s_lo, 1)

                        norm(0, 0, 0)
                        norm(1, 1, 0)
                        dve.wait_ge(s_w, 48)
                        with dve.Fori(0, NBLK // NB - 1) as k:
                            for v in range(NB):
                                norm(k * NB + v + 2, (v + 2) % NB, k + (v + 2) // NB)
                                logits(k * NB + v, v % 2)
                        for v in range(NB):
                            if v < 2:
                                norm(NBLK - NB + v + 2, v + 2, NBLK // NB - 1)
                            logits(NBLK - NB + v, v % 2)

                    @block.tensor
                    def _(pe):
                        def turn(i, v):
                            pe.wait_ge(s_xh, i + 1)
                            for t in range(4):
                                ins = nc.tensor.transpose(ps[:, v % 2, t * P:(t + 1) * P], xh[:, v, t * P:(t + 1) * P], ident)
                            ins.then_inc(s_tp, 1)

                        def gate(i, u):
                            pe.wait_ge(s_lt, i + 1)
                            pe.wait_ge(s_lo, i + 1)
                            for t in range(4):
                                ins = nc.tensor.matmul(ps[:, 2 + u, t * E:(t + 1) * E], lt[:, u, t * P:(t + 1) * P], gw[:],
                                                       start=True, stop=True)
                            ins.then_inc(s_lg, 1)

                        pe.wait_ge(s_w, 48)
                        pe.sem_inc(s_lo, 2)
                        turn(0, 0)
                        with pe.Fori(0, NBLK // NB - 1) as k:
                            for v in range(NB):
                                turn(k * NB + v + 1, (v + 1) % NB)
                                gate(k * NB + v, v % 2)
                        for v in range(NB):
                            if v < NB - 1:
                                turn(NBLK - NB + v + 1, v + 1)
                            gate(NBLK - NB + v, v % 2)

                    @block.scalar
                    def _(act):
                        with act.Fori(0, NBLK // 2) as k:
                            for u in range(2):
                                act.wait_ge(s_tp, k * 2 + u + 1)
                                nc.scalar.activation(lt[:, u, :], ps[:, u, :], ACT.Identity).then_inc(s_lt, 1)

                    @block.sync
                    def _(sp):
                        rows_v = rows_dram.rearrange("(i t p) w -> i p t w", t=4, p=P)
                        for v in range(NB):
                            sp.sem_inc(s_st[v], 16)
                        sp.dma_start(gw[:], a["gate_wT"]).then_inc(s_w, 16)
                        sp.dma_start(gb[:], a["gate_b"]).then_inc(s_w, 16)
                        sp.dma_start(bits[:], a["bits"]).then_inc(s_w, 16)
                        with sp.Fori(0, NBLK // NB) as k:
                            for v in range(NB):
                                i = k * NB + v
                                sp.wait_ge(s_xh, i + 1)
                                sp.sem_inc(s_z, 1)
                                sp.dma_start(rows_v[bass.ds(i, 1), :, :, 0:P].rearrange("i p t w -> (i p) t w"),
                                             xh[:, v, :].rearrange("p (t w) -> p t w", t=4)).then_inc(s_st[v], 16)
                        for v in range(NB):
                            sp.wait_ge(s_st[v], NBLK // NB * 16 + 16)

                def per_tile(v):
                    return v.unsqueeze(2).broadcast_to((P, NT, E))

                def per_expert(v):
                    return v.unsqueeze(1).broadcast_to((P, NT, E))

                s_sc, s_t, s_thr = psem("for_scalar"), psem("turned2"), psem("thr")
                with nc.Block() as block:
                    @block.vector
                    def _(dve):
                        link = Chain(dve, s_c)
                        link(nc.vector.tensor_reduce(n1[:], probs[:], AX.X, ALU.max))
                        nc.vector.tensor_tensor(probs[:], probs[:], per_tile(n1[:]), ALU.subtract).then_inc(s_sc, 1)
                        dve.wait_ge(s_sc, 2)
                        link(nc.vector.tensor_reduce(n1[:], probs[:], AX.X, ALU.add))
                        link(nc.vector.reciprocal(n1[:], n1[:]))
                        link(nc.vector.tensor_tensor(probs[:], probs[:], per_tile(n1[:]), ALU.mult))
                        last = C("last")
                        for src, oh in ((probs, oh1), (bb, oh2)):
                            link(nc.vector.tensor_reduce(n1[:], src[:], AX.X, ALU.max))
                            link(nc.vector.tensor_tensor(aa[:], src[:], per_tile(n1[:]), ALU.is_equal))
                            link(nc.vector.tensor_tensor(aa[:], aa[:], per_expert(last), ALU.mult))
                            link(nc.vector.tensor_reduce(n1[:], aa[:], AX.X, ALU.max))
                            link(nc.vector.tensor_tensor(oh[:], per_expert(last), per_tile(n1[:]), ALU.is_equal))
                            if oh is oh1:
                                link(nc.vector.scalar_tensor_tensor(out=bb[:], in0=oh[:], scalar=-2.0, in1=probs[:],
                                                                    op0=ALU.mult, op1=ALU.add))
                        link(nc.vector.tensor_tensor(aa[:], oh1[:], oh2[:], ALU.add))
                        link(nc.vector.tensor_tensor(wt[:], aa[:], probs[:], ALU.mult))
                        link(nc.vector.tensor_copy(wdest[:, :, 0, :], wt[:]))
                        link(nc.vector.scalar_tensor_tensor(out=wdest[:, :, 1, :], in0=oh2[:], scalar=float(T),
                                                            in1=per_tile(C("token")), op0=ALU.mult, op1=ALU.add))
                        nc.vector.tensor_copy(iota_b[:], C("iota")).then_inc(s_sc, 1)

                    @block.scalar
                    def _(act):
                        act.wait_ge(s_sc, 1)
                        nc.scalar.activation(probs[:], probs[:], ACT.Exp).then_inc(s_sc, 1)

                    @block.tensor
                    def _(pe):
                        pe.wait_ge(s_sc, 3)
                        for n in range(4):
                            ins = nc.tensor.transpose(ps[:, 0, n * P:(n + 1) * P],
                                                      wt[:, n * 16:(n + 1) * 16, :].rearrange("p t e -> p (t e)"), ident)

                K = 3 + CANDS
                weights = aa[:].rearrange("p t e -> p (t e)")
                flags = bb[:].rearrange("p t e -> p (t e)")
                with nc.Block() as block:
                    @block.sync
                    def _(sp):
                        sp.dma_start(rows_dram.rearrange("(t p) w -> p t w", p=P)[:, :, P:XW],
                                     wdest[:].rearrange("p t k e -> p t (k e)")).then_inc(s_row, 16)
                        sp.wait_ge(s_row, 16)

                    @block.vector
                    def _(dve):
                        link = Chain(dve, s_t)
                        link(nc.vector.tensor_copy(weights, ps[:, 0, :]))
                        link(nc.vector.memset(thr[:], 0))
                        with dve.Fori(0, 30 // BITS) as i:
                            link = Chain(dve, s_t, i * K + 2)
                            link(nc.vector.tensor_tensor(cand[:], thr[:].broadcast_to((P, CANDS)),
                                                         bits[:, bass.ds(i * CANDS, CANDS)], ALU.bitwise_or))
                            for c in range(CANDS):
                                ins = nc.vector.tensor_scalar(above[:, c, :], weights, cand[:, c:c + 1].bitcast(F32), None,
                                                              ALU.is_ge, ALU.add, accum_out=count[:, c:c + 1])
                            link(ins)
                            dve.wait_ge(s_thr, i + 1)
                            link(nc.vector.tensor_scalar(take[:], ps[:, 1, 0:CANDS], float(CAP), -1.0, ALU.is_ge, ALU.mult))
                            for c in range(CANDS):
                                dve.sem_inc(s_z, 1)
                                link(nc.vector.copy_predicated(thr[:], take[:, c:c + 1], cand[:, c:c + 1]))
                            assert link.n == K

                    @block.tensor
                    def _(pe):
                        with pe.Fori(0, 30 // BITS) as i:
                            pe.wait_ge(s_t, i * K + 2 + 2)
                            nc.tensor.matmul(ps[:, 1, 0:CANDS], C("same_expert"), count[:], start=True, stop=True)\
                                .then_inc(s_thr, 1)

                s_p, s_q, s_pos = psem("prefix_in"), psem("prefix_out"), psem("pos")
                sel, incl, rank = oh1, oh2, probs
                ones_row = ones_t[:]
                hi, lo = aa, bb
                with nc.Block() as block:
                    @block.vector
                    def _(dve):
                        link = Chain(dve, s_pos)
                        link(nc.vector.memset(ones_row, 1.0))
                        link(nc.vector.tensor_scalar(n1[:], C("token"), C("partition"), 1.0 / P, ALU.subtract, ALU.mult))
                        link(nc.vector.tensor_copy(tile_b[:], per_tile(n1[:])))
                        nc.vector.tensor_scalar(flags[:, 0:P], C("ones"), thr[:].bitcast(F32), None, ALU.mult)\
                            .then_inc(s_p, 1)
                        dve.wait_ge(s_q, 1)
                        link(nc.vector.tensor_copy(thr8[:], ps[:, 0, 0:E]))
                        link(nc.vector.tensor_tensor(sel[:], wt[:], per_expert(thr8[:]), ALU.is_gt))
                        link(nc.vector.tensor_tensor(bb[:], wt[:], per_expert(thr8[:]), ALU.is_equal))
                        nc.vector.scalar_tensor_tensor(out=aa[:], in0=wt[:], scalar=0.0, in1=bb[:],
                                                       op0=ALU.is_gt, op1=ALU.mult).then_inc(s_p, 1)

                        def ranks():
                            tot = ps[:, 2, :].rearrange("p (t e) -> p t e", e=E)
                            for e in range(E):
                                link(nc.vector.tensor_tensor_scan(incl[:, :, e], ones_row, tot[:, :, e], 0.0, ALU.mult,
                                                                  ALU.add))
                            link(nc.vector.tensor_tensor(incl[:], incl[:], tot, ALU.subtract))
                            link(nc.vector.tensor_tensor(rank[:], incl[:], ps[:, 1, :].rearrange("p (t e) -> p t e", e=E),
                                                         ALU.add))

                        dve.wait_ge(s_q, 2)
                        ranks()
                        link(nc.vector.tensor_reduce(room[:], ps[:, 3, :].rearrange("p (t e) -> p e t", e=E), AX.X, ALU.add))
                        link(nc.vector.tensor_scalar(room[:], room[:], -1.0, float(CAP), ALU.mult, ALU.add))
                        link(nc.vector.tensor_tensor(rank[:], rank[:], per_expert(room[:]), ALU.is_lt))
                        link(nc.vector.tensor_tensor(rank[:], rank[:], aa[:], ALU.mult))
                        nc.vector.tensor_tensor(sel[:], sel[:], rank[:], ALU.add).then_inc(s_p, 1)
                        dve.wait_ge(s_q, 3)
                        ranks()
                        link(nc.vector.tensor_copy(pos_i[:], rank[:]))
                        link(nc.vector.tensor_single_scalar(pos_i[:], pos_i[:], 7, ALU.logical_shift_right))
                        link(nc.vector.tensor_copy(hi[:], pos_i[:]))
                        link(nc.vector.scalar_tensor_tensor(out=lo[:], in0=hi[:], scalar=-float(P), in1=rank[:],
                                                            op0=ALU.mult, op1=ALU.add))
                        link(nc.vector.scalar_tensor_tensor(out=lo[:], in0=lo[:], scalar=1.0, in1=sel[:],
                                                            op0=ALU.add, op1=ALU.mult))
                        link(nc.vector.tensor_scalar(lo[:], lo[:], -1.0, None, ALU.add))
                        link(nc.vector.tensor_scalar(neg_lo[:], lo[:].rearrange("p t e -> p (t e)"), -1.0, None, ALU.mult))
                        link(nc.vector.memset(one[:], 1.0))
                        link(nc.vector.tensor_scalar(n1[:, 0:1], C("partition"), 1.0, None, ALU.add))
                        link(nc.vector.tensor_tensor(is_hi[:], C("iota")[:, 0:SLOTS].unsqueeze(1)
                                                     .broadcast_to((P, TE, SLOTS)),
                                                     hi[:].rearrange("p t e -> p (t e)").unsqueeze(2)
                                                     .broadcast_to((P, TE, SLOTS)), ALU.is_equal))
                        dve.sem_inc(s_sc, 1)
                        nc.vector.tensor_tensor(pay[:, :, 1, :], is_hi[:], tile_te.unsqueeze(2)
                                                .broadcast_to((P, TE, SLOTS)), ALU.mult)

                    @block.scalar
                    def _(act):
                        act.wait_ge(s_sc, 4)
                        nc.scalar.activation(pay[:, :, 0, :], is_hi[:], ACT.Identity, scale=n1[:, 0:1])

                    @block.tensor
                    def _(pe):
                        pe.wait_ge(s_p, 1)
                        nc.tensor.transpose(ps[:, 0, 0:P], flags[:, 0:P], ident).then_inc(s_q, 1)
                        pe.wait_ge(s_p, 2)
                        tied, over = aa[:].rearrange("p t e -> p (t e)"), sel[:].rearrange("p t e -> p (t e)")
                        nc.tensor.matmul(ps[:, 1, :], C("before"), tied, start=True, stop=True)
                        nc.tensor.matmul(ps[:, 2, :], C("ones"), tied, start=True, stop=True)
                        nc.tensor.matmul(ps[:, 3, :], C("ones"), over, start=True, stop=True).then_inc(s_q, 1)
                        pe.wait_ge(s_p, 3)
                        nc.tensor.matmul(ps[:, 1, :], C("before"), over, start=True, stop=True)
                        nc.tensor.matmul(ps[:, 2, :], C("ones"), over, start=True, stop=True).then_inc(s_q, 1)

                s_oh, s_li = psem("onehot"), psem("list")
                lo_f = lo[:].rearrange("p t e -> p (t e)")
                EV = E - 1
                apart = psb("apart", [P, NO, P])
                s_oa, s_ap = psem("onehot_act"), psem("apart_ready")
                s_lh = psem("list_hold")
                with nc.Block() as block:
                    @block.vector
                    def _(dve):
                        with dve.Fori(0, NT // NO) as k:
                            for u in range(NO):
                                dve.wait_ge(s_li, k * NO + u + 1)
                                lo_t = lo_f[:, bass.ds((k * NO + u) * E, EV)]
                                nc.vector.tensor_tensor(oh_lo[:, u, 0:EV, :],
                                                        iota_b[:].unsqueeze(1).broadcast_to((P, EV, P)),
                                                        lo_t.unsqueeze(2).broadcast_to((P, EV, P)), ALU.is_equal)\
                                    .then_inc(s_oh, 1)

                    @block.scalar
                    def _(act):
                        with act.Fori(0, NT // NO) as k:
                            for u in range(NO):
                                tile = k * NO + u
                                act.wait_ge(s_li, tile + 1)
                                act.sem_inc(s_lh, 1)
                                nc.scalar.activation(apart[:, u, :], iota_b[:], ACT.Abs,
                                                     bias=neg_lo[:, bass.ds(tile * E + EV, 1)]).then_inc(s_ap, 1)
                                act.wait_ge(s_ap, tile + 1)
                                nc.scalar.activation(oh_lo[:, u, EV, :], apart[:, u, :], ACT.Relu, scale=-1.0,
                                                     bias=one[:]).then_inc(s_oa, 1)

                    @block.tensor
                    def _(pe):
                        def collect(tile, u, start=False, stop=False):
                            pe.wait_ge(s_oh, tile + 1)
                            for e in range(E):
                                if e == EV:
                                    pe.wait_ge(s_oa, tile + 1)
                                rhs = pay[:, bass.ds(tile * E + e, 1), :, :].rearrange("p x k s -> p (x k s)")
                                ins = nc.tensor.matmul(ps[:, e, 0:2 * SLOTS], oh_lo[:, u, e, :], rhs, start=start, stop=stop)
                            ins.then_inc(s_li, 1)

                        pe.sem_inc(s_li, NO)
                        for u in range(NO):
                            collect(u, u, start=(u == 0))
                        with pe.Fori(1, NT // NO - 1) as k:
                            for u in range(NO):
                                collect(k * NO + u, u)
                        for u in range(NO):
                            collect(NT - NO + u, u, stop=(u == NO - 1))

                s_f = psem("final")
                with nc.Block() as block:
                    @block.vector
                    def _(dve):
                        link = Chain(dve, s_f)
                        link(nc.vector.tensor_copy(slot[:], ps[:, :, 0:2 * SLOTS]))
                        first, tile = slot[:, :, 0:SLOTS], slot[:, :, SLOTS:2 * SLOTS]
                        link(nc.vector.tensor_scalar(valid[:], first, 0.5, None, ALU.is_gt))
                        link(nc.vector.scalar_tensor_tensor(out=tile, in0=tile, scalar=float(P), in1=first,
                                                            op0=ALU.mult, op1=ALU.add))
                        link(nc.vector.tensor_scalar(gather_i[:], tile, -1.0, 0.0, ALU.add, ALU.max))
                        link(nc.vector.tensor_scalar(spare[:], valid[:], -1.0, 1.0, ALU.mult, ALU.add))
                        link(nc.vector.tensor_tensor(spare[:].rearrange("p e s -> p (e s)"),
                                                     spare[:].rearrange("p e s -> p (e s)"), C("spare_row"), ALU.mult))

        routing()

        def experts():
            with ExitStack() as ph:
                def psb(name, shape, dt=F32):
                    return sb("ex_" + name, shape, dt, ph)

                def psem(name):
                    return sem("ex_" + name, ph)

                NB2 = SLOTS // 2
                NBUF = 5
                BL = E * NB2
                we1, we2 = psb("we1", [P, 2, HID]), psb("we2", [P, 2, EC, P])
                be = psb("be", [P, E * EC])
                be2 = psb("be2", [P, E, P])
                bs = psb("bs", [P, 2, EC])
                xg = psb("xg", [P, NBUF, 2, XW])
                xt = psb("xt", [P, 2, S])
                ht = psb("ht", [P, 2, EC, S])
                yw = psb("yw", [P, NBUF, 2, P])
                ycol = psb("ycol", [P, NBUF, 2])
                scat = psb("scat", [P, NBUF, 2], I32)
                s_b, s_tp, s_xt, s_h, s_ht, s_y, s_ys, s_c, s_bs = (
                    psem(n) for n in ("biases", "turned", "xt", "hidden", "gelu", "y", "y_ready", "chain", "bias_ready"))
                s_w = [psem(f"weights{u}") for u in range(2)]
                s_xg = [psem(f"gathered{u}") for u in range(NBUF)]
                s_sc = [psem(f"scattered{u}") for u in range(NBUF)]
                s_hold = psem("hold")

                with nc.Block() as block:
                    @block.sync
                    def _(sp):
                        def load(e, u):
                            sp.dma_start(we1[:, u, :], a["ew1"][bass.ds(e, 1), :, :].rearrange("e p f -> (e p) f"))\
                                .then_inc(s_w[u], 16)
                            sp.dma_start(we2[:, u, :, :], a["ew2"][bass.ds(e, 1), :, :]
                                         .rearrange("e (c p) d -> (e p) c d", p=P)).then_inc(s_w[u], 16)

                        sp.dma_start(be[:], a["eb1"]).then_inc(s_b, 16)
                        sp.dma_start(be2[:], a["eb2"]).then_inc(s_b, 16)
                        for u in range(2):
                            load(u, u)
                        with sp.Fori(1, E // 2) as k:
                            for u in range(2):
                                sp.wait_ge(s_y, (k * 2 + u - 1) * NB2)
                                sp.sem_inc(s_hold, 1)
                                load(k * 2 + u, u)

                    @block.gpsimd
                    def _(pool):
                        for n in range(BL + 4):
                            if n < BL:
                                if n >= NBUF:
                                    pool.wait_ge(s_ys, n - NBUF + 1)
                                for t in range(2):
                                    nc.gpsimd.indirect_dma_start(
                                        out=xg[:, n % NBUF, t, :], out_offset=None, in_=rows_dram,
                                        in_offset=bass.IndirectOffsetOnAxis(
                                            ap=gather_i[:, n // NB2, n % NB2 * 2 + t:n % NB2 * 2 + t + 1], axis=0),
                                    ).then_inc(s_xg[n % NBUF], 16)
                            m = n - 4
                            if m >= 0:
                                pool.wait_ge(s_ys, m + 1)
                                for t in range(2):
                                    nc.gpsimd.indirect_dma_start(
                                        out=y_dram, in_=yw[:, m % NBUF, t, :], in_offset=None,
                                        out_offset=bass.IndirectOffsetOnAxis(ap=scat[:, m % NBUF, t:t + 1], axis=0),
                                    ).then_inc(s_sc[m % NBUF], 16)
                        for u in range(NBUF):
                            pool.wait_ge(s_sc[u], 32 * (BL // NBUF))

                    @block.vector
                    def _(dve):
                        def evac(n, j):
                            dve.wait_ge(s_tp, n + 1)
                            nc.vector.tensor_copy(xt[:, j % 2, :], ps[:, j % 2, 0:S]).then_inc(s_xt, 1)

                        def weigh(k, j, first):
                            n, e, buf, s = k * 2 * NB2 + j, k * 2 + j // NB2, j % NBUF, j % NB2 * 2
                            link = Chain(dve, s_c, n * 2)
                            for t in range(2):
                                x = e * SLOTS + s + t
                                ins = nc.vector.scalar_tensor_tensor(
                                    out=ycol[:, buf, t:t + 1], in0=xg[:, buf, t, bass.ds(P + E + e, 1)],
                                    scalar=valid_f[:, bass.ds(x, 1)], in1=spare_f[:, bass.ds(x, 1)],
                                    op0=ALU.mult, op1=ALU.add)
                            link(ins)
                            dve.wait_ge(s_y, n + 1)
                            dve.sem_inc(s_hold, 1)
                            if not (first and j < NBUF):
                                dve.wait_ge(s_sc[buf], (k * 2 + j // NBUF) * 32)
                                dve.sem_inc(s_hold, 1)
                            link(nc.vector.tensor_tensor(yw[:, buf, :, :], ps[:, 6 + j % 2, 0:S].rearrange("p (t d) -> p t d", t=2),
                                                         be2[:, bass.ds(e, 1), :].broadcast_to((P, 2, P)), ALU.add))
                            nc.vector.tensor_copy(scat[:, buf, :], ycol[:, buf, :])
                            for t in range(2):
                                ins = nc.vector.tensor_scalar(yw[:, buf, t, :], yw[:, buf, t, :],
                                                              xg[:, buf, t, bass.ds(P + e, 1)], None, ALU.mult)
                            ins.then_inc(s_ys, 1)

                        valid_f = valid[:].rearrange("p e s -> p (e s)")
                        spare_f = spare[:].rearrange("p e s -> p (e s)")

                        def biases(k, e):
                            nc.vector.tensor_copy(bs[:, e % 2, :], be[:, bass.ds((k * 2 + e) * EC, EC)]).then_inc(s_bs, 1)

                        def pair(k, first=False, final=False):
                            for j in range(2 * NB2):
                                if (j + 1) % NB2 == 0 and not (final and j == 2 * NB2 - 1):
                                    biases(k, (j + 1) // NB2)
                                if not (final and j >= 2 * NB2 - 2):
                                    evac(k * 2 * NB2 + j + 2, j + 2)
                                weigh(k, j, first)

                        dve.wait_ge(s_b, 32)
                        biases(0, 0)
                        evac(0, 0)
                        evac(1, 1)
                        pair(0, first=True)
                        with dve.Fori(1, E // 2 - 1) as k:
                            pair(k)
                        pair(E // 2 - 1, final=True)

                    @block.tensor
                    def _(pe):
                        def turn(k, j):
                            pe.wait_ge(s_xg[j % NBUF], 32 * (k * 2 + j // NBUF + 1))
                            for t in range(2):
                                ins = nc.tensor.transpose(ps[:, j % 2, t * P:(t + 1) * P], xg[:, j % NBUF, t, 0:P], ident)
                            ins.then_inc(s_tp, 1)

                        def hidden(k, j):
                            n, e = k * 2 * NB2 + j, j // NB2
                            pe.wait_ge(s_xt, n + 1)
                            if j % NB2 == 0:
                                pe.wait_ge(s_w[e % 2], 32 * (k + e // 2 + 1))
                            for c in range(EC):
                                ins = nc.tensor.matmul(ps[:, 2 + 2 * (j % 2) + c // 2, c % 2 * S:(c % 2 + 1) * S],
                                                       we1[:, e % 2, c * P:(c + 1) * P], xt[:, j % 2, :],
                                                       start=True, stop=True)
                                if c % 2:
                                    ins.then_inc(s_h, 1)

                        def output(k, j, first):
                            n, u = k * 2 * NB2 + j, j // NB2
                            pe.wait_ge(s_ht, (n + 1) * EC)
                            if not (first and j < 2):
                                pe.wait_ge(s_ys, n - 1)
                            for t in range(2):
                                for c in range(EC):
                                    ins = nc.tensor.matmul(ps[:, 6 + j % 2, t * P:(t + 1) * P],
                                                           ht[:, j % 2, c, t * P:(t + 1) * P],
                                                           we2[:, u, c, :], start=(c == 0), stop=(c == EC - 1))
                            ins.then_inc(s_y, 1)

                        def pair(k, first=False, final=False):
                            for j in range(2 * NB2):
                                if not (final and j == 2 * NB2 - 1):
                                    hidden(k, j + 1)
                                if not (final and j >= 2 * NB2 - 2):
                                    turn(k, j + 2)
                                output(k, j, first)

                        turn(0, 0)
                        hidden(0, 0)
                        turn(0, 1)
                        pair(0, first=True)
                        with pe.Fori(1, E // 2 - 1) as k:
                            pair(k)
                        pair(E // 2 - 1, final=True)

                    @block.scalar
                    def _(act):
                        nc.scalar.preload_act_table(ACT.Gelu)
                        with act.Fori(0, E // 2) as k:
                            for j in range(2 * NB2):
                                n, u = k * 2 * NB2 + j, j // NB2
                                if j % NB2 == 0:
                                    act.wait_ge(s_bs, k * 2 + u + 1)
                                    act.sem_inc(s_hold, 1)
                                for c in range(EC):
                                    act.wait_ge(s_h, n * 2 + c // 2 + 1)
                                    nc.scalar.activation(ht[:, j % 2, c, :],
                                                         ps[:, 2 + 2 * (j % 2) + c // 2, c % 2 * S:(c % 2 + 1) * S],
                                                         ACT.Gelu, bias=bs[:, u, c:c + 1]).then_inc(s_ht, 1)

        experts()

        with ExitStack() as ph:
            CT = 8
            STEPS = NT // CT
            yy = sb("fin_y", [P, 2, 2, CT * P], c=ph)
            s_ld = [sem(f"fin_load{u}", ph) for u in range(2)]
            s_c, s_fin, s_out, s_hold = sem("fin_chain", ph), sem("fin_sum", ph), sem("fin_stored", ph), sem("fin_hold", ph)
            out_v = out.rearrange("b s d -> (b s) d").rearrange("(i t p) d -> i p t d", t=CT, p=P)
            y_v = y_dram[0:2 * T, :].rearrange("(c i t p) d -> c i p t d", c=2, t=CT, p=P)
            with nc.Block() as block:
                @block.sync
                def _(sp):
                    def load(i, u):
                        for c in range(2):
                            sp.dma_start(yy[:, u, c, :].rearrange("p (t d) -> p t d", t=CT),
                                         y_v[c, bass.ds(i, 1)].rearrange("i p t d -> (i p) t d")).then_inc(s_ld[u], 16)

                    load(0, 0)
                    load(1, 1)
                    with sp.Fori(1, STEPS // 2) as k:
                        for u in range(2):
                            sp.wait_ge(s_fin, k * 2 + u - 1)
                            sp.sem_inc(s_hold, 1)
                            load(k * 2 + u, u)

                @block.vector
                def _(dve):
                    with dve.Fori(0, STEPS // 2) as k:
                        for u in range(2):
                            i = k * 2 + u
                            link = Chain(dve, s_c, i)
                            xb = x2[:, bass.ds(i * CT * P, CT * P)]
                            dve.wait_ge(s_ld[u], 32 * (k + 1))
                            link(nc.vector.tensor_tensor(yy[:, u, 0, :], yy[:, u, 0, :], yy[:, u, 1, :], ALU.add))
                            nc.vector.tensor_tensor(xb, xb, yy[:, u, 0, :], ALU.add).then_inc(s_fin, 1)

                @block.scalar
                def _(act):
                    with act.Fori(0, STEPS) as i:
                        act.wait_ge(s_fin, i + 1)
                        act.sem_inc(s_hold, 1)
                        act.dma_start(out_v[bass.ds(i, 1)].rearrange("i p t d -> (i p) t d"),
                                      x2[:, bass.ds(i * CT * P, CT * P)].rearrange("p (t d) -> p t d", t=CT))\
                            .then_inc(s_out, 16)
                    act.wait_ge(s_out, 16 * STEPS)


def host_layout(x, **w):
    w = {k: np.ascontiguousarray(v) for k, v in w.items()}
    t = {k[7:]: v for k, v in w.items() if k.startswith("L0_tok_")}
    col = lambda v: v.reshape(-1, P).T
    rep = lambda v: np.broadcast_to(v[None], (P,) + v.shape)
    return {k: np.ascontiguousarray(v) for k, v in {
        "ids": np.asarray(x, np.int32).reshape(NT, P).T,
        "consts": shape_constants(),
        "emb": t["emb"], "pos": t["pos"], "Wqk": t["Wqk"], "Wv": t["Wv"], "Wo": t["Wo"], "rots": t["rots"],
        "W1": t["W1"], "W2": t["W2"], "ln1_b0": col(t["ln1_b"][0]),
        "b1c": t["b1"].reshape(2, FC, P).transpose(2, 0, 1), "b2r": rep(t["b2"]),
        "lncol": np.concatenate([col(v) for v in (t["ln1_s"][1], t["ln1_b"][1], t["ln2_s"][0], t["ln2_b"][0],
                                                  t["ln2_s"][1], t["ln2_b"][1], w["L0_attn_ln_gamma"],
                                                  w["L0_attn_ln_beta"])], 1),
        "W_gh": w["L0_attn_W_gh"], "gate_wT": w["L0_ffn_gate_w"].T, "gate_b": rep(w["L0_ffn_gate_b"]),
        "bits": np.broadcast_to((np.array([1, 2, 3], np.int32)[None] << np.arange(28, -1, -2, dtype=np.int32)[:, None])
                                .reshape(1, 45), (P, 45)),
        "ew1": w["L0_ffn_w1"], "ew2": w["L0_ffn_w2"],
        "eb1": w["L0_ffn_b1"].reshape(E * EC, P).T, "eb2": rep(w["L0_ffn_b2"]),
    }.items()}


_OUTS = [((B, S, P), "float32")]


def kernel(**inputs):
    import numpy as _np
    import concourse.bacc as _bacc
    from concourse import mybir as _mybir
    from concourse.bass_utils import run_bass_kernel_spmd as _run

    nc = _bacc.Bacc("TRN2", target_bir_lowering=False, num_devices=1)
    arrays, args = {}, {}
    for name, v in host_layout(**inputs).items():
        arrays[f"in_{name}_dram"] = v
        args[name] = nc.dram_tensor(f"in_{name}_dram", v.shape, _mybir.dt.from_np(v.dtype), kind="ExternalInput").ap()
    shape, dtype = _OUTS[0]
    out = nc.dram_tensor("out_0_dram", shape, _mybir.dt.from_np(_np.dtype(dtype)), kind="ExternalOutput").ap()
    build(nc, args, out)
    r = _run(nc, [arrays], core_ids=[0])
    return r.results[0]["out_0_dram"]
```
